# Optimizing a Trainium2 kernel written in Bass

```python
import numpy as np
import jax
import jax.numpy as jnp

def _softmax(x, axis=-1):
    return jax.nn.softmax(x, axis=axis)

def _gelu(x):
    return jax.nn.gelu(x, approximate=True)

def _silu(x):
    return jax.nn.silu(x)

def _sigmoid(x):
    return jax.nn.sigmoid(x)

def _layernorm(x, axis=-1, eps=1e-05):
    m = jnp.mean(x, axis=axis, keepdims=True)
    v = jnp.var(x, axis=axis, keepdims=True)
    return (x - m) / jnp.sqrt(v + eps)

def _scatter_add(tgt, idx, src, axis=0):
    return tgt.at[idx].add(src)

def _segment_sum(src, seg, n):
    return jax.ops.segment_sum(src, seg, n)
kernel_name = 'mk_prb_d2_jaxref_r8_25694c'

def setup_inputs(seed: int=0):
    np.random.seed(seed)
    _w = jnp.asarray

    def _L0_attn_setup():
        import jax, jax.numpy as jnp
        import numpy as np
        LN_EPS = 1e-05
        key = jax.random.key(seed)
        ks = jax.random.split(key, 7)
        B, L, D, N = (8, 256, 128, 16)
        x = jax.random.normal(ks[0], (B, L, D), jnp.float32)
        A = jax.random.normal(ks[1], (D, N, N), jnp.float32) * (0.2 / np.sqrt(N))
        Bp = jax.random.normal(ks[2], (D, N), jnp.float32)
        Cp = jax.random.normal(ks[3], (D, N), jnp.float32)
        Dp = jax.random.normal(ks[4], (D,), jnp.float32)
        Wg = jax.random.normal(ks[5], (D, D), jnp.float32) / np.sqrt(D)
        bg = jnp.zeros((D,), jnp.float32)
        gamma = jnp.ones((D,), jnp.float32)
        beta = jnp.zeros((D,), jnp.float32)
        return dict(x=x, A=A, Bp=Bp, Cp=Cp, Dp=Dp, Wg=Wg, bg=bg, gamma=gamma, beta=beta)
    _L0_attn_in = _L0_attn_setup()

    def _L0_ffn_setup():
        import jax, jax.numpy as jnp
        import numpy as np
        D_MODEL = 128
        D_FF = 512
        N_EXPERTS = 8
        TOP_K = 2
        LN_EPS = 1e-06

        def _moe(x, router_w, w1, b1, w2, b2, gamma, beta):
            B, S, D = x.shape
            x_flat = x.reshape(-1, D)
            N = x_flat.shape[0]
            logits = x_flat @ router_w
            gate_vals, gate_idx = jax.lax.top_k(logits, TOP_K)
            gate_w = jax.nn.softmax(gate_vals, axis=-1)
            gates = jnp.zeros_like(logits).at[jnp.arange(N)[:, None], gate_idx].set(gate_w)
            h = jax.nn.gelu(jnp.einsum('nd,edf->enf', x_flat, w1) + b1[:, None, :], approximate=False)
            out = jnp.einsum('enf,efd->end', h, w2) + b2[:, None, :]
            res = x_flat[None, :, :] + out
            mu = jnp.mean(res, axis=-1, keepdims=True)
            var = jnp.mean(jnp.square(res - mu), axis=-1, keepdims=True)
            normed = (res - mu) * jax.lax.rsqrt(var + LN_EPS)
            expert_out = normed * gamma[:, None, :] + beta[:, None, :]
            y = jnp.einsum('end,ne->nd', expert_out, gates)
            return y.reshape(B, S, D)
        key = jax.random.key(seed)
        ks = jax.random.split(key, 8)
        x = jax.random.normal(ks[0], (2, 256, D_MODEL), dtype=jnp.float32)
        router_w = jax.random.normal(ks[1], (D_MODEL, N_EXPERTS), dtype=jnp.float32) * 0.02
        w1 = jax.random.normal(ks[2], (N_EXPERTS, D_MODEL, D_FF), dtype=jnp.float32) * 0.02
        b1 = jnp.zeros((N_EXPERTS, D_FF), dtype=jnp.float32)
        w2 = jax.random.normal(ks[3], (N_EXPERTS, D_FF, D_MODEL), dtype=jnp.float32) * 0.02
        b2 = jnp.zeros((N_EXPERTS, D_MODEL), dtype=jnp.float32)
        gamma = jnp.ones((N_EXPERTS, D_MODEL), dtype=jnp.float32)
        beta = jnp.zeros((N_EXPERTS, D_MODEL), dtype=jnp.float32)
        return {'x': x, 'router_w': router_w, 'w1': w1, 'b1': b1, 'w2': w2, 'b2': b2, 'gamma': gamma, 'beta': beta}
    _L0_ffn_in = _L0_ffn_setup()

    def _L1_attn_setup():
        import jax, jax.numpy as jnp
        import numpy as np
        B, T, D_MODEL = (4, 512, 128)
        H = 16
        DH = D_MODEL // H
        EPS = 1e-06
        CHUNK = 128

        def _feature(x):
            return jnp.where(x > 0, x + 1.0, jnp.exp(x))

        def _causal_dot_product(Q, K, V):
            b, h, t, d = Q.shape
            nc = t // CHUNK
            mask = jnp.tril(jnp.ones((CHUNK, CHUNK), dtype=Q.dtype))
            qs = jnp.moveaxis(Q.reshape(b, h, nc, CHUNK, d), 2, 0)
            ks = jnp.moveaxis(K.reshape(b, h, nc, CHUNK, d), 2, 0)
            vs = jnp.moveaxis(V.reshape(b, h, nc, CHUNK, d), 2, 0)

            def step(S, qkv):
                q, k, v = qkv
                attn = jnp.einsum('bhid,bhjd->bhij', q, k) * mask
                out = jnp.einsum('bhij,bhjd->bhid', attn, v) + jnp.einsum('bhid,bhde->bhie', q, S)
                S = S + jnp.einsum('bhcd,bhce->bhde', k, v)
                return (S, out)
            S0 = jnp.zeros((b, h, d, d), dtype=Q.dtype)
            _, outs = jax.lax.scan(step, S0, (qs, ks, vs))
            return jnp.moveaxis(outs, 0, 2).reshape(b, h, t, d)
        key = jax.random.key(seed)
        ks = jax.random.split(key, 6)
        s = 0.02
        x = jax.random.normal(ks[0], (B, T, D_MODEL), dtype=jnp.float32)
        Wq = jax.random.normal(ks[1], (D_MODEL, D_MODEL), dtype=jnp.float32) * s
        Wk = jax.random.normal(ks[2], (D_MODEL, D_MODEL), dtype=jnp.float32) * s
        Wv = jax.random.normal(ks[3], (D_MODEL, D_MODEL), dtype=jnp.float32) * s
        Wo = jax.random.normal(ks[4], (D_MODEL, D_MODEL), dtype=jnp.float32) * s
        bo = jax.random.normal(ks[5], (D_MODEL,), dtype=jnp.float32) * s
        return {'x': x, 'Wq': Wq, 'Wk': Wk, 'Wv': Wv, 'Wo': Wo, 'bo': bo}
    _L1_attn_in = _L1_attn_setup()

    def _L1_ffn_setup():
        import jax, jax.numpy as jnp
        import numpy as np
        D_MODEL, D_FF, RANK = (128, 512, 32)
        B, S = (4, 512)
        key = jax.random.key(seed)
        ks = jax.random.split(key, 7)
        return {'x': jax.random.normal(ks[0], (B, S, D_MODEL), dtype=jnp.float32), 'U1': jax.random.normal(ks[1], (D_MODEL, RANK), dtype=jnp.float32) * 0.02, 'V1': jax.random.normal(ks[2], (RANK, D_FF), dtype=jnp.float32) * 0.02, 'b1': jnp.zeros((D_FF,), dtype=jnp.float32), 'U2': jax.random.normal(ks[3], (D_FF, RANK), dtype=jnp.float32) * 0.02, 'V2': jax.random.normal(ks[4], (RANK, D_MODEL), dtype=jnp.float32) * 0.02, 'b2': jnp.zeros((D_MODEL,), dtype=jnp.float32)}
    _L1_ffn_in = _L1_ffn_setup()
    _d = {'L0_attn_x': _L0_attn_in['x'], 'L0_attn_A': _L0_attn_in['A'], 'L0_attn_Bp': _L0_attn_in['Bp'], 'L0_attn_Cp': _L0_attn_in['Cp'], 'L0_attn_Dp': _L0_attn_in['Dp'], 'L0_attn_Wg': _L0_attn_in['Wg'], 'L0_attn_bg': _L0_attn_in['bg'], 'L0_attn_gamma': _L0_attn_in['gamma'], 'L0_attn_beta': _L0_attn_in['beta'], 'L0_ffn_router_w': _L0_ffn_in['router_w'], 'L0_ffn_w1': _L0_ffn_in['w1'], 'L0_ffn_b1': _L0_ffn_in['b1'], 'L0_ffn_w2': _L0_ffn_in['w2'], 'L0_ffn_b2': _L0_ffn_in['b2'], 'L0_ffn_gamma': _L0_ffn_in['gamma'], 'L0_ffn_beta': _L0_ffn_in['beta'], 'L1_attn_Wq': _L1_attn_in['Wq'], 'L1_attn_Wk': _L1_attn_in['Wk'], 'L1_attn_Wv': _L1_attn_in['Wv'], 'L1_attn_Wo': _L1_attn_in['Wo'], 'L1_attn_bo': _L1_attn_in['bo'], 'L1_ffn_U1': _L1_ffn_in['U1'], 'L1_ffn_V1': _L1_ffn_in['V1'], 'L1_ffn_b1': _L1_ffn_in['b1'], 'L1_ffn_U2': _L1_ffn_in['U2'], 'L1_ffn_V2': _L1_ffn_in['V2'], 'L1_ffn_b2': _L1_ffn_in['b2']}
    _x0 = _d['L0_attn_x']
    _d['L0_attn_x'] = jax.random.normal(jax.random.fold_in(jax.random.key(seed), 1), (16, 256, 128), dtype=_x0.dtype)
    del _x0
    return _d

def reference(L0_attn_x, L0_attn_A, L0_attn_Bp, L0_attn_Cp, L0_attn_Dp, L0_attn_Wg, L0_attn_bg, L0_attn_gamma, L0_attn_beta, L0_ffn_router_w, L0_ffn_w1, L0_ffn_b1, L0_ffn_w2, L0_ffn_b2, L0_ffn_gamma, L0_ffn_beta, L1_attn_Wq, L1_attn_Wk, L1_attn_Wv, L1_attn_Wo, L1_attn_bo, L1_ffn_U1, L1_ffn_V1, L1_ffn_b1, L1_ffn_U2, L1_ffn_V2, L1_ffn_b2):

    def _L0_attn_ref(x, A, Bp, Cp, Dp, Wg, bg, gamma, beta):
        import jax, jax.numpy as jnp
        import numpy as np
        LN_EPS = 1e-05
        gate = jax.nn.sigmoid(jnp.einsum('bld,ed->ble', x, Wg) + bg)
        xg = x * gate
        Bsz, L, D = xg.shape
        N = A.shape[-1]

        def step(s, xt):
            s = jnp.einsum('bdn,dnm->bdm', s, A) + xt[..., None] * Bp
            y = jnp.einsum('bdn,dn->bd', s, Cp) + Dp * xt
            return (s, y)
        s0 = jnp.zeros((Bsz, D, N), xg.dtype)
        _, ys = jax.lax.scan(step, s0, jnp.moveaxis(xg, 1, 0))
        y = jnp.moveaxis(ys, 0, 1) + xg
        mu = jnp.mean(y, axis=-1, keepdims=True)
        var = jnp.var(y, axis=-1, keepdims=True)
        return (y - mu) * jax.lax.rsqrt(var + LN_EPS) * gamma + beta

    def _L0_ffn_ref(x, router_w, w1, b1, w2, b2, gamma, beta):
        import jax, jax.numpy as jnp
        import numpy as np
        D_MODEL = 128
        D_FF = 512
        N_EXPERTS = 8
        TOP_K = 2
        LN_EPS = 1e-06

        def _moe(x, router_w, w1, b1, w2, b2, gamma, beta):
            B, S, D = x.shape
            x_flat = x.reshape(-1, D)
            N = x_flat.shape[0]
            logits = x_flat @ router_w
            gate_vals, gate_idx = jax.lax.top_k(logits, TOP_K)
            gate_w = jax.nn.softmax(gate_vals, axis=-1)
            gates = jnp.zeros_like(logits).at[jnp.arange(N)[:, None], gate_idx].set(gate_w)
            h = jax.nn.gelu(jnp.einsum('nd,edf->enf', x_flat, w1) + b1[:, None, :], approximate=False)
            out = jnp.einsum('enf,efd->end', h, w2) + b2[:, None, :]
            res = x_flat[None, :, :] + out
            mu = jnp.mean(res, axis=-1, keepdims=True)
            var = jnp.mean(jnp.square(res - mu), axis=-1, keepdims=True)
            normed = (res - mu) * jax.lax.rsqrt(var + LN_EPS)
            expert_out = normed * gamma[:, None, :] + beta[:, None, :]
            y = jnp.einsum('end,ne->nd', expert_out, gates)
            return y.reshape(B, S, D)
        return _moe(x, router_w, w1, b1, w2, b2, gamma, beta)

    def _L1_attn_ref(x, Wq, Wk, Wv, Wo, bo):
        import jax, jax.numpy as jnp
        import numpy as np
        B, T, D_MODEL = (4, 512, 128)
        H = 16
        DH = D_MODEL // H
        EPS = 1e-06
        CHUNK = 128

        def _feature(x):
            return jnp.where(x > 0, x + 1.0, jnp.exp(x))

        def _causal_dot_product(Q, K, V):
            b, h, t, d = Q.shape
            nc = t // CHUNK
            mask = jnp.tril(jnp.ones((CHUNK, CHUNK), dtype=Q.dtype))
            qs = jnp.moveaxis(Q.reshape(b, h, nc, CHUNK, d), 2, 0)
            ks = jnp.moveaxis(K.reshape(b, h, nc, CHUNK, d), 2, 0)
            vs = jnp.moveaxis(V.reshape(b, h, nc, CHUNK, d), 2, 0)

            def step(S, qkv):
                q, k, v = qkv
                attn = jnp.einsum('bhid,bhjd->bhij', q, k) * mask
                out = jnp.einsum('bhij,bhjd->bhid', attn, v) + jnp.einsum('bhid,bhde->bhie', q, S)
                S = S + jnp.einsum('bhcd,bhce->bhde', k, v)
                return (S, out)
            S0 = jnp.zeros((b, h, d, d), dtype=Q.dtype)
            _, outs = jax.lax.scan(step, S0, (qs, ks, vs))
            return jnp.moveaxis(outs, 0, 2).reshape(b, h, t, d)
        b, t, _ = x.shape

        def proj(W):
            return (x @ W).reshape(b, t, H, DH).transpose(0, 2, 1, 3)
        Q = _feature(proj(Wq))
        K = _feature(proj(Wk))
        V = proj(Wv)
        Z = 1.0 / (jnp.einsum('bhtd,bhtd->bht', Q, jnp.cumsum(K, axis=1)) + EPS)
        unnorm = _causal_dot_product(Q, K, V)
        out = unnorm * Z[..., None]
        out = out.transpose(0, 2, 1, 3).reshape(b, t, H * DH)
        return out @ Wo + bo

    def _L1_ffn_ref(x, U1, V1, b1, U2, V2, b2):
        import jax, jax.numpy as jnp
        import numpy as np
        D_MODEL, D_FF, RANK = (128, 512, 32)
        B, S = (4, 512)
        P = jnp.einsum('bsd,dr->bsr', x, U1)
        H = jax.nn.gelu(jnp.einsum('bsr,rf->bsf', P, V1) + b1)
        Q = jnp.einsum('bsf,fr->bsr', H, U2)
        return jnp.einsum('bsr,rd->bsd', Q, V2) + b2
    x = L0_attn_x
    xn = _layernorm(x, axis=-1)
    x = x + _L0_attn_ref(xn, L0_attn_A, L0_attn_Bp, L0_attn_Cp, L0_attn_Dp, L0_attn_Wg, L0_attn_bg, L0_attn_gamma, L0_attn_beta) + _L0_ffn_ref(xn, L0_ffn_router_w, L0_ffn_w1, L0_ffn_b1, L0_ffn_w2, L0_ffn_b2, L0_ffn_gamma, L0_ffn_beta)
    xn = _layernorm(x, axis=-1)
    x = x + _L1_attn_ref(xn, L1_attn_Wq, L1_attn_Wk, L1_attn_Wv, L1_attn_Wo, L1_attn_bo) + _L1_ffn_ref(xn, L1_ffn_U1, L1_ffn_V1, L1_ffn_b1, L1_ffn_U2, L1_ffn_V2, L1_ffn_b2)
    return x

_drawn_inputs = setup_inputs


def setup_inputs(seed=0):
    import zlib

    import numpy as np

    out = dict(_drawn_inputs(seed))
    spreads = {'L0_attn_bg': (0.0, 0.574),
     'L0_attn_gamma': (1.0, 0.2),
     'L0_attn_beta': (0.0, 0.1),
     'L0_ffn_b1': (0.0, 0.8),
     'L0_ffn_b2': (0.0, 0.368),
     'L0_ffn_gamma': (1.0, 0.2),
     'L0_ffn_beta': (0.0, 0.267),
     'L1_ffn_b1': (0.0, 0.8),
     'L1_ffn_b2': (0.0, 0.361)}
    factors = {'L0_ffn_w1': 3.66,
     'L0_ffn_w2': 3.272,
     'L1_attn_Wq': 8.0,
     'L1_attn_Wk': 6.028,
     'L1_attn_bo': 6.027,
     'L1_ffn_U1': 8.0,
     'L1_ffn_V1': 8.0,
     'L1_ffn_U2': 8.0,
     'L1_ffn_V2': 8.0}
    for name, (base, spread) in spreads.items():
        noise = np.random.default_rng([zlib.crc32(name.encode()), seed]).standard_normal(out[name].shape)
        drawn = base * np.exp(spread * noise) if base else spread * noise
        out[name] = jnp.asarray(drawn.astype(out[name].dtype))
    for name, factor in factors.items():
        out[name] = (out[name] * factor).astype(out[name].dtype)
    return out
```

```python
from contextlib import ExitStack

import concourse.bass as bass
from concourse import mybir

F32 = mybir.dt.float32
I32 = mybir.dt.int32
ALU = mybir.AluOpType
ACT = mybir.ActivationFunctionType
AXX = mybir.AxisListType.X

P = 128
D = 128
BATCH, SEQ = 16, 256
TILES = BATCH * SEQ // P
GT = 4
GROUPS = TILES // GT
GW = GT * P
N = 16
CH8 = P // N
BLK = D // CH8
E = 8
F = 512
FC = F // P
CHD = D // GROUPS
HPAD = SEQ + P
H, DH = 16, 8
R4 = 4
RANK = 32
ONE = 1
NEWTON = 3
NORM = 2 + 3 + 3 * NEWTON


class Count:

    def __init__(self, eng, sem):
        self.eng, self.sem, self.base, self.n = eng, sem, 0, 0

    def mark(self, ins):
        self.n += 1
        ins.then_inc(self.sem, 1)

    def wait(self):
        self.eng.wait_ge(self.sem, self.base + self.n)

    def enter(self, i, per):
        self.start, self.per = self.base + self.n, per
        self.base, self.n = i * per + self.start, 0

    def leave(self, trips):
        assert self.n == self.per, (self.n, self.per)
        self.base, self.n = self.start + trips * self.per, 0


def two_layer_kernel(nc, x, A, At, BpT, CpT, DpR, WgRw, bg, gamma, beta, w1, b1T, w2, b2, egamma, ebeta,
                     Wq, Wk, Wv, Wo, bo, U1R, V1, fb1T, U2, V2R, fb2, out):
    with ExitStack() as ctx:
        def sb(name, shape):
            return ctx.enter_context(nc.sbuf_tensor(name, shape, F32))

        def sem(name):
            return ctx.enter_context(nc.semaphore(name))

        x_all = sb("x_all", [P, TILES, D])
        xnT_all = sb("xnT_all", [P, TILES * P])
        xg_all = sb("xg_all", [P, TILES, D])
        y_all = sb("y_all", [P, TILES, D])
        w1_sb = sb("w1_sb", [P, E, F])
        w2_sb = sb("w2_sb", [P, E, FC, D])
        b1_sb = sb("b1_sb", [P, E, FC])
        b2_sb = sb("b2_sb", [1, E, D])
        egam = sb("egam", [P, E, D])
        ebet = sb("ebet", [E, D])
        gam_bc = sb("gam_bc", [P, D])
        bet_bc = sb("bet_bc", [P, D])
        wg_sb = sb("wg_sb", [P, D + E])
        bg_sb = sb("bg_sb", [1, D + E])
        ident = sb("ident", [P, P])
        flip = sb("flip", [P, P])
        ones = sb("ones", [1, P])
        big = sb("big", [P, 2 * BLK * P])
        M = big[:, 0:BLK * P].rearrange("p (g c) -> p g c", g=BLK)
        Mt = big[:, BLK * P:].rearrange("p (g c) -> p g c", g=BLK)
        toep = big[:, :].rearrange("p (d u) -> p d u", d=CHD)
        AiC = sb("AiC", [P, BLK, N])
        AjB = sb("AjB", [P, BLK, N])
        bc_sb = sb("bc_sb", [P, 2, BLK])
        mask8 = sb("mask8", [P, CH8])
        first_lag = sb("first_lag", [P, 1])
        dp_sb = sb("dp_sb", [P, BLK])
        dp1 = sb("dp1", [P, BLK])
        h_sb = sb("h_sb", [P, BLK, N])
        zero_sb = sb("zero_sb", [P, P])
        mid = sb("mid", [P, 4096])
        Rbd = mid[:, 0:BLK * P].rearrange("p (g d j) -> p g d j", g=BLK, d=CH8)
        hT = mid[:, :].rearrange("p (s c t) -> p s c t", s=2, c=FC)
        stats = sb("stats", [P, GT, 6])
        mv = sb("mv", [P, GT, 2])
        rstd = sb("rstd", [P, GT])
        ve = sb("ve", [P, GT])
        sq = sb("sq", [P, GT])
        xn = sb("xn", [P, GT, D])
        xnT = sb("xnT", [P, GW])
        logits = sb("logits", [P, TILES, E])
        gates = sb("gates", [P, TILES, E])
        gslot = sb("gslot", [P, GT, E])
        gT = sb("gT", [E, GT, P])
        t1 = sb("t1", [P, TILES, E])
        t2 = sb("t2", [P, TILES, E])
        rank8 = sb("rank8", [P, E])
        place8 = sb("place8", [P, DH])
        m1 = sb("m1", [P, TILES])
        m2 = sb("m2", [P, TILES])
        m3 = sb("m3", [P, TILES])
        nr = sb("nr", [P, 2, GT])
        tmp = sb("tmp", [P, 2, GT, D])

        wqk = sb("wqk", [P, 2, D])
        wkv = sb("wkv", [P, 2, D])
        wo_sb = sb("wo_sb", [P, D])
        u1_sb = sb("u1_sb", [P, P])
        v1_sb = sb("v1_sb", [P, P])
        u2_sb = sb("u2_sb", [P, FC, RANK])
        v2_sb = sb("v2_sb", [P, D])
        fb1_sb = sb("fb1_sb", [P, FC])
        bo_bc = sb("bo_bc", [P, D])
        fb2_bc = sb("fb2_bc", [P, D])
        causal = sb("causal", [P, P])
        same_head = sb("same_head", [P, P])
        head_sum = sb("head_sum", [P, P])
        head_pick = sb("head_pick", [P, R4])
        Am = mid[:, 0:2048].rearrange("p (r k t) -> p r k t", r=R4, k=R4)
        Hf = mid[:, 2048:4096].rearrange("p (c t) -> p c t", c=FC)
        QTm = xg_all[:, 0:16, :].rearrange("p a b -> p (a b)").rearrange("p (k t) -> p k t", k=R4)
        Vm = xg_all[:, 16:32, :].rearrange("p a b -> p (a b)").rearrange(
            "p (q r k l e) -> p q r k l e", q=GT, r=R4, k=R4, l=R4)
        l1 = big[:, :].rearrange("p (s t) -> p s t", s=8)
        Eq, Rq, Ek, Rk, QT, KT, prod, zr = [l1[:, i, :] for i in range(8)]
        l2 = xnT_all[:, :].rearrange("p (s t) -> p s t", s=8)
        Ekt, Rkt, Ktok, Vtok, attnT, PT, QfT, yo = [l2[:, i, :] for i in range(8)]
        S = sb("S", [P, 2, P])

        bank = [ctx.enter_context(nc.psum_tensor(f"bank{i}", [P, 512], F32)) for i in range(8)]
        h_dram = nc.dram_tensor("impulse_responses", [D, HPAD], F32, kind="Internal")

        s_x_in = sem("x_in")
        s_a_in = sem("a_in")
        s_wg_in = sem("wg_in")
        s_const_in = sem("const_in")
        s_w_in = sem("w_in")
        s_l1_in = sem("l1_in")
        s_zeroed = sem("zeroed")
        s_masks = sem("masks")
        s_sq_done = sem("sq_done")
        s_m_copied = sem("m_copied")
        s_mt_copied = sem("mt_copied")
        s_pr_done = sem("pr_done")
        s_p_copied = sem("p_copied")
        s_rbd_ready = sem("rbd_ready")
        s_h_done = sem("h_done")
        s_h_ready = sem("h_ready")
        s_h_out = sem("h_out")
        s_toep_in = sem("toep_in")
        s_xn_ready = sem("xn_ready")
        s_tr_done = sem("tr_done")
        s_xnT_ready = sem("xnT_ready")
        s_xnT_all_ready = sem("xnT_all_ready")
        s_gate_done = sem("gate_done")
        s_sig_ready = sem("sig_ready")
        s_xg_ready = sem("xg_ready")
        s_gslot_ready = sem("gslot_ready")
        s_gT_done = sem("gT_done")
        s_gT_ready = sem("gT_ready")
        s_beta_done = sem("beta_done")
        s_beta_added = sem("beta_added")
        s_slot_ready = sem("slot_ready")
        s_hid_done = sem("hid_done")
        s_hid_ready = sem("hid_ready")
        s_o_done = sem("o_done")
        s_tmp_ready = sem("tmp_ready")
        s_tmp_used = sem("tmp_used")
        s_ssm_done = sem("ssm_done")
        s_y_ready = sem("y_ready")
        s_pool_chain = sem("pool_chain")
        s_dve_chain = sem("dve_chain")
        s_xb_ready = sem("xb_ready")
        s_n_ready = sem("n_ready")
        s_n_tr = sem("n_tr")
        s_n_T = sem("n_T")
        s_qkv_done = sem("qkv_done")
        s_ekv_ready = sem("ekv_ready")
        s_qk_ready = sem("qk_ready")
        s_vm_ready = sem("vm_ready")
        s_qtm_ready = sem("qtm_ready")
        s_kt_ready = sem("kt_ready")
        s_kc_done = sem("kc_done")
        s_prod_ready = sem("prod_ready")
        s_den_done = sem("den_done")
        s_st_done = sem("st_done")
        s_st_ready = sem("st_ready")
        s_sc_done = sem("sc_done")
        s_am_ready = sem("am_ready")
        s_av_done = sem("av_done")
        s_attn_ready = sem("attn_ready")
        s_pt_ready = sem("pt_ready")
        s_hf_done = sem("hf_done")
        s_hf_ready = sem("hf_ready")
        s_qf_done = sem("qf_done")
        s_qf_ready = sem("qf_ready")
        s_y_done = sem("y_done")
        s_out_ready = sem("out_ready")
        s_out_done = sem("out_done")
        s_v_ready = sem("v_ready")
        s_tok_done = sem("tok_done")
        s_gap_ready = sem("gap_ready")
        s_gap_exp = sem("gap_exp")
        s_pool_mul = sem("pool_mul")
        s_bias_ready = sem("bias_ready")
        s_small_masks = sem("small_masks")
        s_dve_pace = sem("dve_pace")
        s_pool_pace = sem("pool_pace")
        s_bc_in = sem("bc_in")
        s_first_columns = sem("first_columns")
        s_rev_done = sem("rev_done")
        s_rev_ready = sem("rev_ready")

        block = ctx.enter_context(nc.Block())

        x_t = x.rearrange("(t p) d -> p t d", p=P)
        out_t = out.rearrange("(t p) d -> p t d", p=P)

        @block.sync
        def _(sp):
            sp.dma_start(wg_sb[:, :], WgRw).then_inc(s_wg_in, 16)
            sp.dma_start(bg_sb[:, 0:D], bg).then_inc(s_wg_in, 16)
            for k in range(4):
                sp.dma_start(x_all[:, 8 * k:8 * k + 8, :], x_t[:, 8 * k:8 * k + 8, :]).then_inc(s_x_in, 16)
            sp.wait_ge(s_zeroed, 1)
            for i in range(CH8):
                rows = slice(N * i, N * i + N)
                sp.dma_start(M[rows, :, rows], A.rearrange("(g i) n m -> i n g m", i=CH8)[i]).then_inc(s_a_in, 16)
                sp.dma_start(Mt[rows, :, rows], At.rearrange("(g i) n m -> i n g m", i=CH8)[i]).then_inc(s_a_in, 16)
            sp.dma_start(bc_sb[:, 0, :], CpT).then_inc(s_bc_in, 16)
            sp.dma_start(bc_sb[:, 1, :], BpT).then_inc(s_bc_in, 16)
            sp.dma_start(dp_sb[:, :], DpR).then_inc(s_a_in, 16)
            for src, dst in ((gamma, gam_bc), (beta, bet_bc), (bo, bo_bc), (fb2, fb2_bc)):
                sp.dma_start(dst[:, :], src.rearrange("(a d) -> a d", a=1).broadcast_to([P, D])).then_inc(s_const_in, 16)
            sp.dma_start(b1_sb[:, :, :], b1T).then_inc(s_w_in, 16)
            sp.dma_start(b2_sb[:, :, :], b2.rearrange("(a e) d -> a e d", a=1)).then_inc(s_w_in, 16)
            sp.dma_start(egam[:, :, :], egamma.rearrange("(a e) d -> a e d", a=1).broadcast_to([P, E, D])).then_inc(s_w_in, 16)
            sp.dma_start(ebet[:, :], ebeta).then_inc(s_w_in, 16)
            for k in range(4):
                sp.dma_start(w1_sb[:, 2 * k:2 * k + 2, :], w1.rearrange("e d f -> d e f")[:, 2 * k:2 * k + 2, :]).then_inc(s_w_in, 16)
                sp.dma_start(w2_sb[:, 2 * k:2 * k + 2, :, :],
                             w2.rearrange("e (c f) d -> f e c d", c=FC)[:, 2 * k:2 * k + 2]).then_inc(s_w_in, 16)
            sp.wait_ge(s_h_ready, 1)
            for i in range(CH8):
                sp.dma_start(h_dram.ap().rearrange("(g i) (j k) -> i j g k", i=CH8, k=N)[i, P // N:HPAD // N],
                             h_sb[N * i:N * i + N, :, :]).then_inc(s_h_out, 16)
            sp.dma_start(h_dram.ap()[:, 0:P], zero_sb[:, :]).then_inc(s_h_out, 16)
            for src, dst in ((Wq, wqk[:, 0, :]), (Wk, wqk[:, 1, :]), (Wk, wkv[:, 0, :]), (Wv, wkv[:, 1, :]), (Wo, wo_sb[:, :]),
                             (U1R, u1_sb[:, :]), (V2R, v2_sb[:, :]), (fb1T, fb1_sb[:, :]),
                             (V1, v1_sb[:, :]), (U2.rearrange("(c f) r -> f c r", c=FC), u2_sb[:, :, :])):
                sp.dma_start(dst, src).then_inc(s_l1_in, 16)
            sp.wait_ge(s_h_out, 16 * (CH8 + 1))
            for g in range(GROUPS):
                if g:
                    sp.wait_ge(s_ssm_done, g)
                sp.dma_start(toep, bass.AP(tensor=h_dram, offset=g * (CHD * HPAD) + 1,
                                           ap=[[1, P], [HPAD, CHD], [1, SEQ]])).then_inc(s_toep_in, 16)
            with sp.Fori(0, GROUPS) as g:
                sp.wait_ge(s_out_ready, g + 1 + ONE)
                sp.dma_start(out_t[:, bass.ds(GT * g, GT), :], yo.rearrange("p (q d) -> p q d", q=GT)).then_inc(s_out_done, 16)
            sp.wait_ge(s_out_done, 16 * GROUPS + ONE)

        @block.gpsimd
        def _(pool):
            chain = Count(pool, s_pool_chain)
            for started in (s_sig_ready, s_rev_ready, s_y_ready, s_hid_ready, s_tmp_ready, s_out_ready, s_am_ready, s_beta_done, s_o_done, s_tr_done, s_gT_done, s_tmp_used, s_av_done, s_out_done, s_sc_done):
                pool.sem_inc(started, ONE)
            pool.memset(big[:, :], 0.0).then_inc(s_zeroed, 1)
            pool.memset(zero_sb[:, :], 0.0)
            pool.memset(ones[:, :], 1.0)
            pool.memset(bg_sb[:, D:], 0.0)
            for t in (ident, flip, causal, same_head, head_sum, mask8):
                last = pool.memset(t[:, :], 1.0)
            chain.mark(last)
            chain.wait()

            def keep(t, view, pattern, base, mult, op):
                pool.affine_select(out=view, in_=view, pattern=pattern, compare_op=op, fill=0.0, base=base,
                                   channel_multiplier=mult)

            keep(ident, ident[:, :], [[-1, P]], 0, 1, ALU.is_equal)
            keep(flip, flip[:, :], [[1, P]], 1 - P, 1, ALU.is_equal)
            keep(causal, causal[:, :], [[1, P]], 0, -1, ALU.is_ge)
            last = pool.affine_select(out=mask8[:, :], in_=mask8[:, :], pattern=[[-N, CH8]], compare_op=ALU.is_ge, fill=0.0,
                                      base=0, channel_multiplier=1)
            hv = same_head[:, :].rearrange("p (h e) -> p h e", h=H)
            pool.affine_select(out=hv, in_=hv, pattern=[[-DH, H], [0, DH]], compare_op=ALU.is_ge, fill=0.0,
                               base=0, channel_multiplier=1)
            sv = head_sum[:, :].rearrange("p (h e) -> p h e", h=H)
            last = pool.affine_select(out=sv, in_=sv, pattern=[[DH, H], [1, DH]], compare_op=ALU.is_ge, fill=0.0,
                                      base=0, channel_multiplier=-1)
            chain.mark(last)
            chain.wait()
            last = pool.affine_select(out=mask8[:, :], in_=mask8[:, :], pattern=[[N, CH8]], compare_op=ALU.is_ge, fill=0.0,
                                      base=N - 1, channel_multiplier=-1)
            chain.mark(pool.affine_select(out=hv, in_=hv, pattern=[[DH, H], [0, DH]], compare_op=ALU.is_ge, fill=0.0,
                                      base=DH - 1, channel_multiplier=-1))
            chain.mark(pool.iota(rank8[:, :], pattern=[[-1, E]], base=E, channel_multiplier=0,
                                 allow_small_or_imprecise_dtypes=True))
            chain.wait()
            pool.sem_inc(s_masks, 1)

            pool.wait_ge(s_bc_in, 32)
            pool.tensor_copy(AiC[:, :, 0], bc_sb[:, 0, :]).then_inc(s_first_columns, 1)
            pool.tensor_copy(AjB[:, :, 0], bc_sb[:, 1, :]).then_inc(s_first_columns, 1)

            pool.wait_ge(s_xnT_all_ready, GROUPS)
            pool.wait_ge(s_gate_done, 2 * GROUPS)
            pool.wait_ge(s_w_in, 16 * 12)
            with pool.Fori(0, GROUPS) as g:
                pool.wait_ge(s_o_done, E * g + ONE)
                pool.tensor_copy(xnT[:, :], xnT_all[:, bass.ds(GW * g, GW)]).then_inc(s_slot_ready, 1)
                pool.wait_ge(s_beta_added, g + 1)
                xs = x_all[:, bass.ds(GT * g, GT), :]
                for e in range(E):
                    t = tmp[:, e % 2, :, :]
                    pool.wait_ge(s_tmp_ready, E * g + e + 1 + ONE)
                    pool.tensor_tensor(t, t, egam[:, e:e + 1, :].broadcast_to([P, GT, D]), ALU.mult).then_inc(s_pool_mul, 1)
                    pool.wait_ge(s_pool_mul, E * g + e + 1)
                    pool.wait_ge(s_tmp_used, E * g + e + ONE)
                    pool.sem_inc(s_pool_pace, 1)
                    pool.tensor_tensor(xs, xs, t, ALU.add).then_inc(s_tmp_used, 1)
            pool.wait_ge(s_const_in, 64)
            pool.tensor_tensor(bo_bc[:, :], bo_bc[:, :], fb2_bc[:, :], ALU.add).then_inc(s_bias_ready, 1)
            pool.wait_ge(s_bias_ready, 1)
            with pool.Fori(0, GROUPS) as g:
                pool.wait_ge(s_n_ready, GT * g + GT)
                xs = x_all[:, bass.ds(GT * g, GT), :]
                pool.sem_inc(s_pool_pace, 1)
                pool.tensor_tensor(xs, xs, bo_bc[:, :].rearrange("p (a d) -> p a d", a=1).broadcast_to([P, GT, D]), ALU.add).then_inc(s_xb_ready, 1)
                pool.wait_ge(s_qk_ready, 2 * g + 2)
                pool.wait_ge(s_sc_done, GT * g + ONE)
                pool.sem_inc(s_pool_pace, 1)
                for k in range(R4):
                    pool.tensor_scalar(QTm[:, k, :], QT, head_pick[:, k:k + 1], None, ALU.mult).then_inc(s_qtm_ready, 1)

        @block.tensor
        def _(pe):
            mm = nc.tensor.matmul
            pe.wait_ge(s_a_in, 16 * (2 * CH8 + 1))
            pe.wait_ge(s_first_columns, 2)
            for lv in range(8):
                k = 2 ** (lv % 4)
                vec, mat = (AiC, Mt) if lv < 4 else (AjB, M)
                if lv:
                    pe.wait_ge(s_p_copied, lv)
                pw = bank[4 + lv % 2][:, 0:BLK * 8].rearrange("p (g k) -> p g k", g=BLK)
                for q in range(4):
                    n = 4 * lv + q
                    if n >= 4:
                        pe.wait_ge(s_m_copied, n - 3)
                        pe.wait_ge(s_mt_copied, n - 3)
                    for g in range(4 * q, 4 * q + 4):
                        last = mm(pw[:, g, 0:k], mat[:, g, :], vec[:, g, 0:k], start=True, stop=True)
                    if q == 3:
                        last.then_inc(s_pr_done, 1)
                    if lv == 7:
                        continue
                    if n >= 2:
                        pe.wait_ge(s_m_copied, n - 1)
                        pe.wait_ge(s_mt_copied, n - 1)
                    for g in range(4 * q, 4 * q + 4):
                        c = slice(P * (g % 4), P * (g % 4) + P)
                        mm(bank[2 * (q % 2)][:, c], Mt[:, g, :], M[:, g, :], start=True, stop=True)
                        sq = mm(bank[2 * (q % 2) + 1][:, c], M[:, g, :], Mt[:, g, :], start=True, stop=True)
                    sq.then_inc(s_sq_done, 1)
            pe.wait_ge(s_p_copied, 8)
            pe.wait_ge(s_rbd_ready, 1)
            hp = bank[6][:, 0:BLK * N].rearrange("p (g i) -> p g i", g=BLK)
            for g in range(BLK):
                last = mm(hp[:, g, :], Rbd[:, g, :, :].rearrange("p d j -> p (d j)"), AiC[:, g, :], start=True, stop=True)
            last.then_inc(s_h_done, 1)

            pe.wait_ge(s_wg_in, 32)
            pe.wait_ge(s_masks, 1)
            pe.wait_ge(s_m_copied, 28)
            pe.wait_ge(s_mt_copied, 28)
            with pe.Fori(0, GROUPS) as g:
                for q in range(GT):
                    pe.wait_ge(s_xn_ready, GT * g + q + 1)
                    last = nc.tensor.transpose(bank[0][:, P * q:P * q + P], xn[:, q, :], ident[:, :])
                last.then_inc(s_tr_done, 1)
                pe.wait_ge(s_xnT_ready, g + 1)
                pe.wait_ge(s_sig_ready, 2 * g + ONE)
                for q in range(GT):
                    gp = bank[1 + q // 2][:, (D + E) * (q % 2):(D + E) * (q % 2 + 1)]
                    mm(gp, xnT[:, P * q:P * q + P], wg_sb[:, :], start=True, stop=False)
                    last = mm(gp, ones[:, :], bg_sb[:, :], start=False, stop=True)
                    if q % 2:
                        last.then_inc(s_gate_done, 1)

            pe.wait_ge(s_sig_ready, 2 * GROUPS + ONE)
            with pe.Fori(0, GROUPS // 2) as h:
                for j in range(2):
                    pe.wait_ge(s_xg_ready, 2 * h + j + 1)
                    pe.wait_ge(s_rev_ready, 2 * h + ONE)
                    mm(bank[2 + j][:, :], flip[:, :], xg_all[:, bass.ds(GT * 2 * h + GT * j, GT), :].rearrange("p q d -> p (q d)"),
                       start=True, stop=True).then_inc(s_rev_done, 1)

            pe.wait_ge(s_w_in, 16 * 12)
            pe.wait_ge(s_rev_ready, GROUPS + ONE)
            yp = bank[6][:, :].rearrange("p (t d) -> p t d", d=CHD)
            with pe.Fori(0, GROUPS) as g:
                pe.wait_ge(s_toep_in, 16 * g + 16)
                pe.wait_ge(s_y_ready, g + ONE)
                for d in range(CHD):
                    mm(yp[:, :, d], toep[:, d, 0:P], xg_all[:, :, bass.ds(CHD * g + d, 1)].rearrange("p t a -> p (t a)"),
                       start=True, stop=False, skip_group_check=True)
                    last = mm(yp[:, 1::2, d], toep[:, d, P:SEQ], xg_all[:, 0::2, bass.ds(CHD * g + d, 1)].rearrange("p t a -> p (t a)"),
                              start=False, stop=True, skip_group_check=True)
                last.then_inc(s_ssm_done, 1)
                pe.wait_ge(s_gslot_ready, g + 1)
                for q in range(GT):
                    last = nc.tensor.transpose(bank[7][0:E, P * q:P * q + P], gslot[:, q, :], ident[:, :])
                last.then_inc(s_gT_done, 1)
                pe.wait_ge(s_gT_ready, g + 1)
                for q in range(GT):
                    last = mm(bank[7][:, P * q:P * q + P], gT[:, q, :], ebet[:, :], start=True, stop=True)
                last.then_inc(s_beta_done, 1)
                pe.wait_ge(s_slot_ready, g + 1)
                for e in range(E + 1):
                    if e < E:
                        for c in range(FC):
                            pe.wait_ge(s_hid_ready, (E * FC) * g + FC * (e - 1) + c + 1 + ONE if e else (E * FC) * g + ONE)
                            mm(bank[c][:, :], w1_sb[:, e, P * c:P * c + P], xnT[:, :], start=True, stop=True).then_inc(s_hid_done, 1)
                    if e > 0:
                        o, ee = bank[4 + (e - 1) % 2], e - 1
                        pe.wait_ge(s_hid_ready, (E * FC) * g + FC * ee + FC + ONE)
                        pe.wait_ge(s_tmp_ready, E * g + max(ee - 1, 0) + ONE)
                        for q in range(GT):
                            cols = slice(P * q, P * q + P)
                            mm(o[:, cols], xnT[:, cols], ident[:, :], start=True, stop=False)
                            mm(o[:, cols], ones[:, :], b2_sb[:, ee, :], start=False, stop=False)
                            for c in range(FC):
                                last = mm(o[:, cols], hT[:, ee % 2, c, cols], w2_sb[:, ee, c, :], start=False, stop=(c == FC - 1))
                        last.then_inc(s_o_done, 1)

            pe.wait_ge(s_l1_in, 160)
            pe.wait_ge(s_small_masks, 1)
            with pe.Fori(0, GROUPS) as g:
                pe.wait_ge(s_out_ready, g + ONE)
                for q in range(GT):
                    pe.wait_ge(s_n_ready, GT * g + q + 1)
                    last = nc.tensor.transpose(bank[4][:, P * q:P * q + P], xn[:, q, :], ident[:, :])
                last.then_inc(s_n_tr, 1)
                pe.wait_ge(s_n_T, g + 1)
                mm(bank[5][:, :], wqk[:, 0, :], xnT[:, :], start=True, stop=True).then_inc(s_qkv_done, 1)
                mm(bank[6][:, :], wqk[:, 1, :], xnT[:, :], start=True, stop=True).then_inc(s_qkv_done, 1)
                mm(bank[7][:, :], u1_sb[:, :], xnT[:, :], start=True, stop=True).then_inc(s_qkv_done, 1)
                for q in range(GT):
                    last = mm(bank[q // 2][:, 256 * (q % 2):256 * (q % 2) + 256], xnT[:, P * q:P * q + P],
                              wkv[:, :, :].rearrange("p a d -> p (a d)"), start=True, stop=True)
                    if q % 2:
                        last.then_inc(s_tok_done, 1)
                pe.wait_ge(s_pt_ready, g + 1)
                pe.wait_ge(s_v_ready, 2 * g + 2)
                for c in range(FC):
                    rows = slice(RANK * c, RANK * c + RANK)
                    last = mm(bank[c][:, :], v1_sb[rows, :], PT[rows, :], start=True, stop=True)
                last.then_inc(s_hf_done, 1)
                pe.wait_ge(s_qk_ready, 2 * g + 2)
                mm(bank[5][:, :], head_sum[:, :], KT, start=True, stop=True).then_inc(s_kc_done, 1)
                pe.wait_ge(s_kt_ready, g + 1)
                for b in range(2):
                    cols = slice(256 * b, 256 * b + P)
                    last = mm(bank[4][:, P * b:P * b + P], Ktok[:, cols], Vtok[:, cols], start=True, stop=True)
                last.then_inc(s_st_done, 1)
                pe.wait_ge(s_hf_ready, g + 1)
                for c in range(FC):
                    last = mm(bank[7][RANK * c:RANK * c + RANK, :], u2_sb[:, c, :], Hf[:, c, :], start=True, stop=True,
                              tile_position=(0, RANK * c))
                last.then_inc(s_qf_done, 1)
                pe.wait_ge(s_prod_ready, g + 1)
                mm(bank[6][:, :], same_head[:, :], prod, start=True, stop=True).then_inc(s_den_done, 1)
                pe.wait_ge(s_qtm_ready, R4 * g + R4)
                pe.wait_ge(s_st_ready, g + 1)
                pe.wait_ge(s_vm_ready, g + 1)
                for q in range(GT):
                    cols = slice(P * q, P * q + P)
                    for r in range(R4):
                        rows = slice(32 * r, 32 * r + 32)
                        pe.wait_ge(s_am_ready, GT * R4 * g + R4 * (q - 1) + r + 1 + ONE if q else GT * R4 * g + ONE)
                        last = mm(bank[r][:, :].rearrange("p (k t) -> p k t", k=R4), KT[rows, cols], QTm[rows, :, cols],
                                  start=True, stop=True)
                    last.then_inc(s_sc_done, 1)
                    if q == 0:
                        pe.wait_ge(s_prod_ready, g + 1)
                    av = bank[5][:, cols]
                    if q % 2:
                        mm(av, S[:, q // 2, :], QT[:, cols], start=True, stop=False, skip_group_check=True)
                    for r in range(R4):
                        rows = slice(32 * r, 32 * r + 32)
                        pe.wait_ge(s_am_ready, GT * R4 * g + R4 * q + r + 1 + ONE)
                        for k in range(R4):
                            last = mm(av[rows, :], Vm[:, q, r, k, :, :].rearrange("p l e -> p (l e)"), Am[:, r, k, :],
                                      start=(k == 0 and q % 2 == 0), stop=(k == R4 - 1), skip_group_check=True,
                                      tile_position=(0, 32 * r))
                    last.then_inc(s_av_done, 1)
                pe.wait_ge(s_attn_ready, g + 1)
                pe.wait_ge(s_qf_ready, g + 1)
                for q in range(GT):
                    cols = slice(P * q, P * q + P)
                    mm(bank[4][:, cols], attnT[:, cols], wo_sb[:, :], start=True, stop=False)
                    last = mm(bank[4][:, cols], QfT[:, cols], v2_sb[:, :], start=False, stop=True)
                last.then_inc(s_y_done, 1)

        @block.scalar
        def _(act):
            copy = nc.scalar.copy
            for lv in range(7):
                for q in range(4):
                    act.wait_ge(s_sq_done, 4 * lv + q + 1)
                    copy(Mt[:, 4 * q:4 * q + 4, :], bank[2 * (q % 2) + 1][:, :].rearrange("p (g c) -> p g c", g=4)).then_inc(s_mt_copied, 1)
            with act.Fori(0, GROUPS) as g:
                act.wait_ge(s_tr_done, g + 1 + ONE)
                copy(xnT[:, :], bank[0][:, :]).then_inc(s_xnT_ready, 1)
                copy(xnT_all[:, bass.ds(GW * g, GW)], bank[0][:, :]).then_inc(s_xnT_all_ready, 1)
                for j in range(2):
                    act.wait_ge(s_gate_done, 2 * g + j + 1)
                    gp = bank[1 + j][:, 0:2 * (D + E)].rearrange("p (q c) -> p q c", q=2)
                    copy(logits[:, bass.ds(GT * g + 2 * j, 2), :], gp[:, :, D:D + E])
                    nc.scalar.activation(xg_all[:, bass.ds(GT * g + 2 * j, 2), :], gp[:, :, 0:D], ACT.Sigmoid).then_inc(s_sig_ready, 1)
            with act.Fori(0, GROUPS // 2) as h:
                for j in range(2):
                    act.wait_ge(s_rev_done, 2 * h + j + 1)
                    copy(xg_all[:, bass.ds(GT * 2 * h + GT * j, GT), :].rearrange("p q d -> p (q d)"), bank[2 + j][:, :]).then_inc(s_rev_ready, 1)
            act.wait_ge(s_gap_ready, 1)
            nc.scalar.activation(m1[:, :], m3[:, :], ACT.Exp).then_inc(s_gap_exp, 1)
            with act.Fori(0, GROUPS) as g:
                act.wait_ge(s_ssm_done, g + 1)
                copy(y_all[:, :, bass.ds(CHD * g, CHD)], bank[6][:, :].rearrange("p (t d) -> p t d", d=CHD)).then_inc(s_y_ready, 1)
                act.wait_ge(s_gT_done, g + 1 + ONE)
                act.wait_ge(s_beta_done, g + ONE)
                copy(gT[:, :, :].rearrange("p q t -> p (q t)"), bank[7][0:E, :]).then_inc(s_gT_ready, 1)
                for e in range(E):
                    for c in range(FC):
                        act.wait_ge(s_hid_done, (E * FC) * g + FC * e + c + 1)
                        if c == 0:
                            act.wait_ge(s_o_done, E * g + max(e - 1, 0) + ONE)
                        nc.scalar.activation(hT[:, e % 2, c, :], bank[c][:, :], ACT.Gelu, bias=b1_sb[:, e, c:c + 1]).then_inc(s_hid_ready, 1)
            with act.Fori(0, GROUPS) as g:
                act.wait_ge(s_n_tr, g + 1)
                copy(xnT[:, :], bank[4][:, :]).then_inc(s_n_T, 1)
                for i, (ex, re) in enumerate(((Eq, Rq), (Ek, Rk))):
                    act.wait_ge(s_qkv_done, 3 * g + i + 1)
                    nc.scalar.activation(ex, bank[5 + i][:, :], ACT.Exp)
                    nc.scalar.activation(re, bank[5 + i][:, :], ACT.Relu).then_inc(s_ekv_ready, 1)
                act.wait_ge(s_qkv_done, 3 * g + 3)
                copy(PT, bank[7][:, :]).then_inc(s_pt_ready, 1)
                for j in range(2):
                    act.wait_ge(s_tok_done, 2 * g + j + 1)
                    kv = bank[j][:, :].rearrange("p (q a d) -> p q a d", q=2, a=2)
                    half = slice(256 * j, 256 * j + 256)
                    nc.scalar.activation(Ekt[:, half].rearrange("p (q d) -> p q d", q=2), kv[:, :, 0, :], ACT.Exp)
                    nc.scalar.activation(Rkt[:, half].rearrange("p (q d) -> p q d", q=2), kv[:, :, 0, :], ACT.Relu)
                    copy(Vtok[:, half].rearrange("p (q d) -> p q d", q=2), kv[:, :, 1, :]).then_inc(s_v_ready, 1)
                act.wait_ge(s_hf_done, g + 1)
                for c in range(FC):
                    last = nc.scalar.activation(Hf[:, c, :], bank[c][:, :], ACT.Gelu_apprx_tanh, bias=fb1_sb[:, c:c + 1])
                last.then_inc(s_hf_ready, 1)
                act.wait_ge(s_qf_done, g + 1)
                copy(QfT, bank[7][:, :]).then_inc(s_qf_ready, 1)

        @block.vector
        def _(dve):
            v = nc.vector
            chain = Count(dve, s_dve_chain)

            def inverse_root(var, eps):
                chain.mark(v.tensor_scalar(ve[:, :], var, eps, None, ALU.add))
                chain.wait()
                chain.mark(v.tensor_scalar(rstd[:, :].bitcast(I32), ve[:, :].bitcast(I32), 1, None, ALU.logical_shift_right))
                chain.wait()
                chain.mark(v.tensor_scalar(rstd[:, :].bitcast(I32), rstd[:, :].bitcast(I32), -1.0, float(0x5F3759DF), ALU.mult, ALU.add))
                chain.wait()
                for _ in range(NEWTON):
                    chain.mark(v.tensor_tensor(sq[:, :], rstd[:, :], rstd[:, :], ALU.mult))
                    chain.wait()
                    chain.mark(v.scalar_tensor_tensor(out=sq[:, :], in0=sq[:, :], scalar=-0.5, in1=ve[:, :], op0=ALU.mult, op1=ALU.mult))
                    chain.wait()
                    chain.mark(v.scalar_tensor_tensor(out=rstd[:, :], in0=sq[:, :], scalar=1.5, in1=rstd[:, :], op0=ALU.add, op1=ALU.mult))
                    chain.wait()

            def layer_norm(src, eps):
                dve.sem_inc(s_dve_pace, 1)
                for q in range(GT):
                    last = v.bn_stats(stats[:, q, :], src(q))
                chain.mark(last)
                chain.wait()
                dve.sem_inc(s_dve_pace, 1)
                for q in range(GT):
                    last = v.bn_aggr(mv[:, q, :], stats[:, q, :])
                chain.mark(last)
                chain.wait()
                inverse_root(mv[:, :, 1], eps)

            dve.wait_ge(s_masks, 1)
            v.tensor_reduce(head_pick[:, :], same_head[:, :].rearrange("p (r k e) -> p k r e", r=R4, k=R4)[:, :, :, 0], AXX, ALU.add)
            v.tensor_reduce(first_lag[:, :], ident[:, :].rearrange("p (i j) -> p i j", j=N)[:, :, 0], AXX, ALU.add)
            chain.mark(v.tensor_reduce(place8[:, :], ident[:, :].rearrange("p (h e) -> p e h", h=H), AXX, ALU.add))
            chain.wait()
            hs = head_sum[:, :].rearrange("p (h e) -> p h e", h=H)
            v.tensor_tensor(hs, hs, place8[:, :].rearrange("p (a e) -> p a e", a=1).broadcast_to([P, H, DH]), ALU.mult).then_inc(s_small_masks, 1)

            for lv in range(8):
                k = 2 ** (lv % 4)
                vec = AiC if lv < 4 else AjB
                if lv < 7:
                    for q in range(4):
                        dve.wait_ge(s_sq_done, 4 * lv + q + 1)
                        v.tensor_copy(M[:, 4 * q:4 * q + 4, :], bank[2 * (q % 2)][:, :].rearrange("p (g c) -> p g c", g=4)).then_inc(s_m_copied, 1)
                dve.wait_ge(s_pr_done, lv + 1)
                pw = bank[4 + lv % 2][:, 0:BLK * 8].rearrange("p (g k) -> p g k", g=BLK)
                v.tensor_copy(vec[:, :, k:2 * k], pw[:, :, 0:k]).then_inc(s_p_copied, 1)
            dve.wait_ge(s_p_copied, 8)
            for g in range(BLK):
                last = v.tensor_tensor(Rbd[:, g, :, :], AjB[:, g:g + 1, :].broadcast_to([P, CH8, N]),
                                       mask8[:, :].rearrange("p (d a) -> p d a", a=1).broadcast_to([P, CH8, N]), ALU.mult)
            last.then_inc(s_rbd_ready, 1)
            chain.mark(v.tensor_scalar(dp1[:, :], dp_sb[:, :], 1.0, first_lag[:, 0:1], ALU.add, ALU.mult))
            chain.wait()
            dve.wait_ge(s_h_done, 1)
            hp = bank[6][:, 0:BLK * N].rearrange("p (g i) -> p g i", g=BLK)
            v.tensor_copy(h_sb[:, :, 1:N], hp[:, :, 1:N])
            v.tensor_tensor(h_sb[:, :, 0], hp[:, :, 0], dp1[:, :], ALU.add).then_inc(s_h_ready, 1)

            dve.wait_ge(s_x_in, 64)
            start = chain.n
            with dve.Fori(0, GROUPS) as g:
                chain.base, chain.n = g * NORM + start, 0
                layer_norm(lambda q: x_all[:, bass.ds(GT * g + q, 1), :].rearrange("p a d -> p (a d)"), 1e-5)
                dve.wait_ge(s_tr_done, g + ONE)
                for q in range(GT):
                    v.tensor_scalar(xn[:, q, :], x_all[:, bass.ds(GT * g + q, 1), :].rearrange("p a d -> p (a d)"),
                                    mv[:, q, 0:1], rstd[:, q:q + 1], ALU.subtract, ALU.mult).then_inc(s_xn_ready, 1)
                dve.wait_ge(s_xn_ready, GT * g + GT)
                dve.wait_ge(s_sig_ready, 2 * g + 2 + ONE)
                xs = xg_all[:, bass.ds(GT * g, GT), :]
                v.tensor_tensor(xs, xs, xn[:, :, :], ALU.mult).then_inc(s_xg_ready, 1)
            chain.base, chain.n = start + GROUPS * NORM, 0

            full = [P, TILES, E]
            bc = lambda t: t[:, :].rearrange("p (t a) -> p t a", a=1).broadcast_to(full)
            rk = rank8[:, :].rearrange("p (a e) -> p a e", a=1).broadcast_to(full)

            def best(lg, mx, onehot):
                chain.mark(v.tensor_reduce(mx[:, :], lg, AXX, ALU.max))
                chain.wait()
                chain.mark(v.tensor_tensor(onehot, lg, bc(mx), ALU.is_ge))
                chain.wait()
                chain.mark(v.tensor_tensor(onehot, onehot, rk, ALU.mult))
                chain.wait()
                chain.mark(v.tensor_reduce(m3[:, :], onehot, AXX, ALU.max))
                chain.wait()
                chain.mark(v.tensor_tensor(onehot, rk, bc(m3), ALU.is_equal))
                chain.wait()

            dve.wait_ge(s_sig_ready, 2 * GROUPS + ONE)
            best(logits[:, :, :], m1, gates[:, :, :])
            chain.mark(v.scalar_tensor_tensor(out=t2[:, :, :], in0=gates[:, :, :], scalar=-3.0e38, in1=logits[:, :, :], op0=ALU.mult, op1=ALU.add))
            chain.wait()
            best(t2[:, :, :], m2, t1[:, :, :])
            chain.mark(v.tensor_tensor(m3[:, :], m2[:, :], m1[:, :], ALU.subtract))
            chain.wait()
            dve.sem_inc(s_gap_ready, 1)
            dve.wait_ge(s_gap_exp, 1)
            chain.mark(v.tensor_scalar(m2[:, :], m1[:, :], 1.0, None, ALU.add))
            chain.wait()
            chain.mark(v.reciprocal(m2[:, :], m2[:, :]))
            chain.wait()
            chain.mark(v.tensor_tensor(m3[:, :], m1[:, :], m2[:, :], ALU.mult))
            chain.mark(v.tensor_tensor(gates[:, :, :], gates[:, :, :], bc(m2), ALU.mult))
            chain.wait()
            chain.mark(v.tensor_tensor(t1[:, :, :], t1[:, :, :], bc(m3), ALU.mult))
            chain.wait()
            chain.mark(v.tensor_tensor(gates[:, :, :], gates[:, :, :], t1[:, :, :], ALU.add))
            chain.wait()

            start = chain.base + chain.n
            with dve.Fori(0, GROUPS) as g:
                chain.base, chain.n = g * ((NORM + 1) * E) + start, 0
                dve.wait_ge(s_gT_done, g + ONE)
                v.tensor_copy(gslot[:, :, :], gates[:, bass.ds(GT * g, GT), :]).then_inc(s_gslot_ready, 1)
                dve.wait_ge(s_beta_done, g + 1 + ONE)
                xs = x_all[:, bass.ds(GT * g, GT), :]
                v.tensor_tensor(xs, xs, bank[7][:, :].rearrange("p (q d) -> p q d", q=GT), ALU.add).then_inc(s_beta_added, 1)
                for e in range(E):
                    o = bank[4 + e % 2]
                    dve.wait_ge(s_o_done, E * g + e + 1 + ONE)
                    layer_norm(lambda q: o[:, P * q:P * q + P], 1e-6)
                    chain.mark(v.tensor_tensor(nr[:, e % 2, :], rstd[:, :], gslot[:, :, e], ALU.mult))
                    chain.wait()
                    dve.wait_ge(s_tmp_used, E * g + max(e - 1, 0) + ONE)
                    for q in range(GT):
                        last = v.tensor_scalar(tmp[:, e % 2, q, :], o[:, P * q:P * q + P], mv[:, q, 0:1], nr[:, e % 2, q:q + 1],
                                               ALU.subtract, ALU.mult)
                    last.then_inc(s_tmp_ready, 1)
            chain.base, chain.n = start + GROUPS * (NORM + 1) * E, 0

            dve.wait_ge(s_tmp_used, E * GROUPS + ONE)
            dve.wait_ge(s_y_ready, GROUPS + ONE)
            dve.wait_ge(s_const_in, 64)
            v.memset(Vm, 0.0)
            start = chain.base + chain.n
            with dve.Fori(0, GROUPS) as g:
                chain.base, chain.n = g * (2 * NORM + 6) + start, 0
                xs = x_all[:, bass.ds(GT * g, GT), :]
                ys = y_all[:, bass.ds(GT * g, GT), :]
                one = lambda t, q: t[:, bass.ds(GT * g + q, 1), :].rearrange("p a d -> p (a d)")
                layer_norm(lambda q: one(y_all, q), 1e-5)
                for q in range(GT):
                    last = v.tensor_scalar(one(y_all, q), one(y_all, q), mv[:, q, 0:1], rstd[:, q:q + 1], ALU.subtract, ALU.mult)
                chain.mark(last)
                chain.wait()
                row = lambda t: t[:, :].rearrange("p (a d) -> p a d", a=1).broadcast_to([P, GT, D])
                chain.mark(v.tensor_tensor(ys, ys, row(gam_bc), ALU.mult))
                chain.mark(v.tensor_tensor(xs, xs, row(bet_bc), ALU.add))
                chain.wait()
                chain.mark(v.tensor_tensor(xs, xs, ys, ALU.add))
                chain.wait()
                layer_norm(lambda q: one(x_all, q), 1e-5)
                for q in range(GT):
                    v.tensor_scalar(xn[:, q, :], one(x_all, q), mv[:, q, 0:1], rstd[:, q:q + 1], ALU.subtract, ALU.mult).then_inc(s_n_ready, 1)
                for i, (ex, re, to) in enumerate(((Eq, Rq, QT), (Ek, Rk, KT))):
                    dve.wait_ge(s_ekv_ready, 2 * g + i + 1)
                    v.scalar_tensor_tensor(out=to, in0=ex, scalar=1.0, in1=re, op0=ALU.min, op1=ALU.add).then_inc(s_qk_ready, 1)
                dve.wait_ge(s_v_ready, 2 * g + 2)
                v.scalar_tensor_tensor(out=Ktok, in0=Ekt, scalar=1.0, in1=Rkt, op0=ALU.min, op1=ALU.add).then_inc(s_kt_ready, 1)
                for q in range(GT):
                    full_v = Vm[:, q, :, :, :, :].rearrange("p r k l e -> p r (k l) e")
                    last = v.tensor_copy(full_v[:, :, 0:16:5, :], Vtok[:, P * q:P * q + P].rearrange("p (r k e) -> p r k e", r=R4, k=R4))
                last.then_inc(s_vm_ready, 1)
                dve.wait_ge(s_qk_ready, 2 * g + 2)
                dve.wait_ge(s_kc_done, g + 1)
                v.tensor_tensor(prod, QT, bank[5][:, :], ALU.mult).then_inc(s_prod_ready, 1)
                dve.wait_ge(s_st_done, g + 1)
                v.tensor_tensor(S[:, :, :], bank[4][:, 0:2 * P].rearrange("p (b c) -> p b c", b=2),
                                same_head[:, :].rearrange("p (a c) -> p a c", a=1).broadcast_to([P, 2, P]), ALU.mult).then_inc(s_st_ready, 1)
                dve.wait_ge(s_den_done, g + 1)
                chain.mark(v.tensor_scalar(zr, bank[6][:, :], 1e-6, None, ALU.add))
                chain.wait()
                chain.mark(v.reciprocal(zr, zr))
                for q in range(GT):
                    dve.wait_ge(s_sc_done, GT * g + q + 1 + ONE)
                    dve.wait_ge(s_av_done, GT * g + q + ONE)
                    for r in range(R4):
                        v.tensor_tensor(Am[:, r, :, :], bank[r][:, :].rearrange("p (k t) -> p k t", k=R4),
                                        causal[:, :].rearrange("p (a t) -> p a t", a=1).broadcast_to([P, R4, P]), ALU.mult).then_inc(s_am_ready, 1)
                chain.wait()
                dve.wait_ge(s_av_done, GT * g + GT + ONE)
                v.tensor_tensor(attnT, bank[5][:, :], zr, ALU.mult).then_inc(s_attn_ready, 1)
                dve.wait_ge(s_y_done, g + 1)
                dve.wait_ge(s_xb_ready, g + 1)
                dve.wait_ge(s_out_done, 16 * g + ONE)
                v.tensor_tensor(yo.rearrange("p (q d) -> p q d", q=GT), bank[4][:, :].rearrange("p (q d) -> p q d", q=GT), xs, ALU.add).then_inc(s_out_ready, 1)


def kernel(**inputs):
    import numpy as np
    import concourse.bacc as bacc
    from concourse.bass_utils import run_bass_kernel_spmd

    a = {k: np.asarray(v) for k, v in inputs.items()}
    pairs = lambda t: t.reshape(BLK, CH8, N).transpose(1, 2, 0).reshape(P, BLK)
    laid = [
        ("x", a["L0_attn_x"].reshape(TILES * P, D)),
        ("A", a["L0_attn_A"]),
        ("At", a["L0_attn_A"].transpose(0, 2, 1)),
        ("BpT", pairs(a["L0_attn_Bp"])),
        ("CpT", pairs(a["L0_attn_Cp"])),
        ("DpR", np.repeat(a["L0_attn_Dp"].reshape(BLK, CH8).T, N, axis=0)),
        ("WgRw", np.concatenate([a["L0_attn_Wg"].T, a["L0_ffn_router_w"]], axis=1)),
        ("bg", a["L0_attn_bg"].reshape(1, D)),
        ("gamma", a["L0_attn_gamma"]),
        ("beta", a["L0_attn_beta"]),
        ("w1", a["L0_ffn_w1"]),
        ("b1T", a["L0_ffn_b1"].reshape(E, FC, P).transpose(2, 0, 1)),
        ("w2", a["L0_ffn_w2"]),
        ("b2", a["L0_ffn_b2"]),
        ("egamma", a["L0_ffn_gamma"]),
        ("ebeta", a["L0_ffn_beta"]),
        ("Wq", a["L1_attn_Wq"]),
        ("Wk", a["L1_attn_Wk"]),
        ("Wv", a["L1_attn_Wv"]),
        ("Wo", a["L1_attn_Wo"]),
        ("bo", a["L1_attn_bo"]),
        ("U1R", np.concatenate([a["L1_ffn_U1"]] * FC, axis=1)),
        ("V1", a["L1_ffn_V1"].reshape(RANK, FC, P).transpose(1, 0, 2).reshape(P, P)),
        ("fb1T", a["L1_ffn_b1"].reshape(FC, P).T),
        ("U2", a["L1_ffn_U2"]),
        ("V2R", np.concatenate([a["L1_ffn_V2"]] * FC, axis=0)),
        ("fb2", a["L1_ffn_b2"]),
    ]
    nc = bacc.Bacc("TRN2", target_bir_lowering=False, num_devices=1)
    arrays, args = {}, []
    for name, t in laid:
        t = np.ascontiguousarray(t)
        arrays[f"in_{name}"] = t
        args.append(nc.dram_tensor(f"in_{name}", t.shape, F32, kind="ExternalInput").ap())
    out = nc.dram_tensor("out_x", (TILES * P, D), F32, kind="ExternalOutput").ap()
    two_layer_kernel(nc, *args, out)
    r = run_bass_kernel_spmd(nc, [arrays], core_ids=[0])
    return r.results[0]["out_x"].reshape(BATCH, SEQ, D)
```

```python
from contextlib import ExitStack

import concourse.bass as bass
from concourse import mybir

F32 = mybir.dt.float32
I32 = mybir.dt.int32
ALU = mybir.AluOpType
ACT = mybir.ActivationFunctionType
AXX = mybir.AxisListType.X

P = 128
D = 128
BATCH, SEQ = 16, 256
TILES = BATCH * SEQ // P
GT = 4
GROUPS = TILES // GT
GW = GT * P
N = 16
CH8 = P // N
BLK = D // CH8
E = 8
F = 512
FC = F // P
CHD = D // GROUPS
HPAD = SEQ + P
H, DH = 16, 8
R4 = 4
RANK = 32
TOPK = 2
MQ = 2
MW = MQ * P
MTILES = (TILES * P * TOPK + E * (MW - 1)) // MW
MTILES += -MTILES % 4
SLOTS = MTILES * MW
LEAD = 2
ONE = 1
NEWTON = 3
NORM = 2 + 3 + 3 * NEWTON


class Count:

    def __init__(self, eng, sem):
        self.eng, self.sem, self.base, self.n = eng, sem, 0, 0

    def mark(self, ins):
        self.n += 1
        ins.then_inc(self.sem, 1)

    def wait(self):
        self.eng.wait_ge(self.sem, self.base + self.n)

    def enter(self, i, per):
        self.start, self.per = self.base + self.n, per
        self.base, self.n = i * per + self.start, 0

    def leave(self, trips):
        assert self.n == self.per, (self.n, self.per)
        self.base, self.n = self.start + trips * self.per, 0


def two_layer_kernel(nc, x, A, At, BpT, CpT, DpR, WgRw, bg, gamma, beta, w1, b1T, w2, b2, egamma, ebeta,
                     Wq, Wk, Wv, Wo, bo, U1R, V1, fb1T, U2, V2R, fb2, out):
    with ExitStack() as ctx:
        def sb(name, shape):
            return ctx.enter_context(nc.sbuf_tensor(name, shape, F32))

        def sem(name):
            return ctx.enter_context(nc.semaphore(name))

        x_all = sb("x_all", [P, TILES, D])
        xn_all = sb("xn_all", [P, TILES, D])
        xg_all = sb("xg_all", [P, TILES, D])
        y_all = sb("y_all", [P, TILES, D])
        w1_sb = sb("w1_sb", [P, E, F])
        w2_sb = sb("w2_sb", [P, E, FC, D])
        b1_sb = sb("b1_sb", [P, E, FC])
        etab = sb("etab", [P, 3, E, D])
        eb2, egam, ebet = [etab[:, i, :, :] for i in range(3)]
        gam_bc = sb("gam_bc", [P, D])
        bet_bc = sb("bet_bc", [P, D])
        wg_sb = sb("wg_sb", [P, D + E])
        bg_sb = sb("bg_sb", [1, D + E])
        ident = sb("ident", [P, P])
        flip = sb("flip", [P, P])
        ones = sb("ones", [1, P])
        big = sb("big", [P, 2 * BLK * P])
        M = big[:, 0:BLK * P].rearrange("p (g c) -> p g c", g=BLK)
        Mt = big[:, BLK * P:].rearrange("p (g c) -> p g c", g=BLK)
        toep2 = sb("toep2", [P, 2 * BLK * P])
        toep = [t[:, :].rearrange("p (d u) -> p d u", d=CHD) for t in (big, toep2)]
        AiC = sb("AiC", [P, BLK, N])
        AjB = sb("AjB", [P, BLK, N])
        bc_sb = sb("bc_sb", [P, 2, BLK])
        mask8 = sb("mask8", [P, CH8])
        first_lag = sb("first_lag", [P, 1])
        dp_sb = sb("dp_sb", [P, BLK])
        dp1 = sb("dp1", [P, BLK])
        h_sb = sb("h_sb", [P, BLK, N])
        zero_sb = sb("zero_sb", [P, P])
        mid = sb("mid", [P, 4096])
        Rbd = mid[:, 0:BLK * P].rearrange("p (g d j) -> p g d j", g=BLK, d=CH8)
        hT = mid[:, 0:2048].rearrange("p (s c t) -> p s c t", s=2, c=FC)
        w1s = mid[:, 2048:3072].rearrange("p (s f) -> p s f", s=2)
        eo = mid[:, 3072:4096].rearrange("p (s q d) -> p s q d", s=4, q=MQ)
        res = sb("res", [P, 2, MQ, D])
        xt = sb("xt", [P, 4, MQ, D])
        xb = sb("xb", [P, 4, MQ, D])
        xT = sb("xT", [P, 2, MW])
        stats = sb("stats", [P, TILES, 6])
        mv = sb("mv", [P, TILES, 2])
        rstd = sb("rstd", [P, TILES])
        ve = sb("ve", [P, TILES])
        sq = sb("sq", [P, TILES])
        mv4 = sb("mv4", [P, GT, 2])
        rstd4 = sb("rstd4", [P, GT])
        xn = sb("xn", [P, GT, D])
        xnT = sb("xnT", [P, GW])
        logits = sb("logits", [P, TILES, E])
        hot1 = sb("hot1", [P, TILES, E])
        mask = sb("mask", [P, TILES, E])
        cum = sb("cum", [P, TILES, E])
        off = sb("off", [P, TILES, E])
        counts = sb("counts", [P, 4, E])
        ends = sb("ends", [P, 2, E])
        starts = sb("starts", [P, MTILES])
        eidf = sb("eidf", [P, MTILES])
        eid = ctx.enter_context(nc.sbuf_tensor("eid", [P, MTILES], I32))
        pos = ctx.enter_context(nc.sbuf_tensor("pos", [P, TOPK, TILES], I32))
        posf = sb("posf", [P, TILES])
        gw = sb("gw", [P, TOPK, TILES])
        ones_sq = sb("ones_sq", [P, P])
        hot2 = sb("hot2", [P, TILES, E])
        t2 = sb("t2", [P, TILES, E])
        rank8 = sb("rank8", [P, E])
        place8 = sb("place8", [P, DH])
        m1 = sb("m1", [P, TILES])
        m2 = sb("m2", [P, TILES])
        m3 = sb("m3", [P, TILES])
        eps_sb = sb("eps_sb", [P, 1])

        wqk = sb("wqk", [P, 2, D])
        wkv = sb("wkv", [P, 2, D])
        wo_sb = sb("wo_sb", [P, D])
        u1_sb = sb("u1_sb", [P, P])
        v1_sb = sb("v1_sb", [P, P])
        u2_sb = sb("u2_sb", [P, FC, RANK])
        v2_sb = sb("v2_sb", [P, D])
        fb1_sb = sb("fb1_sb", [P, FC])
        bo_bc = sb("bo_bc", [P, D])
        fb2_bc = sb("fb2_bc", [P, D])
        causal = sb("causal", [P, P])
        same_head = sb("same_head", [P, P])
        head_sum = sb("head_sum", [P, P])
        head_pick = sb("head_pick", [P, R4])
        Am = [t.rearrange("p (r k t) -> p r k t", r=R4, k=R4) for t in (mid[:, 0:2048], toep2[:, 0:2048])]
        Hf = mid[:, 2048:4096].rearrange("p (c t) -> p c t", c=FC)
        xg_flat = xg_all[:, :, :].rearrange("p a b -> p (a b)")
        etab_flat = etab[:, :, :, :].rearrange("p i e d -> p (i e d)")
        QTm = [t.rearrange("p (k t) -> p k t", k=R4) for t in (xg_flat[:, 0:2048], toep2[:, 2048:4096])]
        Vm = [t.rearrange("p (q r k l e) -> p q r k l e", q=GT, r=R4, k=R4, l=R4) for t in (xg_flat[:, 2048:4096], etab_flat[:, 0:2048])]
        l1 = big[:, :].rearrange("p (s t) -> p s t", s=8)
        QT, KT, (Rq, Rk, zr, prod) = (l1[:, 0, :], l1[:, 1, :]), (l1[:, 2, :], l1[:, 3, :]), [l1[:, i, :] for i in range(4, 8)]
        l2 = xn_all[:, :, :].rearrange("p a b -> p (a b)").rearrange("p (s t) -> p s t", s=8)
        Ktok, Rkt, Vtok, PT, QfT, attnT = [l2[:, i, :] for i in range(6)]
        yo = (l2[:, 6, :], l2[:, 7, :])
        S = [sb(f"S{p}", [P, 2, P]) for p in range(2)]

        bank = [ctx.enter_context(nc.psum_tensor(f"bank{i}", [P, 512], F32)) for i in range(8)]
        y1_all = w1_sb[:, :, :].rearrange("p e f -> p (e f)").rearrange("p (t d) -> p t d", d=D)
        y2_all = w2_sb[:, :, :, :].rearrange("p e c d -> p (e c) d")
        slots_in = nc.dram_tensor("slots_in", [SLOTS, D], F32, kind="Internal")
        slots_out = nc.dram_tensor("slots_out", [SLOTS, D], F32, kind="Internal")
        h_dram = nc.dram_tensor("impulse_responses", [D, HPAD], F32, kind="Internal")

        s_x_in = sem("x_in")
        s_a_in = sem("a_in")
        s_wg_in = sem("wg_in")
        s_const_in = sem("const_in")
        s_w_in = sem("w_in")
        s_l1_in = sem("l1_in")
        s_zeroed = sem("zeroed")
        s_masks = sem("masks")
        s_sq_done = sem("sq_done")
        s_m_copied = sem("m_copied")
        s_pr_done = sem("pr_done")
        s_p_copied = sem("p_copied")
        s_rbd_ready = sem("rbd_ready")
        s_h_done = sem("h_done")
        s_h_ready = sem("h_ready")
        s_h_out = sem("h_out")
        s_toep_in0 = sem("toep_in0")
        s_toep_in1 = sem("toep_in1")
        s_xn_ready = sem("xn_ready")
        s_xn_saved = sem("xn_saved")
        s_tr_done = sem("tr_done")
        s_xnT_ready = sem("xnT_ready")
        s_gate_done = sem("gate_done")
        s_sig_ready = sem("sig_ready")
        s_xg_ready = sem("xg_ready")
        s_rev_done = sem("rev_done")
        s_rev_ready = sem("rev_ready")
        s_mask_ready = sem("mask_ready")
        s_counted = sem("counted")
        s_pos_ready = sem("pos_ready")
        s_gap_ready = sem("gap_ready")
        s_gap_exp = sem("gap_exp")
        s_slots_zeroed = sem("slots_zeroed")
        s_scattered = sem("scattered")
        s_xT_tr = sem("xT_tr")
        s_xT_ready = sem("xT_ready")
        s_w1s_ready = sem("w1s_ready")
        s_xb_ready = sem("xb_ready")
        s_hid_done = sem("hid_done")
        s_hid_ready = sem("hid_ready")
        s_o_done = sem("o_done")
        s_res_ready = sem("res_ready")
        s_e_ready = sem("e_ready")
        s_e_scaled = sem("e_scaled")
        s_st_ready = sem("st_ready")
        s_ssm_done = sem("ssm_done")
        s_y_ready = sem("y_ready")
        s_gathered = sem("gathered")
        s_pool_chain = sem("pool_chain")
        s_dve_chain = sem("dve_chain")
        s_n_ready = sem("n_ready")
        s_n_tr = sem("n_tr")
        s_n_T = sem("n_T")
        s_q_done = sem("q_done")
        s_ekv_ready = sem("ekv_ready")
        s_qk_ready = sem("qk_ready")
        s_vm_ready = sem("vm_ready")
        s_qtm_ready = sem("qtm_ready")
        s_kt_ready = sem("kt_ready")
        s_kc_done = sem("kc_done")
        s_u_done = sem("u_done")
        s_k_done = sem("k_done")
        s_den_ready = sem("den_ready")
        s_zr_ready = sem("zr_ready")
        s_base_ready = sem("base_ready")
        s_bet_added = sem("bet_added")
        s_prod_ready = sem("prod_ready")
        s_den_done = sem("den_done")
        s_st_done = sem("st_done")
        s_s_ready = sem("s_ready")
        s_sc_done = sem("sc_done")
        s_am_ready = sem("am_ready")
        s_av_done = sem("av_done")
        s_attn_ready = sem("attn_ready")
        s_pt_ready = sem("pt_ready")
        s_hf_done = sem("hf_done")
        s_hf_ready = sem("hf_ready")
        s_qf_done = sem("qf_done")
        s_qf_ready = sem("qf_ready")
        s_y_done = sem("y_done")
        s_out_ready = sem("out_ready")
        s_v_ready = sem("v_ready")
        s_tok_done = sem("tok_done")
        s_bias_ready = sem("bias_ready")
        s_small_masks = sem("small_masks")
        s_dve_pace = sem("dve_pace")
        s_pool_pace = sem("pool_pace")
        s_act_pace = sem("act_pace")
        s_bc_in = sem("bc_in")
        s_first_columns = sem("first_columns")
        s_group_in = [sem(f"group_in{g}") for g in range(GROUPS)]
        s_toep_in = (s_toep_in0, s_toep_in1)
        s_xt_in = [sem(f"xt_in{r}") for r in range(4)]
        s_out_stored = [sem(f"out_stored{p}") for p in range(2)]
        s_st_out = [sem(f"st_out{r}") for r in range(4)]

        block = ctx.enter_context(nc.Block())

        x_t = x.rearrange("(t p) d -> p t d", p=P)
        out_t = out.rearrange("(t p) d -> p t d", p=P)

        @block.sync
        def _(sp):
            sp.dma_start(wg_sb[:, :], WgRw).then_inc(s_wg_in, 16)
            sp.dma_start(bg_sb[:, 0:D], bg).then_inc(s_wg_in, 16)
            for k in range(4):
                sp.dma_start(x_all[:, 8 * k:8 * k + 8, :], x_t[:, 8 * k:8 * k + 8, :]).then_inc(s_x_in, 16)
            sp.wait_ge(s_zeroed, 1)
            for i in range(CH8):
                rows = slice(N * i, N * i + N)
                sp.dma_start(M[rows, :, rows], A.rearrange("(g i) n m -> i n g m", i=CH8)[i]).then_inc(s_a_in, 16)
                sp.dma_start(Mt[rows, :, rows], At.rearrange("(g i) n m -> i n g m", i=CH8)[i]).then_inc(s_a_in, 16)
            sp.dma_start(bc_sb[:, 0, :], CpT).then_inc(s_bc_in, 16)
            sp.dma_start(bc_sb[:, 1, :], BpT).then_inc(s_bc_in, 16)
            sp.dma_start(dp_sb[:, :], DpR).then_inc(s_a_in, 16)
            for src, dst in ((gamma, gam_bc), (beta, bet_bc), (bo, bo_bc), (fb2, fb2_bc)):
                sp.dma_start(dst[:, :], src.rearrange("(a d) -> a d", a=1).broadcast_to([P, D])).then_inc(s_const_in, 16)
            sp.dma_start(slots_in.ap().rearrange("(q p) d -> p q d", p=P),
                         zero_sb[:, :].rearrange("p (a d) -> p a d", a=1).broadcast_to([P, SLOTS // P, D])).then_inc(s_slots_zeroed, 16)
            sp.dma_start(b1_sb[:, :, :], b1T).then_inc(s_w_in, 16)
            for src, dst in ((b2, eb2), (egamma, egam), (ebeta, ebet)):
                sp.dma_start(dst, src.rearrange("(a e) d -> a e d", a=1).broadcast_to([P, E, D])).then_inc(s_w_in, 16)
            for k in range(4):
                sp.dma_start(w1_sb[:, 2 * k:2 * k + 2, :], w1.rearrange("e d f -> d e f")[:, 2 * k:2 * k + 2, :]).then_inc(s_w_in, 16)
                sp.dma_start(w2_sb[:, 2 * k:2 * k + 2, :, :],
                             w2.rearrange("e (c f) d -> f e c d", c=FC)[:, 2 * k:2 * k + 2]).then_inc(s_w_in, 16)
            sp.wait_ge(s_h_ready, 1)
            for i in range(CH8):
                sp.dma_start(h_dram.ap().rearrange("(g i) (j k) -> i j g k", i=CH8, k=N)[i, P // N:HPAD // N],
                             h_sb[N * i:N * i + N, :, :]).then_inc(s_h_out, 16)
            sp.dma_start(h_dram.ap()[:, 0:P], zero_sb[:, :]).then_inc(s_h_out, 16)
            for src, dst in ((Wq, wqk[:, 0, :]), (Wk, wqk[:, 1, :]), (Wk, wkv[:, 0, :]), (Wv, wkv[:, 1, :]), (Wo, wo_sb[:, :]),
                             (U1R, u1_sb[:, :]), (V2R, v2_sb[:, :]), (fb1T, fb1_sb[:, :]),
                             (V1, v1_sb[:, :]), (U2.rearrange("(c f) r -> f c r", c=FC), u2_sb[:, :, :])):
                sp.dma_start(dst, src).then_inc(s_l1_in, 16)
            sp.wait_ge(s_h_out, 16 * (CH8 + 1))
            for g in range(GROUPS):
                if g >= 2:
                    sp.wait_ge(s_ssm_done, g - 1)
                sp.dma_start(toep[g % 2], bass.AP(tensor=h_dram, offset=g * (CHD * HPAD) + 1,
                                                  ap=[[1, P], [HPAD, CHD], [1, SEQ]])).then_inc(s_toep_in[g % 2], 16)

            slots_r = slots_in.ap().rearrange("(j q p) d -> p j q d", q=MQ, p=P)
            slots_w = slots_out.ap().rearrange("(j q p) d -> p j q d", q=MQ, p=P)

            def load(j, r):
                sp.dma_start(xt[:, r, :, :], slots_r[:, bass.ds(j, 1), :, :].rearrange("p a q d -> p (a q) d")).then_inc(s_xt_in[r], 16)

            def store(j, r):
                sp.wait_ge(s_st_ready, j + 1)
                sp.dma_start(slots_w[:, bass.ds(j, 1), :, :].rearrange("p a q d -> p (a q) d"), eo[:, r, :, :]).then_inc(s_st_out[r], 16)

            def refill(j, r):
                sp.wait_ge(s_xT_tr, j + 1)
                sp.wait_ge(s_xb_ready, j + 1)
                load(j + 4, r)

            sp.wait_ge(s_scattered, 16 * TOPK * TILES)
            for r in range(4):
                load(r, r)
            for r in range(4):
                refill(r, r)
            with sp.Fori(0, MTILES // 4 - 2) as i:
                for r in range(4):
                    refill(4 * i + r + 4, r)
                    store(4 * i + r, r)
            for j in range(MTILES - 8, MTILES):
                store(j, j % 4)
            with sp.Fori(0, GROUPS // 2) as i:
                for p in range(2):
                    g = 2 * i + p
                    sp.wait_ge(s_out_ready, g + 1 + ONE)
                    sp.dma_start(out_t[:, bass.ds(GT * g, GT), :], yo[p].rearrange("p (q d) -> p q d", q=GT)).then_inc(s_out_stored[p], 16)
            for p in range(2):
                sp.wait_ge(s_out_stored[p], 16 * (GROUPS // 2) + ONE)

        @block.gpsimd
        def _(pool):
            chain = Count(pool, s_pool_chain)
            for started in (s_sig_ready, s_rev_ready, s_y_ready, s_out_ready, s_tr_done, s_xn_saved, s_attn_ready,
                            *s_out_stored, *s_st_out):
                pool.sem_inc(started, ONE)
            for started in (s_res_ready, s_o_done, s_e_ready, s_av_done):
                pool.sem_inc(started, LEAD)
            pool.memset(zero_sb[:, :], 0.0)
            pool.memset(big[:, :], 0.0).then_inc(s_zeroed, 1)
            pool.memset(ones[:, :], 1.0)
            pool.memset(bg_sb[:, D:], 0.0)
            pool.memset(eps_sb[:, :], 1e-6)
            for t in (ident, flip, causal, same_head, head_sum, mask8, ones_sq):
                last = pool.memset(t[:, :], 1.0)
            chain.mark(last)
            chain.wait()

            def keep(t, view, pattern, base, mult, op):
                pool.affine_select(out=view, in_=view, pattern=pattern, compare_op=op, fill=0.0, base=base,
                                   channel_multiplier=mult)

            keep(ident, ident[:, :], [[-1, P]], 0, 1, ALU.is_equal)
            keep(flip, flip[:, :], [[1, P]], 1 - P, 1, ALU.is_equal)
            keep(causal, causal[:, :], [[1, P]], 0, -1, ALU.is_ge)
            last = pool.affine_select(out=mask8[:, :], in_=mask8[:, :], pattern=[[-N, CH8]], compare_op=ALU.is_ge, fill=0.0,
                                      base=0, channel_multiplier=1)
            hv = same_head[:, :].rearrange("p (h e) -> p h e", h=H)
            pool.affine_select(out=hv, in_=hv, pattern=[[-DH, H], [0, DH]], compare_op=ALU.is_ge, fill=0.0,
                               base=0, channel_multiplier=1)
            sv = head_sum[:, :].rearrange("p (h e) -> p h e", h=H)
            last = pool.affine_select(out=sv, in_=sv, pattern=[[DH, H], [1, DH]], compare_op=ALU.is_ge, fill=0.0,
                                      base=0, channel_multiplier=-1)
            chain.mark(last)
            chain.wait()
            last = pool.affine_select(out=mask8[:, :], in_=mask8[:, :], pattern=[[N, CH8]], compare_op=ALU.is_ge, fill=0.0,
                                      base=N - 1, channel_multiplier=-1)
            chain.mark(pool.affine_select(out=hv, in_=hv, pattern=[[DH, H], [0, DH]], compare_op=ALU.is_ge, fill=0.0,
                                      base=DH - 1, channel_multiplier=-1))
            pool.iota(starts[:, :], pattern=[[MW, MTILES]], base=0, channel_multiplier=0, allow_small_or_imprecise_dtypes=True)
            chain.mark(pool.iota(rank8[:, :], pattern=[[-1, E]], base=E, channel_multiplier=0,
                                 allow_small_or_imprecise_dtypes=True))
            chain.wait()
            pool.sem_inc(s_masks, 1)

            pool.wait_ge(s_bc_in, 32)
            pool.tensor_copy(AiC[:, :, 0], bc_sb[:, 0, :]).then_inc(s_first_columns, 1)
            pool.tensor_copy(AjB[:, :, 0], bc_sb[:, 1, :]).then_inc(s_first_columns, 1)

            with pool.Fori(0, GROUPS) as g:
                pool.wait_ge(s_xn_ready, GT * g + GT)
                pool.sem_inc(s_pool_pace, 1)
                pool.tensor_copy(xn_all[:, bass.ds(GT * g, GT), :], xn[:, :, :]).then_inc(s_xn_saved, 1)

            pool.wait_ge(s_slots_zeroed, 16)
            pool.wait_ge(s_pos_ready, 1)
            pool.wait_ge(s_xn_saved, GROUPS + ONE)
            for t in range(TILES):
                for k in range(TOPK):
                    pool.indirect_dma_start(out=slots_in.ap(), out_offset=bass.IndirectOffsetOnAxis(ap=pos[:, k, t:t + 1], axis=0),
                                            in_=xn_all[:, t, :], in_offset=None).then_inc(s_scattered, 16)

            pool.wait_ge(s_const_in, 64)
            row = lambda t: t[:, :].rearrange("p (a d) -> p a d", a=1).broadcast_to([P, GT, D])
            pool.tensor_tensor(bo_bc[:, :], bo_bc[:, :], fb2_bc[:, :], ALU.add).then_inc(s_bias_ready, 1)
            with pool.Fori(0, GROUPS) as g:
                xs = x_all[:, bass.ds(GT * g, GT), :]
                pool.tensor_tensor(xs, xs, row(bet_bc), ALU.add).then_inc(s_bet_added, 1)

            def prepare(j, k, r):
                e = pool.value_load(eid[0:1, bass.ds(j, 1)], min_val=0, max_val=E - 1)
                pool.wait_ge(s_xt_in[r], 16 * k + 16)
                if not isinstance(j, int):
                    pool.wait_ge(s_res_ready, j - 3 + LEAD)
                    pool.sem_inc(s_pool_pace, 1)
                pool.tensor_tensor(xb[:, r, :, :], xt[:, r, :, :], eb2[:, bass.ds(e, 1), :].broadcast_to([P, MQ, D]), ALU.add)\
                    .then_inc(s_xb_ready, 1)

            def scale(j, r):
                e = pool.value_load(eid[0:1, bass.ds(j, 1)], min_val=0, max_val=E - 1)
                pool.wait_ge(s_e_ready, j + 1 + LEAD)
                pool.sem_inc(s_pool_pace, 1)
                pool.tensor_tensor(eo[:, r, :, :], eo[:, r, :, :], egam[:, bass.ds(e, 1), :].broadcast_to([P, MQ, D]), ALU.mult)\
                    .then_inc(s_e_scaled, 1)
                pool.wait_ge(s_e_scaled, j + 1)
                pool.sem_inc(s_pool_pace, 1)
                pool.tensor_tensor(eo[:, r, :, :], eo[:, r, :, :], ebet[:, bass.ds(e, 1), :].broadcast_to([P, MQ, D]), ALU.add)\
                    .then_inc(s_st_ready, 1)

            pool.wait_ge(s_w_in, 16 * 12)
            for j in range(4):
                prepare(j, 0, j)
            with pool.Fori(0, MTILES // 4 - 1) as i:
                for b in range(2):
                    for r in (2 * b, 2 * b + 1):
                        scale(4 * i + r, r)
                    for r in (2 * b, 2 * b + 1):
                        prepare(4 * i + r + 4, i + 1, r)
            for r in range(4):
                scale(MTILES - 4 + r, r)

            for r in range(4):
                pool.wait_ge(s_st_out[r], 16 * (MTILES // 4) + ONE)
            pool.wait_ge(s_o_done, MTILES + LEAD)
            def add_biases(g):
                pool.wait_ge(s_n_ready, GT * g + GT)
                xs = x_all[:, GT * g:GT * g + GT, :]
                pool.tensor_tensor(xs, xs, row(bo_bc), ALU.add).then_inc(s_bias_ready, 1)

            for g in range(GROUPS):
                for t in range(GT * g, GT * g + GT):
                    for k, dst in enumerate((y1_all, y2_all)):
                        pool.indirect_dma_start(out=dst[:, t, :], out_offset=None, in_=slots_out.ap(),
                                                in_offset=bass.IndirectOffsetOnAxis(ap=pos[:, k, t:t + 1], axis=0)).then_inc(s_group_in[g], 16)
                if g:
                    pool.wait_ge(s_group_in[g - 1], 16 * TOPK * GT)
                    pool.sem_inc(s_gathered, 1)
                if g >= 2:
                    add_biases(g - 2)
            pool.wait_ge(s_group_in[GROUPS - 1], 16 * TOPK * GT)
            pool.sem_inc(s_gathered, 1)
            for g in range(GROUPS - 2, GROUPS):
                add_biases(g)

        @block.tensor
        def _(pe):
            mm = nc.tensor.matmul
            pe.wait_ge(s_a_in, 16 * (2 * CH8 + 1))
            pe.wait_ge(s_first_columns, 2)
            def level(lv):
                k = 2 ** (lv % 4)
                vec, mat = (AiC, Mt) if lv < 4 else (AjB, M)
                if lv:
                    pe.wait_ge(s_p_copied, lv)
                pw = bank[4 + lv % 2][:, 0:BLK * 8].rearrange("p (g k) -> p g k", g=BLK)
                for q in range(4):
                    n = 4 * lv + q
                    if n >= 4:
                        pe.wait_ge(s_m_copied, n - 3)
                    for g in range(4 * q, 4 * q + 4):
                        last = mm(pw[:, g, 0:k], mat[:, g, :], vec[:, g, 0:k], start=True, stop=True)
                    if q == 3:
                        last.then_inc(s_pr_done, 1)
                    if lv == 7:
                        continue
                    if n >= 2:
                        pe.wait_ge(s_m_copied, n - 1)
                    for g in range(4 * q, 4 * q + 4):
                        c = slice(P * (g % 4), P * (g % 4) + P)
                        mm(bank[2 * (q % 2)][:, c], Mt[:, g, :], M[:, g, :], start=True, stop=True)
                        sq = mm(bank[2 * (q % 2) + 1][:, c], M[:, g, :], Mt[:, g, :], start=True, stop=True)
                    sq.then_inc(s_sq_done, 1)

            for lv in range(4):
                level(lv)

            pe.wait_ge(s_wg_in, 32)
            pe.wait_ge(s_masks, 1)
            pe.wait_ge(s_m_copied, 16)
            with pe.Fori(0, GROUPS) as g:
                for q in range(GT):
                    pe.wait_ge(s_xn_ready, GT * g + q + 1)
                    last = nc.tensor.transpose(bank[0][:, P * q:P * q + P], xn[:, q, :], ident[:, :])
                last.then_inc(s_tr_done, 1)
                pe.wait_ge(s_xnT_ready, g + 1)
                pe.wait_ge(s_sig_ready, 2 * g + ONE)
                for q in range(GT):
                    gp = bank[1 + q // 2][:, (D + E) * (q % 2):(D + E) * (q % 2 + 1)]
                    mm(gp, xnT[:, P * q:P * q + P], wg_sb[:, :], start=True, stop=False)
                    last = mm(gp, ones[:, :], bg_sb[:, :], start=False, stop=True)
                    if q % 2:
                        last.then_inc(s_gate_done, 1)
            pe.wait_ge(s_sig_ready, 2 * GROUPS + ONE)

            level(4)
            level(5)
            pe.wait_ge(s_mask_ready, 1)
            mflat = mask[:, :, :].rearrange("p t e -> p (t e)")
            mm(bank[7][:, 0:TILES * E], causal[:, :], mflat, start=True, stop=True)
            mm(bank[7][:, TILES * E:2 * TILES * E], ones_sq[:, :], mflat, start=True, stop=True).then_inc(s_counted, 1)
            level(6)
            level(7)
            pe.wait_ge(s_p_copied, 8)
            pe.wait_ge(s_rbd_ready, 1)
            hp = bank[6][:, 0:BLK * N].rearrange("p (g i) -> p g i", g=BLK)
            for g in range(BLK):
                last = mm(hp[:, g, :], Rbd[:, g, :, :].rearrange("p d j -> p (d j)"), AiC[:, g, :], start=True, stop=True)
            last.then_inc(s_h_done, 1)

            pe.wait_ge(s_m_copied, 28)
            with pe.Fori(0, GROUPS // 2) as h:
                for j in range(2):
                    pe.wait_ge(s_xg_ready, 2 * h + j + 1)
                    pe.wait_ge(s_rev_ready, 2 * h + ONE)
                    mm(bank[2 + j][:, :], flip[:, :], xg_all[:, bass.ds(GT * 2 * h + GT * j, GT), :].rearrange("p q d -> p (q d)"),
                       start=True, stop=True).then_inc(s_rev_done, 1)

            pe.wait_ge(s_rev_ready, GROUPS + ONE)
            with pe.Fori(0, GROUPS // 2) as h:
                for b in range(2):
                    yp = bank[4 + b][:, :].rearrange("p (t d) -> p t d", d=CHD)
                    pe.wait_ge(s_toep_in[b], 16 * h + 16)
                    pe.wait_ge(s_y_ready, 2 * h + ONE)
                    for d in range(CHD):
                        ch = bass.ds(2 * CHD * h + (CHD * b + d), 1)
                        mm(yp[:, :, d], toep[b][:, d, 0:P], xg_all[:, :, ch].rearrange("p t a -> p (t a)"),
                           start=True, stop=False, skip_group_check=True)
                        last = mm(yp[:, 1::2, d], toep[b][:, d, P:SEQ], xg_all[:, 0::2, ch].rearrange("p t a -> p (t a)"),
                                  start=False, stop=True, skip_group_check=True)
                    last.then_inc(s_ssm_done, 1)

            def turn(j, k, r):
                pe.wait_ge(s_xt_in[r], 16 * k + 16)
                for q in range(MQ):
                    last = nc.tensor.transpose(bank[6 + r % 2][:, P * q:P * q + P], xt[:, r, q, :], ident[:, :])
                last.then_inc(s_xT_tr, 1)

            def first(j, p):
                pe.wait_ge(s_xT_ready, j + 1)
                pe.wait_ge(s_w1s_ready, j + 1)
                for c in range(FC):
                    last = mm(bank[2 * p + c // 2][:, MW * (c % 2):MW * (c % 2) + MW], w1s[:, p, P * c:P * c + P], xT[:, p, :],
                              start=True, stop=True)
                    if c % 2:
                        last.then_inc(s_hid_done, 1)

            def second(j, p):
                e = pe.value_load(eid[0:1, bass.ds(j, 1)], min_val=0, max_val=E - 1)
                pe.wait_ge(s_hid_ready, j + 1)
                pe.wait_ge(s_res_ready, j - 1 + LEAD)
                for q in range(MQ):
                    for c in range(FC):
                        last = mm(bank[4 + p][:, P * q:P * q + P], hT[:, p, c, P * q:P * q + P],
                                  w2_sb[:, bass.ds(e, 1), c, :].rearrange("p a d -> p (a d)"), start=(c == 0), stop=(c == FC - 1))
                last.then_inc(s_o_done, 1)

            pe.wait_ge(s_w_in, 16 * 12)
            pe.wait_ge(s_y_ready, GROUPS + ONE)
            pe.wait_ge(s_h_ready, 1)
            pe.wait_ge(s_pos_ready, 1)
            turn(0, 0, 0)
            turn(1, 0, 1)
            first(0, 0)
            with pe.Fori(0, MTILES // 4 - 1) as i:
                for r in range(4):
                    pe.wait_ge(s_xT_ready, 4 * i + r + 1)
                    turn(4 * i + r + 2, i + (r + 2) // 4, (r + 2) % 4)
                    first(4 * i + r + 1, (r + 1) % 2)
                    second(4 * i + r, r % 2)
            for j in range(MTILES - 4, MTILES):
                if j + 2 < MTILES:
                    pe.wait_ge(s_xT_ready, j + 1)
                    turn(j + 2, (j + 2) // 4, (j + 2) % 4)
                if j + 1 < MTILES:
                    first(j + 1, (j + 1) % 2)
                second(j, j % 2)

            pe.wait_ge(s_l1_in, 160)
            pe.wait_ge(s_small_masks, 1)
            pe.wait_ge(s_res_ready, MTILES + LEAD)

            def scores(g, p, q):
                cols = slice(P * q, P * q + P)
                for r in range(R4):
                    rows = slice(32 * r, 32 * r + 32)
                    if q:
                        pe.wait_ge(s_am_ready, GT * R4 * g + R4 * (q - 1) + r + 1)
                    else:
                        pe.wait_ge(s_hf_ready, FC * g + r + 1)
                    mm(bank[r][:, :].rearrange("p (k t) -> p k t", k=R4), KT[p][rows, cols], QTm[p][rows, :, cols],
                       start=True, stop=True).then_inc(s_sc_done, 1)

            def values(g, p, q):
                cols = slice(P * q, P * q + P)
                av = bank[5][:, cols]
                if q % 2:
                    mm(av, S[p][:, q // 2, :], QT[p][:, cols], start=True, stop=False, skip_group_check=True)
                for r in range(R4):
                    rows = slice(32 * r, 32 * r + 32)
                    pe.wait_ge(s_am_ready, GT * R4 * g + R4 * q + r + 1)
                    for k in range(R4):
                        last = mm(av[rows, :], Vm[p][:, q, r, k, :, :].rearrange("p l e -> p (l e)"), Am[q % 2][:, r, k, :],
                                  start=(k == 0 and q % 2 == 0), stop=(k == R4 - 1), skip_group_check=True,
                                  tile_position=(0, 32 * r))
                last.then_inc(s_av_done, 1)

            def tokens(n, j):
                for q in (2 * j, 2 * j + 1):
                    last = mm(bank[7 - j][:, 2 * P * (q % 2):2 * P * (q % 2) + 2 * P], xnT[:, P * q:P * q + P],
                              wkv[:, :, :].rearrange("p a d -> p (a d)"), start=True, stop=True)
                last.then_inc(s_tok_done, 1)

            def step(g, n, p):
                back, front = g is not None, n is not None
                if back:
                    pe.wait_ge(s_kt_ready, g + 1)
                    pe.wait_ge(s_qtm_ready, R4 * g + R4)
                    scores(g, p, 0)
                    pe.wait_ge(s_den_ready, g + 1)
                    pe.wait_ge(s_hf_ready, FC * g + FC)
                    for c in range(FC):
                        last = mm(bank[7][RANK * c:RANK * c + RANK, :], u2_sb[:, c, :], Hf[:, c, :], start=True, stop=True,
                                  tile_position=(0, RANK * c))
                    last.then_inc(s_qf_done, 1)
                    scores(g, p, 1)
                    pe.wait_ge(s_qf_ready, g + 1)
                if front:
                    for q in range(GT):
                        pe.wait_ge(s_n_ready, GT * n + q + 1)
                        last = nc.tensor.transpose(bank[7][:, P * q:P * q + P], xn[:, q, :], ident[:, :])
                    last.then_inc(s_n_tr, 1)
                if back:
                    pe.wait_ge(s_vm_ready, g + 1)
                    pe.wait_ge(s_attn_ready, g + ONE)
                    pe.wait_ge(s_s_ready, g + 1)
                    values(g, p, 0)
                if front:
                    pe.wait_ge(s_n_T, n + 1)
                    mm(bank[6][:, :], wqk[:, 0, :], xnT[:, :], start=True, stop=True).then_inc(s_q_done, 1)
                if back:
                    scores(g, p, 2)
                if front:
                    mm(bank[7][:, :], wqk[:, 1, :], xnT[:, :], start=True, stop=True).then_inc(s_k_done, 1)
                if back:
                    values(g, p, 1)
                if front:
                    pe.wait_ge(s_ekv_ready, 2 * n + 1)
                    mm(bank[6][:, :], u1_sb[:, :], xnT[:, :], start=True, stop=True).then_inc(s_u_done, 1)
                if back:
                    scores(g, p, 3)
                if front:
                    pe.wait_ge(s_ekv_ready, 2 * n + 2)
                    tokens(n, 0)
                if back:
                    values(g, p, 2)
                if front:
                    pe.wait_ge(s_pt_ready, n + 1)
                    tokens(n, 1)
                    pe.wait_ge(s_v_ready, 2 * n + 1)
                    pe.wait_ge(s_qk_ready, 2 * n + 2)
                    mm(bank[7][:, :], head_sum[:, :], KT[1 - p], start=True, stop=True).then_inc(s_kc_done, 1)
                if back:
                    values(g, p, 3)
                if front:
                    for c in range(FC):
                        rows = slice(RANK * c, RANK * c + RANK)
                        mm(bank[c][:, :], v1_sb[rows, :], PT[rows, :], start=True, stop=True).then_inc(s_hf_done, 1)
                    pe.wait_ge(s_v_ready, 2 * n + 2)
                    pe.wait_ge(s_kt_ready, n + 1)
                    for b in range(2):
                        cols = slice(2 * P * b, 2 * P * b + P)
                        last = mm(bank[6][:, P * b:P * b + P], Ktok[:, cols], Vtok[:, cols], start=True, stop=True)
                    last.then_inc(s_st_done, 1)
                if back:
                    pe.wait_ge(s_attn_ready, g + 1 + ONE)
                    pe.wait_ge(s_out_ready, g + ONE)
                    for q in range(GT):
                        cols = slice(P * q, P * q + P)
                        mm(bank[4][:, cols], attnT[:, cols], wo_sb[:, :], start=True, stop=False)
                        last = mm(bank[4][:, cols], QfT[:, cols], v2_sb[:, :], start=False, stop=True)
                    last.then_inc(s_y_done, 1)
                if front:
                    pe.wait_ge(s_prod_ready, n + 1)
                    mm(bank[7][:, :], same_head[:, :], prod, start=True, stop=True).then_inc(s_den_done, 1)

            step(None, 0, 1)
            with pe.Fori(0, GROUPS // 2 - 1) as i:
                step(2 * i, 2 * i + 1, 0)
                step(2 * i + 1, 2 * i + 2, 1)
            step(GROUPS - 2, GROUPS - 1, 0)
            step(GROUPS - 1, None, 1)

        @block.scalar
        def _(act):
            copy = nc.scalar.copy

            def level(lv):
                k = 2 ** (lv % 4)
                vec = AiC if lv < 4 else AjB
                if lv < 7:
                    for q in range(4):
                        act.wait_ge(s_sq_done, 4 * lv + q + 1)
                        b = bank[2 * (q % 2):2 * (q % 2) + 2]
                        if q == 3:
                            pw = bank[4 + lv % 2][:, 0:BLK * 8].rearrange("p (g k) -> p g k", g=BLK)
                            copy(vec[:, :, k:2 * k], pw[:, :, 0:k]).then_inc(s_p_copied, 1)
                        copy(M[:, 4 * q:4 * q + 4, :], b[0][:, :].rearrange("p (g c) -> p g c", g=4))
                        copy(Mt[:, 4 * q:4 * q + 4, :], b[1][:, :].rearrange("p (g c) -> p g c", g=4)).then_inc(s_m_copied, 1)
                else:
                    act.wait_ge(s_pr_done, 8)
                    pw = bank[4 + lv % 2][:, 0:BLK * 8].rearrange("p (g k) -> p g k", g=BLK)
                    copy(vec[:, :, k:2 * k], pw[:, :, 0:k]).then_inc(s_p_copied, 1)

            for lv in range(4):
                level(lv)
            with act.Fori(0, GROUPS) as g:
                act.wait_ge(s_tr_done, g + 1 + ONE)
                copy(xnT[:, :], bank[0][:, :]).then_inc(s_xnT_ready, 1)
                for j in range(2):
                    act.wait_ge(s_gate_done, 2 * g + j + 1)
                    gp = bank[1 + j][:, 0:2 * (D + E)].rearrange("p (q c) -> p q c", q=2)
                    copy(logits[:, bass.ds(GT * g + 2 * j, 2), :], gp[:, :, D:D + E])
                    nc.scalar.activation(xg_all[:, bass.ds(GT * g + 2 * j, 2), :], gp[:, :, 0:D], ACT.Sigmoid).then_inc(s_sig_ready, 1)
            for lv in range(4, 8):
                level(lv)
            with act.Fori(0, GROUPS // 2) as h:
                for j in range(2):
                    act.wait_ge(s_rev_done, 2 * h + j + 1)
                    copy(xg_all[:, bass.ds(GT * 2 * h + GT * j, GT), :].rearrange("p q d -> p (q d)"), bank[2 + j][:, :]).then_inc(s_rev_ready, 1)
            act.wait_ge(s_gap_ready, 1)
            nc.scalar.activation(gw[:, 1, :], gw[:, 0, :], ACT.Exp).then_inc(s_gap_exp, 1)
            with act.Fori(0, GROUPS // 2) as h:
                for b in range(2):
                    act.wait_ge(s_ssm_done, 2 * h + b + 1)
                    copy(y_all[:, :, bass.ds(2 * CHD * h + CHD * b, CHD)], bank[4 + b][:, :].rearrange("p (t d) -> p t d", d=CHD)).then_inc(s_y_ready, 1)

            def turned(j, p):
                act.wait_ge(s_xT_tr, j + 1)
                copy(xT[:, p, :], bank[6 + p][:, 0:MW]).then_inc(s_xT_ready, 1)

            def weights(j, p):
                e = act.value_load(eid[0:1, bass.ds(j, 1)], min_val=0, max_val=E - 1)
                copy(w1s[:, p, :], w1_sb[:, bass.ds(e, 1), :].rearrange("p a f -> p (a f)")).then_inc(s_w1s_ready, 1)

            def hidden(j, p):
                e = act.value_load(eid[0:1, bass.ds(j, 1)], min_val=0, max_val=E - 1)
                act.wait_ge(s_o_done, j - 1 + LEAD)
                for c in range(FC):
                    if c % 2 == 0:
                        act.wait_ge(s_hid_done, 2 * j + c // 2 + 1)
                        act.sem_inc(s_act_pace, 1)
                    last = nc.scalar.activation(hT[:, p, c, :], bank[2 * p + c // 2][:, MW * (c % 2):MW * (c % 2) + MW], ACT.Gelu,
                                                bias=b1_sb[:, bass.ds(e, 1), c])
                last.then_inc(s_hid_ready, 1)

            act.wait_ge(s_w_in, 16 * 12)
            act.wait_ge(s_pos_ready, 1)
            for j in range(2):
                turned(j, j)
                weights(j, j)
            hidden(0, 0)
            with act.Fori(0, MTILES // 2 - 1) as i:
                for p in range(2):
                    turned(2 * i + p + 2, p)
                    weights(2 * i + p + 2, p)
                    hidden(2 * i + p + 1, 1 - p)
            hidden(MTILES - 1, 1)

            def step(g, n, p):
                if g is not None:
                    act.wait_ge(s_qf_done, g + 1)
                    copy(QfT, bank[7][:, :]).then_inc(s_qf_ready, 1)
                if n is None:
                    return
                act.wait_ge(s_n_tr, n + 1)
                copy(xnT[:, :], bank[7][:, :]).then_inc(s_n_T, 1)
                act.wait_ge(s_q_done, n + 1)
                nc.scalar.activation(QT[1 - p], bank[6][:, :], ACT.Exp)
                nc.scalar.activation(Rq, bank[6][:, :], ACT.Relu).then_inc(s_ekv_ready, 1)
                act.wait_ge(s_k_done, n + 1)
                nc.scalar.activation(KT[1 - p], bank[7][:, :], ACT.Exp)
                nc.scalar.activation(Rk, bank[7][:, :], ACT.Relu).then_inc(s_ekv_ready, 1)
                act.wait_ge(s_u_done, n + 1)
                copy(PT, bank[6][:, :]).then_inc(s_pt_ready, 1)
                act.wait_ge(s_qk_ready, 2 * n + 1)
                for k in range(R4):
                    nc.scalar.activation(QTm[1 - p][:, k, :], QT[1 - p], ACT.Copy, scale=head_pick[:, k:k + 1]).then_inc(s_qtm_ready, 1)
                for j in range(2):
                    act.wait_ge(s_tok_done, 2 * n + j + 1)
                    kv = bank[7 - j][:, :].rearrange("p (q a d) -> p q a d", q=2, a=2)
                    half = slice(2 * P * j, 2 * P * j + 2 * P)
                    nc.scalar.activation(Ktok[:, half].rearrange("p (q d) -> p q d", q=2), kv[:, :, 0, :], ACT.Exp)
                    nc.scalar.activation(Rkt[:, half].rearrange("p (q d) -> p q d", q=2), kv[:, :, 0, :], ACT.Relu)
                    copy(Vtok[:, half].rearrange("p (q d) -> p q d", q=2), kv[:, :, 1, :]).then_inc(s_v_ready, 1)
                for c in range(FC):
                    act.wait_ge(s_hf_done, FC * n + c + 1)
                    nc.scalar.activation(Hf[:, c, :], bank[c][:, :], ACT.Gelu_apprx_tanh, bias=fb1_sb[:, c:c + 1]).then_inc(s_hf_ready, 1)
                act.wait_ge(s_den_done, n + 1)
                nc.scalar.activation(zr, bank[7][:, :], ACT.Identity, bias=eps_sb[:, 0:1]).then_inc(s_den_ready, 1)

            step(None, 0, 1)
            with act.Fori(0, GROUPS // 2 - 1) as i:
                step(2 * i, 2 * i + 1, 0)
                step(2 * i + 1, 2 * i + 2, 1)
            step(GROUPS - 2, GROUPS - 1, 0)
            step(GROUPS - 1, None, 1)

        @block.vector
        def _(dve):
            v = nc.vector
            chain = Count(dve, s_dve_chain)

            def inverse_root(out, var, eps):
                w = var.shape[1]
                a, b = ve[:, 0:w], sq[:, 0:w]
                chain.mark(v.tensor_scalar(a, var, eps, None, ALU.add))
                chain.wait()
                chain.mark(v.tensor_scalar(out.bitcast(I32), a.bitcast(I32), 1, None, ALU.logical_shift_right))
                chain.wait()
                chain.mark(v.tensor_scalar(out.bitcast(I32), out.bitcast(I32), -1.0, float(0x5F3759DF), ALU.mult, ALU.add))
                chain.wait()
                for _ in range(NEWTON):
                    chain.mark(v.tensor_tensor(b, out, out, ALU.mult))
                    chain.wait()
                    chain.mark(v.scalar_tensor_tensor(out=b, in0=b, scalar=-0.5, in1=a, op0=ALU.mult, op1=ALU.mult))
                    chain.wait()
                    chain.mark(v.scalar_tensor_tensor(out=out, in0=b, scalar=1.5, in1=out, op0=ALU.add, op1=ALU.mult))
                    chain.wait()

            def layer_norm(src, n, mean_var, root, eps):
                dve.sem_inc(s_dve_pace, 1)
                for q in range(n):
                    last = v.bn_stats(stats[:, q, :], src(q))
                chain.mark(last)
                chain.wait()
                dve.sem_inc(s_dve_pace, 1)
                for q in range(n):
                    last = v.bn_aggr(mean_var[:, q, :], stats[:, q, :])
                chain.mark(last)
                chain.wait()
                inverse_root(root, mean_var[:, 0:n, 1], eps)

            dve.wait_ge(s_masks, 1)
            v.tensor_reduce(head_pick[:, :], same_head[:, :].rearrange("p (r k e) -> p k r e", r=R4, k=R4)[:, :, :, 0], AXX, ALU.add)
            v.tensor_reduce(first_lag[:, :], ident[:, :].rearrange("p (i j) -> p i j", j=N)[:, :, 0], AXX, ALU.add)
            chain.mark(v.tensor_reduce(place8[:, :], ident[:, :].rearrange("p (h e) -> p e h", h=H), AXX, ALU.add))
            chain.wait()
            hs = head_sum[:, :].rearrange("p (h e) -> p h e", h=H)
            v.tensor_tensor(hs, hs, place8[:, :].rearrange("p (a e) -> p a e", a=1).broadcast_to([P, H, DH]), ALU.mult).then_inc(s_small_masks, 1)

            dve.wait_ge(s_x_in, 64)
            layer_norm(lambda q: x_all[:, q, :], TILES, mv, rstd[:, :], 1e-5)
            with dve.Fori(0, GROUPS) as g:
                dve.wait_ge(s_tr_done, g + ONE)
                dve.wait_ge(s_xn_saved, g + ONE)
                for q in range(GT):
                    t = bass.ds(GT * g + q, 1)
                    v.tensor_scalar(xn[:, q, :], x_all[:, t, :].rearrange("p a d -> p (a d)"), mv[:, t, 0], rstd[:, t],
                                    ALU.subtract, ALU.mult).then_inc(s_xn_ready, 1)
            with dve.Fori(0, GROUPS) as g:
                dve.wait_ge(s_xn_saved, g + 1 + ONE)
                dve.wait_ge(s_sig_ready, 2 * g + 2 + ONE)
                xs = xg_all[:, bass.ds(GT * g, GT), :]
                v.tensor_tensor(xs, xs, xn_all[:, bass.ds(GT * g, GT), :], ALU.mult).then_inc(s_xg_ready, 1)

            full = [P, TILES, E]
            bc = lambda t: t[:, :].rearrange("p (t a) -> p t a", a=1).broadcast_to(full)
            rk = rank8[:, :].rearrange("p (a e) -> p a e", a=1).broadcast_to(full)

            def best(lg, mx, onehot):
                chain.mark(v.tensor_reduce(mx[:, :], lg, AXX, ALU.max))
                chain.wait()
                chain.mark(v.tensor_tensor(onehot, lg, bc(mx), ALU.is_ge))
                chain.wait()
                chain.mark(v.tensor_tensor(onehot, onehot, rk, ALU.mult))
                chain.wait()
                chain.mark(v.tensor_reduce(m3[:, :], onehot, AXX, ALU.max))
                chain.wait()
                chain.mark(v.tensor_tensor(onehot, rk, bc(m3), ALU.is_equal))
                chain.wait()

            dve.wait_ge(s_sig_ready, 2 * GROUPS + ONE)
            best(logits[:, :, :], m1, hot1[:, :, :])
            chain.mark(v.scalar_tensor_tensor(out=t2[:, :, :], in0=hot1[:, :, :], scalar=-3.0e38, in1=logits[:, :, :], op0=ALU.mult, op1=ALU.add))
            chain.wait()
            best(t2[:, :, :], m2, hot2[:, :, :])
            v.tensor_tensor(mask[:, :, :], hot1[:, :, :], hot2[:, :, :], ALU.add).then_inc(s_mask_ready, 1)
            v.tensor_tensor(gw[:, 0, :], m2[:, :], m1[:, :], ALU.subtract).then_inc(s_gap_ready, 1)

            dve.wait_ge(s_counted, 1)
            total = bank[7][:, TILES * E:2 * TILES * E].rearrange("p (t e) -> p t e", e=E)
            within = bank[7][:, 0:TILES * E].rearrange("p (t e) -> p t e", e=E)

            def running_sum(a, b, n):
                step = 1
                while step < n:
                    v.tensor_copy(b[:, 0:step], a[:, 0:step])
                    chain.mark(v.tensor_tensor(b[:, step:n], a[:, step:n], a[:, 0:n - step], ALU.add))
                    chain.wait()
                    a, b, step = b, a, 2 * step
                return a

            chain.mark(v.tensor_copy(cum[:, :, :], total))
            chain.wait()
            upto = running_sum(cum, t2, TILES)
            chain.mark(v.tensor_scalar(counts[:, 0, :].bitcast(I32), upto[:, TILES - 1, :], float(MW - 1), None, ALU.add))
            chain.wait()
            chain.mark(v.tensor_scalar(counts[:, 1, :].bitcast(I32), counts[:, 0, :].bitcast(I32), -MW, None, ALU.bitwise_and))
            chain.wait()
            v.tensor_copy(counts[:, 2, :], counts[:, 1, :].bitcast(I32))
            chain.mark(v.tensor_copy(ends[:, 0, :], counts[:, 1, :].bitcast(I32)))
            chain.wait()
            end = running_sum(ends[:, 0, :], ends[:, 1, :], E)
            chain.mark(v.tensor_tensor(counts[:, 3, :], end, counts[:, 2, :], ALU.subtract))
            chain.mark(v.tensor_tensor(off[:, :, :], upto[:, :, :], total, ALU.subtract))
            chain.wait()
            chain.mark(v.tensor_tensor(off[:, :, :], off[:, :, :], counts[:, 3:4, :].broadcast_to(full), ALU.add))
            chain.wait()
            chain.mark(v.scalar_tensor_tensor(out=off[:, :, :], in0=within, scalar=-1.0, in1=off[:, :, :], op0=ALU.add, op1=ALU.add))
            chain.wait()
            for k, hot in enumerate((hot1, hot2)):
                chain.mark(v.tensor_tensor(hot[:, :, :], hot[:, :, :], off[:, :, :], ALU.mult))
                chain.wait()
                chain.mark(v.tensor_reduce(posf[:, :], hot[:, :, :], AXX, ALU.add))
                chain.wait()
                chain.mark(v.tensor_copy(pos[:, k, :], posf[:, :]))
                chain.wait()
            v.memset(eidf[:, :], 0.0)
            chain.mark(v.memset(m3[:, :], 0.0))
            chain.wait()
            for e in range(E - 1):
                chain.mark(v.scalar_tensor_tensor(out=eidf[:, :], in0=starts[:, :], scalar=end[:, e:e + 1], in1=eidf[:, :], op0=ALU.is_ge, op1=ALU.add))
                chain.wait()
            v.tensor_copy(eid[:, :], eidf[:, :]).then_inc(s_pos_ready, 1)

            dve.wait_ge(s_p_copied, 8)
            for g in range(BLK):
                last = v.tensor_tensor(Rbd[:, g, :, :], AjB[:, g:g + 1, :].broadcast_to([P, CH8, N]),
                                       mask8[:, :].rearrange("p (d a) -> p d a", a=1).broadcast_to([P, CH8, N]), ALU.mult)
            last.then_inc(s_rbd_ready, 1)
            chain.mark(v.tensor_scalar(dp1[:, :], dp_sb[:, :], 1.0, first_lag[:, 0:1], ALU.add, ALU.mult))
            chain.wait()
            dve.wait_ge(s_h_done, 1)
            hp = bank[6][:, 0:BLK * N].rearrange("p (g i) -> p g i", g=BLK)
            v.tensor_copy(h_sb[:, :, 1:N], hp[:, :, 1:N])
            v.tensor_tensor(h_sb[:, :, 0], hp[:, :, 0], dp1[:, :], ALU.add).then_inc(s_h_ready, 1)

            dve.wait_ge(s_gap_exp, 1)
            chain.mark(v.tensor_scalar(m3[:, :], gw[:, 1, :], 1.0, None, ALU.add))
            chain.wait()
            chain.mark(v.reciprocal(gw[:, 0, :], m3[:, :]))
            chain.wait()
            chain.mark(v.tensor_tensor(gw[:, 1, :], gw[:, 1, :], gw[:, 0, :], ALU.mult))

            dve.wait_ge(s_y_ready, GROUPS + ONE)
            dve.wait_ge(s_const_in, 64)
            layer_norm(lambda q: y_all[:, q, :], TILES, mv, rstd[:, :], 1e-5)
            chain.mark(v.memset(Vm[0], 0.0))
            row = lambda t: t[:, :].rearrange("p (a d) -> p a d", a=1).broadcast_to([P, GT, D])
            one = lambda t, g, q: t[:, bass.ds(GT * g + q, 1), :].rearrange("p a d -> p (a d)")

            def recurrence(g):
                xs = x_all[:, bass.ds(GT * g, GT), :]
                ys = y_all[:, bass.ds(GT * g, GT), :]
                for q in range(GT):
                    t = bass.ds(GT * g + q, 1)
                    last = v.tensor_scalar(one(y_all, g, q), one(y_all, g, q), mv[:, t, 0], rstd[:, t], ALU.subtract, ALU.mult)
                chain.mark(last)
                chain.wait()
                chain.mark(v.tensor_tensor(ys, ys, row(gam_bc), ALU.mult))
                chain.wait()
                chain.mark(v.tensor_tensor(xs, xs, ys, ALU.add))

            def experts(i):
                for b in range(2):
                    for p in range(2):
                        j = 4 * i + 2 * b + p
                        dve.wait_ge(s_o_done, j + 1 + LEAD)
                        dve.wait_ge(s_xb_ready, j + 1)
                        dve.wait_ge(s_e_ready, j - 1 + LEAD)
                        v.tensor_tensor(res[:, p, :, :], bank[4 + p][:, 0:MW].rearrange("p (q d) -> p q d", q=MQ), xb[:, 2 * b + p, :, :],
                                        ALU.add).then_inc(s_res_ready, 1)
                    dve.wait_ge(s_res_ready, 4 * i + 2 * b + 2 + LEAD)
                    layer_norm(lambda q: res[:, q // MQ, q % MQ, :], 2 * MQ, mv4, rstd4[:, :], 1e-6)
                    for p in range(2):
                        r = 2 * b + p
                        dve.wait_ge(s_st_out[r], 16 * i + ONE)
                        for q in range(MQ):
                            last = v.tensor_scalar(eo[:, r, q, :], res[:, p, q, :], mv4[:, MQ * p + q, 0:1],
                                                   rstd4[:, MQ * p + q:MQ * p + q + 1], ALU.subtract, ALU.mult)
                        last.then_inc(s_e_ready, 1)

            dve.wait_ge(s_bet_added, GROUPS)
            start = chain.base + chain.n
            with dve.Fori(0, GROUPS) as i:
                chain.base, chain.n = i * (2 * NORM + 3) + start, 0
                experts(i)
                recurrence(i)
            start += GROUPS * (2 * NORM + 3)
            for i in range(GROUPS, MTILES // 4):
                chain.base, chain.n = start + (i - GROUPS) * 2 * NORM, 0
                experts(i)

            dve.wait_ge(s_st_ready, MTILES)
            chain.mark(v.memset(Vm[1], 0.0))
            chain.wait()

            def outputs(m, k):
                dve.wait_ge(s_gathered, m + 1)
                for q in range(GT):
                    last = v.scalar_tensor_tensor(out=one(x_all, m, q), in0=one((y1_all, y2_all)[k], m, q), scalar=gw[:, k, bass.ds(GT * m + q, 1)],
                                                  in1=one(x_all, m, q), op0=ALU.mult, op1=ALU.add)
                chain.mark(last)
                chain.wait()

            def normalise(m):
                for q in range(GT):
                    v.tensor_scalar(xn[:, q, :], one(x_all, m, q), mv4[:, q, 0:1], rstd4[:, q:q + 1], ALU.subtract, ALU.mult).then_inc(s_n_ready, 1)

            def masked(g, q):
                dve.wait_ge(s_av_done, GT * g + q - 1 + LEAD)
                for r in range(R4):
                    dve.wait_ge(s_sc_done, GT * R4 * g + R4 * q + r + 1)
                    v.tensor_tensor(Am[q % 2][:, r, :, :], bank[r][:, :].rearrange("p (k t) -> p k t", k=R4),
                                    causal[:, :].rearrange("p (a t) -> p a t", a=1).broadcast_to([P, R4, P]), ALU.mult).then_inc(s_am_ready, 1)

            def feature(n, i, to, re):
                dve.wait_ge(s_ekv_ready, 2 * n + i + 1)
                v.scalar_tensor_tensor(out=to, in0=to, scalar=1.0, in1=re, op0=ALU.min, op1=ALU.add).then_inc(s_qk_ready, 1)

            STEP = 2 + NORM

            def step(g, n, m, p, i=0):
                back, front, norm = g is not None, n is not None, m is not None
                if back:
                    dve.wait_ge(s_den_ready, g + 1)
                    masked(g, 0)
                if norm:
                    outputs(m, 0)
                if back:
                    masked(g, 1)
                if front:
                    feature(n, 0, QT[1 - p], Rq)
                if norm:
                    outputs(m, 1)
                if back:
                    masked(g, 2)
                if front:
                    feature(n, 1, KT[1 - p], Rk)
                if norm:
                    layer_norm(lambda q: one(x_all, m, q), GT, mv4, rstd4[:, :], 1e-5)
                if back:
                    masked(g, 3)
                    v.reciprocal(zr, zr).then_inc(s_zr_ready, 1)
                if front:
                    dve.wait_ge(s_v_ready, 2 * n + 2)
                    v.scalar_tensor_tensor(out=Ktok, in0=Ktok, scalar=1.0, in1=Rkt, op0=ALU.min, op1=ALU.add).then_inc(s_kt_ready, 1)
                    dve.wait_ge(s_kc_done, n + 1)
                    dve.wait_ge(s_qk_ready, 2 * n + 2)
                    v.tensor_tensor(prod, QT[1 - p], bank[7][:, :], ALU.mult).then_inc(s_prod_ready, 1)
                if back:
                    dve.wait_ge(s_zr_ready, g + 1)
                    dve.wait_ge(s_av_done, GT * g + GT + LEAD)
                    v.tensor_tensor(attnT, bank[5][:, :], zr, ALU.mult).then_inc(s_attn_ready, 1)
                if front:
                    for q in range(GT):
                        full_v = Vm[1 - p][:, q, :, :, :, :].rearrange("p r k l e -> p r (k l) e")
                        last = v.tensor_copy(full_v[:, :, 0:16:5, :], Vtok[:, P * q:P * q + P].rearrange("p (r k e) -> p r k e", r=R4, k=R4))
                    last.then_inc(s_vm_ready, 1)
                    dve.wait_ge(s_st_done, n + 1)
                    v.tensor_tensor(S[1 - p][:, :, :], bank[6][:, 0:2 * P].rearrange("p (b c) -> p b c", b=2),
                                    same_head[:, :].rearrange("p (a c) -> p a c", a=1).broadcast_to([P, 2, P]), ALU.mult).then_inc(s_s_ready, 1)
                if norm:
                    normalise(m)
                if back:
                    dve.wait_ge(s_y_done, g + 1)
                    dve.wait_ge(s_bias_ready, g + 2)
                    dve.wait_ge(s_out_stored[p], 16 * i + ONE)
                    v.tensor_tensor(yo[p].rearrange("p (q d) -> p q d", q=GT), bank[4][:, :].rearrange("p (q d) -> p q d", q=GT),
                                    x_all[:, bass.ds(GT * g, GT), :], ALU.add).then_inc(s_out_ready, 1)

            outputs(0, 0)
            outputs(0, 1)
            layer_norm(lambda q: one(x_all, 0, q), GT, mv4, rstd4[:, :], 1e-5)
            normalise(0)
            step(None, 0, 1, 1)
            start = chain.base + chain.n
            with dve.Fori(0, GROUPS // 2 - 1) as i:
                chain.base, chain.n = i * (2 * STEP) + start, 0
                step(2 * i, 2 * i + 1, 2 * i + 2, 0, i)
                step(2 * i + 1, 2 * i + 2, 2 * i + 3, 1, i)
            step(GROUPS - 2, GROUPS - 1, None, 0, GROUPS // 2 - 1)
            step(GROUPS - 1, None, None, 1, GROUPS // 2 - 1)


def kernel(**inputs):
    import numpy as np
    import concourse.bacc as bacc
    from concourse.bass_utils import run_bass_kernel_spmd

    a = {k: np.asarray(v) for k, v in inputs.items()}
    pairs = lambda t: t.reshape(BLK, CH8, N).transpose(1, 2, 0).reshape(P, BLK)
    laid = [
        ("x", a["L0_attn_x"].reshape(TILES * P, D)),
        ("A", a["L0_attn_A"]),
        ("At", a["L0_attn_A"].transpose(0, 2, 1)),
        ("BpT", pairs(a["L0_attn_Bp"])),
        ("CpT", pairs(a["L0_attn_Cp"])),
        ("DpR", np.repeat(a["L0_attn_Dp"].reshape(BLK, CH8).T, N, axis=0)),
        ("WgRw", np.concatenate([a["L0_attn_Wg"].T, a["L0_ffn_router_w"]], axis=1)),
        ("bg", a["L0_attn_bg"].reshape(1, D)),
        ("gamma", a["L0_attn_gamma"]),
        ("beta", a["L0_attn_beta"]),
        ("w1", a["L0_ffn_w1"]),
        ("b1T", a["L0_ffn_b1"].reshape(E, FC, P).transpose(2, 0, 1)),
        ("w2", a["L0_ffn_w2"]),
        ("b2", a["L0_ffn_b2"]),
        ("egamma", a["L0_ffn_gamma"]),
        ("ebeta", a["L0_ffn_beta"]),
        ("Wq", a["L1_attn_Wq"]),
        ("Wk", a["L1_attn_Wk"]),
        ("Wv", a["L1_attn_Wv"]),
        ("Wo", a["L1_attn_Wo"]),
        ("bo", a["L1_attn_bo"]),
        ("U1R", np.concatenate([a["L1_ffn_U1"]] * FC, axis=1)),
        ("V1", a["L1_ffn_V1"].reshape(RANK, FC, P).transpose(1, 0, 2).reshape(P, P)),
        ("fb1T", a["L1_ffn_b1"].reshape(FC, P).T),
        ("U2", a["L1_ffn_U2"]),
        ("V2R", np.concatenate([a["L1_ffn_V2"]] * FC, axis=0)),
        ("fb2", a["L1_ffn_b2"]),
    ]
    nc = bacc.Bacc("TRN2", target_bir_lowering=False, num_devices=1)
    arrays, args = {}, []
    for name, t in laid:
        t = np.ascontiguousarray(t)
        arrays[f"in_{name}"] = t
        args.append(nc.dram_tensor(f"in_{name}", t.shape, F32, kind="ExternalInput").ap())
    out = nc.dram_tensor("out_x", (TILES * P, D), F32, kind="ExternalOutput").ap()
    two_layer_kernel(nc, *args, out)
    r = run_bass_kernel_spmd(nc, [arrays], core_ids=[0])
    return r.results[0]["out_x"].reshape(BATCH, SEQ, D)
```

```python
from contextlib import ExitStack

import concourse.bass as bass
from concourse import mybir

F32 = mybir.dt.float32
I32 = mybir.dt.int32
ALU = mybir.AluOpType
ACT = mybir.ActivationFunctionType
AXX = mybir.AxisListType.X

P = 128
D = 128
BATCH, SEQ = 16, 256
TILES = BATCH * SEQ // P
GT = 4
GROUPS = TILES // GT
GW = GT * P
N = 16
CH8 = P // N
BLK = D // CH8
SQ3 = 3
SQ_STEPS = [range(b, min(b + SQ3, BLK)) for b in range(0, BLK, SQ3)]
LEVELS = 7
NI, NJ = 32, 8
NI_LEVELS = 5
SQ_W = P + NI // 2
HR = CH8 * NJ
E = 8
F = 512
FC = F // P
CHD = D // GROUPS
HPAD = SEQ + P
H, DH = 16, 8
R4 = 4
RANK = 32
TOPK = 2
MQ = 2
MW = MQ * P
MTILES = (TILES * P * TOPK + E * (MW - 1)) // MW
MTILES += -MTILES % 4
SLOTS = MTILES * MW
LEAD = 2
ONE = 1
NEWTON = 3
NORM = 2 + 3 + 3 * NEWTON


class Count:

    def __init__(self, eng, sem):
        self.eng, self.sem, self.base, self.n = eng, sem, 0, 0

    def mark(self, ins):
        self.n += 1
        ins.then_inc(self.sem, 1)

    def wait(self):
        self.eng.wait_ge(self.sem, self.base + self.n)


def two_layer_kernel(nc, x, A, At, BpT, CpT, DpR, WgRw, bg, gamma, beta, w1, b1T, w2, b2, egamma, ebeta,
                     Wq, Wk, Wv, Wo, bo, U1R, V1, fb1T, U2, V2R, fb2, out):
    with ExitStack() as ctx:
        def sb(name, shape):
            return ctx.enter_context(nc.sbuf_tensor(name, shape, F32))

        def sem(name):
            return ctx.enter_context(nc.semaphore(name))

        x_all = sb("x_all", [P, TILES, D])
        xn_all = sb("xn_all", [P, TILES, D])
        xg_all = sb("xg_all", [P, TILES, D])
        y_all = sb("y_all", [P, TILES, D])
        w1_sb = sb("w1_sb", [P, E, F])
        w2_sb = sb("w2_sb", [P, E, FC, D])
        b1_sb = sb("b1_sb", [P, E, FC])
        etab = sb("etab", [P, 3, E, D])
        eb2, egam, ebet = [etab[:, i, :, :] for i in range(3)]
        gam_bc = sb("gam_bc", [P, D])
        bet_bc = sb("bet_bc", [P, D])
        wg_sb = sb("wg_sb", [P, D + E])
        bg_bc = sb("bg_bc", [P, D])
        ident = sb("ident", [P, P])
        flip = sb("flip", [P, P])
        next_tile = sb("next_tile", [P, P])
        big = sb("big", [P, BLK * (2 * P + NI + NJ)])
        M = big[:, 0:BLK * (P + NI)].rearrange("p (g c) -> p g c", g=BLK)
        Mt = big[:, BLK * (P + NI):].rearrange("p (g c) -> p g c", g=BLK)
        AiC = M[:, :, P:]
        AjB = Mt[:, :, P:]
        toep2 = sb("toep2", [P, 2 * BLK * P])
        toep = [t[:, 0:CHD * SEQ].rearrange("p (d u) -> p d u", d=CHD) for t in (big, toep2)]
        bc_sb = sb("bc_sb", [P, 2, BLK])
        mask8 = sb("mask8", [P, CH8])
        first_lag = sb("first_lag", [HR, 1])
        dp_sb = sb("dp_sb", [HR, BLK])
        dp1 = sb("dp1", [HR, BLK])
        zero_sb = sb("zero_sb", [P, P])
        mid = sb("mid", [P, 4096])
        Rbd = mid[:, 0:BLK * HR].rearrange("p (g d j) -> p g d j", g=BLK, d=CH8)
        A_rows = mid[:, 2048:2048 + 2 * BLK * N].rearrange("p (s g m) -> p s g m", s=2, g=BLK)
        h_sb = mid[0:HR, 1024:1024 + BLK * NI].rearrange("p (g i) -> p g i", g=BLK)
        hT = mid[:, 0:2048].rearrange("p (s c t) -> p s c t", s=2, c=FC)
        w1s = mid[:, 2048:3072].rearrange("p (s f) -> p s f", s=2)
        xc = [sb(f"xc{b}", [P, CHD, TILES]) for b in range(2)]
        conv = [mid[:, 1024 * (b + 1):1024 * (b + 2)].rearrange("p (k t) -> p k t", k=CHD // 4) for b in range(2)]
        eo = mid[:, 3072:4096].rearrange("p (s q d) -> p s q d", s=4, q=MQ)
        res = sb("res", [P, 2, MQ, D])
        xt = sb("xt", [P, 4, MQ, D])
        xb = sb("xb", [P, 4, MQ, D])
        xT = sb("xT", [P, 2, MW])
        stats = sb("stats", [P, TILES, 6])
        mv = sb("mv", [P, TILES, 2])
        rstd = sb("rstd", [P, TILES])
        ve = sb("ve", [P, TILES])
        sq = sb("sq", [P, TILES])
        mv8 = sb("mv8", [P, 2 * GT, 2])
        rstd8 = sb("rstd8", [P, 2 * GT])
        xn = sb("xn", [P, 2, GT, D])
        xnT = sb("xnT", [P, 2, GW])
        logits = sb("logits", [P, TILES, E])
        hot1 = sb("hot1", [P, TILES, E])
        mask = sb("mask", [P, TILES, E])
        cum = sb("cum", [P, TILES, E])
        off = sb("off", [P, TILES, E])
        counts = sb("counts", [P, 4, E])
        ends = sb("ends", [P, 2, E])
        starts = sb("starts", [P, MTILES])
        eidf = sb("eidf", [P, MTILES])
        eid = ctx.enter_context(nc.sbuf_tensor("eid", [P, MTILES], I32))
        pos = ctx.enter_context(nc.sbuf_tensor("pos", [P, TOPK, TILES], I32))
        posf = sb("posf", [P, TILES])
        gw = sb("gw", [P, TOPK, TILES])
        ones_sq = sb("ones_sq", [P, P])
        hot2 = sb("hot2", [P, TILES, E])
        t2 = sb("t2", [P, TILES, E])
        rank8 = sb("rank8", [P, E])
        place8 = sb("place8", [P, DH])
        m1 = sb("m1", [P, TILES])
        m2 = sb("m2", [P, TILES])
        m3 = sb("m3", [P, TILES])
        eps_sb = sb("eps_sb", [P, 1])

        wqk = sb("wqk", [P, 2, D])
        wkv = sb("wkv", [P, 2, D])
        wo_sb = sb("wo_sb", [P, D])
        u1_sb = sb("u1_sb", [P, P])
        v1_sb = sb("v1_sb", [P, P])
        u2_sb = sb("u2_sb", [P, FC, RANK])
        v2_sb = sb("v2_sb", [P, D])
        fb1_sb = sb("fb1_sb", [P, FC])
        bo_bc = sb("bo_bc", [P, D])
        fb2_bc = sb("fb2_bc", [P, D])
        causal = sb("causal", [P, P])
        same_head = sb("same_head", [P, P])
        head_sum = sb("head_sum", [P, P])
        head_pick = sb("head_pick", [P, R4])
        Am = [t.rearrange("p (r k t) -> p r k t", r=R4, k=R4) for t in (mid[:, 0:2048], toep2[:, 0:2048])]
        Hf = mid[:, 2048:4096].rearrange("p (c t) -> p c t", c=FC)
        xg_flat = xg_all[:, :, :].rearrange("p a b -> p (a b)")
        etab_flat = etab[:, :, :, :].rearrange("p i e d -> p (i e d)")
        QTm = [t.rearrange("p (k t) -> p k t", k=R4) for t in (xg_flat[:, 0:2048], toep2[:, 2048:4096])]
        Vm = [t.rearrange("p (q r k l e) -> p q r k l e", q=GT, r=R4, k=R4, l=R4) for t in (xg_flat[:, 2048:4096], etab_flat[:, 0:2048])]
        l1 = big[:, 0:8 * GW].rearrange("p (s t) -> p s t", s=8)
        QT, KT, (Rq, Rk, zr, prod) = (l1[:, 0, :], l1[:, 1, :]), (l1[:, 2, :], l1[:, 3, :]), [l1[:, i, :] for i in range(4, 8)]
        l2 = xn_all[:, :, :].rearrange("p a b -> p (a b)").rearrange("p (s t) -> p s t", s=8)
        Ktok, Rkt, Vtok, PT, QfT, attnT = [l2[:, i, :] for i in range(6)]
        yo = (l2[:, 6, :], l2[:, 7, :])
        S = [sb(f"S{p}", [P, 2, P]) for p in range(2)]

        bank = [ctx.enter_context(nc.psum_tensor(f"bank{i}", [P, 512], F32)) for i in range(8)]
        y1_all = w1_sb[:, :, :].rearrange("p e f -> p (e f)").rearrange("p (t d) -> p t d", d=D)
        y2_all = w2_sb[:, :, :, :].rearrange("p e c d -> p (e c) d")
        slots_in = nc.dram_tensor("slots_in", [SLOTS, D], F32, kind="Internal")
        slots_out = nc.dram_tensor("slots_out", [SLOTS, D], F32, kind="Internal")
        h_dram = nc.dram_tensor("impulse_responses", [D, HPAD], F32, kind="Internal")

        s_a_in = sem("a_in")
        s_wg_in = sem("wg_in")
        s_const_in = sem("const_in")
        s_w_in = sem("w_in")
        s_l1_in = sem("l1_in")
        s_zeroed = sem("zeroed")
        s_masks = sem("masks")
        s_mask8_ready = sem("mask8_ready")
        s_blocks_ready = sem("blocks_ready")
        s_sq_done = sem("sq_done")
        s_m_copied = sem("m_copied")
        s_pr_done = sem("pr_done")
        s_columns_done = sem("columns_done")
        s_pre_ready = sem("pre_ready")
        s_xc_ready = sem("xc_ready")
        s_conv_ready = sem("conv_ready")
        s_back_done = sem("back_done")
        s_yn_ready = sem("yn_ready")
        s_rbd_ready = sem("rbd_ready")
        s_h_done = sem("h_done")
        s_h_ready = sem("h_ready")
        s_h_out = sem("h_out")
        s_toep_in0 = sem("toep_in0")
        s_toep_in1 = sem("toep_in1")
        s_xn_ready = sem("xn_ready")
        s_xn_saved = sem("xn_saved")
        s_tr_done = sem("tr_done")
        s_xnT_ready = sem("xnT_ready")
        s_gate_done = sem("gate_done")
        s_sig_ready = sem("sig_ready")
        s_xg_ready = sem("xg_ready")
        s_rev_done = sem("rev_done")
        s_rev_ready = sem("rev_ready")
        s_mask_ready = sem("mask_ready")
        s_counted = sem("counted")
        s_pos_ready = sem("pos_ready")
        s_eid_ready = sem("eid_ready")
        s_gap_ready = sem("gap_ready")
        s_gap_exp = sem("gap_exp")
        s_slots_zeroed = sem("slots_zeroed")
        s_scattered = sem("scattered")
        s_xT_tr = sem("xT_tr")
        s_xT_ready = sem("xT_ready")
        s_w1s_ready = sem("w1s_ready")
        s_xb_ready = sem("xb_ready")
        s_hid_done = sem("hid_done")
        s_hid_ready = sem("hid_ready")
        s_o_done = sem("o_done")
        s_res_ready = sem("res_ready")
        s_e_ready = sem("e_ready")
        s_e_scaled = sem("e_scaled")
        s_st_ready = sem("st_ready")
        s_ssm_done = sem("ssm_done")
        s_y_ready = sem("y_ready")
        s_gathered = sem("gathered")
        s_pool_chain = sem("pool_chain")
        s_dve_chain = sem("dve_chain")
        s_n_ready = sem("n_ready")
        s_n_tr = sem("n_tr")
        s_n_T = sem("n_T")
        s_q_done = sem("q_done")
        s_ekv_ready = sem("ekv_ready")
        s_qk_ready = sem("qk_ready")
        s_vm_ready = sem("vm_ready")
        s_qtm_ready = sem("qtm_ready")
        s_kt_ready = sem("kt_ready")
        s_kc_done = sem("kc_done")
        s_u_done = sem("u_done")
        s_k_done = sem("k_done")
        s_den_ready = sem("den_ready")
        s_zr_ready = sem("zr_ready")
        s_base_ready = sem("base_ready")
        s_prod_ready = sem("prod_ready")
        s_den_done = sem("den_done")
        s_st_done = sem("st_done")
        s_s_ready = sem("s_ready")
        s_sc_done = sem("sc_done")
        s_am_ready = sem("am_ready")
        s_av_done = sem("av_done")
        s_attn_ready = sem("attn_ready")
        s_pt_ready = sem("pt_ready")
        s_hf_done = sem("hf_done")
        s_hf_ready = sem("hf_ready")
        s_qf_done = sem("qf_done")
        s_qf_ready = sem("qf_ready")
        s_y_done = sem("y_done")
        s_out_ready = sem("out_ready")
        s_v_ready = sem("v_ready")
        s_tok_done = sem("tok_done")
        s_bias_ready = sem("bias_ready")
        s_small_masks = sem("small_masks")
        s_dve_pace = sem("dve_pace")
        s_pool_pace = sem("pool_pace")
        s_act_pace = sem("act_pace")
        s_bc_in = sem("bc_in")
        s_first_columns = sem("first_columns")
        s_group_in = [sem(f"group_in{g}") for g in range(GROUPS)]
        s_x_in = [sem(f"x_in{k}") for k in range(4)]
        s_toep_in = (s_toep_in0, s_toep_in1)
        s_xt_in = [sem(f"xt_in{r}") for r in range(4)]
        s_out_stored = [sem(f"out_stored{p}") for p in range(2)]
        s_st_out = [sem(f"st_out{r}") for r in range(4)]

        block = ctx.enter_context(nc.Block())

        x_t = x.rearrange("(t p) d -> p t d", p=P)
        out_t = out.rearrange("(t p) d -> p t d", p=P)

        def toeplitz(eng, g):
            eng.dma_start(toep[g % 2], bass.AP(tensor=h_dram, offset=g * (CHD * HPAD) + 1,
                                               ap=[[1, P], [HPAD, CHD], [1, SEQ]])).then_inc(s_toep_in[g % 2], 16)

        def sq_banks(lv, q):
            pair = 2 if lv == 1 else (len(SQ_STEPS) * lv + q) % 3
            return bank[2 * pair], bank[2 * pair + 1]

        @block.sync
        def _(sp):
            for k, src in enumerate((A, At)):
                sp.dma_start(A_rows[:, k, :, :], src.rearrange("(g i) n m -> (i n) g m", i=CH8)).then_inc(s_a_in, 16)
            sp.dma_start(bc_sb[:, 0, :], CpT).then_inc(s_bc_in, 16)
            sp.dma_start(bc_sb[:, 1, :], BpT).then_inc(s_bc_in, 16)
            for k in range(4):
                sp.dma_start(x_all[:, 8 * k:8 * k + 8, :], x_t[:, 8 * k:8 * k + 8, :]).then_inc(s_x_in[k], 16)
            sp.dma_start(wg_sb[:, :], WgRw).then_inc(s_wg_in, 16)
            sp.dma_start(bg_bc[:, :], bg.broadcast_to([P, D])).then_inc(s_wg_in, 16)
            sp.dma_start(dp_sb[:, :], DpR).then_inc(s_const_in, 16)
            sp.wait_ge(s_zeroed, 1)
            for src, dst in ((gamma, gam_bc), (beta, bet_bc), (bo, bo_bc), (fb2, fb2_bc)):
                sp.dma_start(dst[:, :], src.rearrange("(a d) -> a d", a=1).broadcast_to([P, D])).then_inc(s_const_in, 16)
            sp.dma_start(slots_in.ap().rearrange("(q p) d -> p q d", p=P),
                         zero_sb[:, :].rearrange("p (a d) -> p a d", a=1).broadcast_to([P, SLOTS // P, D])).then_inc(s_slots_zeroed, 16)
            sp.dma_start(b1_sb[:, :, :], b1T).then_inc(s_w_in, 16)
            for src, dst in ((b2, eb2), (egamma, egam), (ebeta, ebet)):
                sp.dma_start(dst, src.rearrange("(a e) d -> a e d", a=1).broadcast_to([P, E, D])).then_inc(s_w_in, 16)
            for k in range(4):
                sp.dma_start(w1_sb[:, 2 * k:2 * k + 2, :], w1.rearrange("e d f -> d e f")[:, 2 * k:2 * k + 2, :]).then_inc(s_w_in, 16)
                sp.dma_start(w2_sb[:, 2 * k:2 * k + 2, :, :],
                             w2.rearrange("e (c f) d -> f e c d", c=FC)[:, 2 * k:2 * k + 2]).then_inc(s_w_in, 16)
            for src, dst in ((Wq, wqk[:, 0, :]), (Wk, wqk[:, 1, :]), (Wk, wkv[:, 0, :]), (Wv, wkv[:, 1, :]), (Wo, wo_sb[:, :]),
                             (U1R, u1_sb[:, :]), (V2R, v2_sb[:, :]), (fb1T, fb1_sb[:, :]),
                             (V1, v1_sb[:, :]), (U2.rearrange("(c f) r -> f c r", c=FC), u2_sb[:, :, :])):
                sp.dma_start(dst, src).then_inc(s_l1_in, 16)
            sp.dma_start(h_dram.ap()[:, 0:P], zero_sb[:, :]).then_inc(s_h_out, 16)
            sp.wait_ge(s_h_ready, 1)
            for i in range(CH8):
                sp.dma_start(h_dram.ap().rearrange("(g i) (j k) -> i j g k", i=CH8, k=NI)[i, P // NI:HPAD // NI],
                             h_sb[NJ * i:NJ * i + NJ, :, :]).then_inc(s_h_out, 16)
            sp.wait_ge(s_h_out, 16 * (CH8 + 1))

            for g in range(2):
                toeplitz(sp, g)

            slots_r = slots_in.ap().rearrange("(j q p) d -> p j q d", q=MQ, p=P)
            slots_w = slots_out.ap().rearrange("(j q p) d -> p j q d", q=MQ, p=P)

            def load(j, r):
                sp.dma_start(xt[:, r, :, :], slots_r[:, bass.ds(j, 1), :, :].rearrange("p a q d -> p (a q) d")).then_inc(s_xt_in[r], 16)

            def store(j, r):
                sp.wait_ge(s_st_ready, j + 1)
                sp.dma_start(slots_w[:, bass.ds(j, 1), :, :].rearrange("p a q d -> p (a q) d"), eo[:, r, :, :]).then_inc(s_st_out[r], 16)

            def refill(j, r):
                sp.wait_ge(s_xT_tr, j + 1)
                sp.wait_ge(s_xb_ready, j + 1)
                load(j + 4, r)

            sp.wait_ge(s_ssm_done, 1)
            toeplitz(sp, 2)
            sp.wait_ge(s_scattered, 16 * TOPK * TILES)
            for r in range(4):
                load(r, r)
            for g in range(3, 5):
                sp.wait_ge(s_ssm_done, g - 1)
                toeplitz(sp, g)
            for r in range(4):
                refill(r, r)
            with sp.Fori(0, MTILES // 4 - 2) as i:
                for r in range(4):
                    refill(4 * i + r + 4, r)
                    store(4 * i + r, r)
            for j in range(MTILES - 8, MTILES):
                store(j, j % 4)
            with sp.Fori(0, GROUPS // 2) as i:
                for p in range(2):
                    g = 2 * i + p
                    sp.wait_ge(s_out_ready, g + 1 + ONE)
                    sp.dma_start(out_t[:, bass.ds(GT * g, GT), :], yo[p].rearrange("p (q d) -> p q d", q=GT)).then_inc(s_out_stored[p], 16)
            for p in range(2):
                sp.wait_ge(s_out_stored[p], 16 * (GROUPS // 2) + ONE)

        @block.gpsimd
        def _(pool):
            chain = Count(pool, s_pool_chain)
            for started in (s_pre_ready, s_rev_ready, s_out_ready, s_attn_ready,
                            *s_out_stored, *s_st_out):
                pool.sem_inc(started, ONE)
            for started in (s_res_ready, s_o_done, s_e_ready, s_av_done, s_y_ready):
                pool.sem_inc(started, LEAD)
            spread = lambda t: t.rearrange("p g (a m) -> p g a m", a=1).broadcast_to([P, BLK, CH8, N])
            diagonal = mask8[:, :].rearrange("p (a d b) -> p a d b", a=1, b=1).broadcast_to([P, BLK, CH8, N])
            chain.mark(pool.memset(mask8[:, :], 1.0))
            chain.wait()
            chain.mark(pool.affine_select(out=mask8[:, :], in_=mask8[:, :], pattern=[[-N, CH8]], compare_op=ALU.is_ge, fill=0.0,
                                          base=0, channel_multiplier=1))
            chain.wait()
            pool.affine_select(out=mask8[:, :], in_=mask8[:, :], pattern=[[N, CH8]], compare_op=ALU.is_ge, fill=0.0,
                               base=N - 1, channel_multiplier=-1).then_inc(s_mask8_ready, 1)
            pool.memset(zero_sb[:, :], 0.0).then_inc(s_zeroed, 1)
            pool.wait_ge(s_mask8_ready, 1)
            pool.wait_ge(s_a_in, 32)
            pool.tensor_tensor(Mt[:, :, 0:P].rearrange("p g (d m) -> p g d m", m=N), spread(A_rows[:, 1, :, :]), diagonal, ALU.mult)\
                .then_inc(s_blocks_ready, 1)
            pool.wait_ge(s_bc_in, 32)
            pool.tensor_copy(AiC[:, :, 0], bc_sb[:, 0, :]).then_inc(s_first_columns, 1)
            pool.tensor_copy(AjB[:, :, 0], bc_sb[:, 1, :]).then_inc(s_first_columns, 1)

            pool.memset(eps_sb[:, :], 1e-6)
            pool.memset(next_tile[:, 0::2], 0.0)
            pool.memset(next_tile[:, 1::2], 1.0)
            for t in (ident, flip, causal, same_head, head_sum, ones_sq):
                last = pool.memset(t[:, :], 1.0)
            chain.mark(last)
            chain.wait()

            def keep(t, view, pattern, base, mult, op):
                pool.affine_select(out=view, in_=view, pattern=pattern, compare_op=op, fill=0.0, base=base,
                                   channel_multiplier=mult)

            keep(ident, ident[:, :], [[-1, P]], 0, 1, ALU.is_equal)
            keep(next_tile, next_tile[:, :], [[-1, P]], 1, 1, ALU.is_equal)
            keep(flip, flip[:, :], [[1, P]], 1 - P, 1, ALU.is_equal)
            keep(causal, causal[:, :], [[1, P]], 0, -1, ALU.is_ge)
            hv = same_head[:, :].rearrange("p (h e) -> p h e", h=H)
            pool.affine_select(out=hv, in_=hv, pattern=[[-DH, H], [0, DH]], compare_op=ALU.is_ge, fill=0.0,
                               base=0, channel_multiplier=1)
            sv = head_sum[:, :].rearrange("p (h e) -> p h e", h=H)
            last = pool.affine_select(out=sv, in_=sv, pattern=[[DH, H], [1, DH]], compare_op=ALU.is_ge, fill=0.0,
                                      base=0, channel_multiplier=-1)
            chain.mark(last)
            chain.wait()
            chain.mark(pool.affine_select(out=hv, in_=hv, pattern=[[DH, H], [0, DH]], compare_op=ALU.is_ge, fill=0.0,
                                      base=DH - 1, channel_multiplier=-1))
            pool.iota(starts[:, :], pattern=[[MW, MTILES]], base=0, channel_multiplier=0, allow_small_or_imprecise_dtypes=True)
            chain.mark(pool.iota(rank8[:, :], pattern=[[-1, E]], base=E, channel_multiplier=0,
                                 allow_small_or_imprecise_dtypes=True))
            chain.wait()
            pool.sem_inc(s_masks, 1)

            with pool.Fori(0, GROUPS // 2) as h:
                for b in range(2):
                    g = 2 * h + b
                    pool.wait_ge(s_xn_ready, GT * g + GT)
                    pool.sem_inc(s_pool_pace, 1)
                    pool.tensor_copy(xn_all[:, bass.ds(GT * g, GT), :], xn[:, b, :, :]).then_inc(s_xn_saved, 1)

            pool.wait_ge(s_slots_zeroed, 16)
            pool.wait_ge(s_xn_saved, GROUPS)
            for k in range(TOPK):
                pool.wait_ge(s_pos_ready, k + 1)
                for t in range(TILES):
                    pool.indirect_dma_start(out=slots_in.ap(), out_offset=bass.IndirectOffsetOnAxis(ap=pos[:, k, t:t + 1], axis=0),
                                            in_=xn_all[:, t, :], in_offset=None).then_inc(s_scattered, 16)

            pool.wait_ge(s_const_in, 80)
            pool.tensor_tensor(bo_bc[:, :], bo_bc[:, :], fb2_bc[:, :], ALU.add).then_inc(s_bias_ready, 1)

            def prepare(j, k, r):
                e = pool.value_load(eid[0:1, bass.ds(j, 1)], min_val=0, max_val=E - 1)
                pool.wait_ge(s_xt_in[r], 16 * k + 16)
                if not isinstance(j, int):
                    pool.wait_ge(s_res_ready, j - 3 + LEAD)
                    pool.sem_inc(s_pool_pace, 1)
                pool.tensor_tensor(xb[:, r, :, :], xt[:, r, :, :], eb2[:, bass.ds(e, 1), :].broadcast_to([P, MQ, D]), ALU.add)\
                    .then_inc(s_xb_ready, 1)

            def scale(j, r):
                e = pool.value_load(eid[0:1, bass.ds(j, 1)], min_val=0, max_val=E - 1)
                pool.wait_ge(s_e_ready, j + 1 + LEAD)
                pool.sem_inc(s_pool_pace, 1)
                pool.tensor_tensor(eo[:, r, :, :], eo[:, r, :, :], egam[:, bass.ds(e, 1), :].broadcast_to([P, MQ, D]), ALU.mult)\
                    .then_inc(s_e_scaled, 1)
                pool.wait_ge(s_e_scaled, j + 1)
                pool.sem_inc(s_pool_pace, 1)
                pool.tensor_tensor(eo[:, r, :, :], eo[:, r, :, :], ebet[:, bass.ds(e, 1), :].broadcast_to([P, MQ, D]), ALU.add)\
                    .then_inc(s_st_ready, 1)

            pool.wait_ge(s_w_in, 16 * 12)
            pool.wait_ge(s_eid_ready, 1)
            for j in range(4):
                prepare(j, 0, j)
            with pool.Fori(0, MTILES // 4 - 1) as i:
                for b in range(2):
                    for r in (2 * b, 2 * b + 1):
                        scale(4 * i + r, r)
                    for r in (2 * b, 2 * b + 1):
                        prepare(4 * i + r + 4, i + 1, r)
            for r in range(4):
                scale(MTILES - 4 + r, r)

            for r in range(4):
                pool.wait_ge(s_st_out[r], 16 * (MTILES // 4) + ONE)
            pool.wait_ge(s_o_done, MTILES + LEAD)
            def gather(g):
                for t in range(GT * g, GT * g + GT):
                    for k, dst in enumerate((y1_all, y2_all)):
                        pool.indirect_dma_start(out=dst[:, t, :], out_offset=None, in_=slots_out.ap(),
                                                in_offset=bass.IndirectOffsetOnAxis(ap=pos[:, k, t:t + 1], axis=0)).then_inc(s_group_in[g], 16)
                if g != 1:
                    pool.wait_ge(s_group_in[max(g - 1, 0)], 16 * TOPK * GT)
                    pool.sem_inc(s_gathered, 1)

            row = lambda t: t[:, :].rearrange("p (a d) -> p a d", a=1).broadcast_to([P, GT, D])

            def base(g, first):
                chain.base, chain.n = first, 0
                xs = x_all[:, bass.ds(GT * g, GT), :]
                ys = y_all[:, bass.ds(GT * g, GT), :]
                chain.mark(pool.tensor_tensor(xs, xs, row(bet_bc), ALU.add))
                pool.wait_ge(s_yn_ready, g - 1)
                pool.sem_inc(s_pool_pace, 1)
                chain.mark(pool.tensor_tensor(ys, ys, row(gam_bc), ALU.mult))
                chain.wait()
                pool.sem_inc(s_pool_pace, 1)
                pool.tensor_tensor(xs, xs, ys, ALU.add).then_inc(s_base_ready, 1)

            def biases(g):
                pool.wait_ge(s_n_ready, GT * g + GT)
                pool.sem_inc(s_pool_pace, 1)
                xs = x_all[:, bass.ds(GT * g, GT), :]
                pool.tensor_tensor(xs, xs, row(bo_bc), ALU.add).then_inc(s_bias_ready, 1)

            start = chain.base + chain.n
            for g in range(GROUPS):
                gather(g)
                if g >= 4:
                    base(g - 2, start + 2 * (g - 4))
                if g >= 5:
                    biases(g - 5)
            pool.wait_ge(s_group_in[GROUPS - 1], 16 * TOPK * GT)
            pool.sem_inc(s_gathered, 1)
            for g in range(GROUPS - 2, GROUPS):
                base(g, start + 2 * (g - 2))
                biases(g - 3)
            for g in range(GROUPS - 3, GROUPS):
                biases(g)

        @block.tensor
        def _(pe):
            mm = nc.tensor.matmul
            pe.wait_ge(s_blocks_ready, 2)
            pe.wait_ge(s_first_columns, 2)

            def square(lv, q):
                k = 2 ** (lv % NI_LEVELS)
                w, wt = (P + k, P) if lv < NI_LEVELS else (P, P + k)
                n = len(SQ_STEPS) * lv + q
                if n >= 3:
                    pe.wait_ge(s_m_copied, n if lv == 1 else n - 2)
                b, bt = sq_banks(lv, q)
                for i, g in enumerate(SQ_STEPS[q]):
                    mm(b[:, SQ_W * i:SQ_W * i + w], Mt[:, g, 0:P], M[:, g, 0:w], start=True, stop=True)
                    last = mm(bt[:, SQ_W * i:SQ_W * i + wt], M[:, g, 0:P], Mt[:, g, 0:wt], start=True, stop=True)
                last.then_inc(s_sq_done, 1)

            def level(lv):
                for q in range(len(SQ_STEPS)):
                    square(lv, q)

            level(0)

            def turned(g, b):
                for q in range(GT):
                    pe.wait_ge(s_xn_ready, GT * g + q + 1)
                    last = nc.tensor.transpose(bank[6 + b][:, P * q:P * q + P], xn[:, b, q, :], ident[:, :])
                last.then_inc(s_tr_done, 1)

            def gates(g, b):
                pe.wait_ge(s_xnT_ready, g + 1)
                if not isinstance(g, int) or g:
                    pe.wait_ge(s_pre_ready, g - 1 + ONE)
                for q in range(GT):
                    last = mm(bank[2 * b + q // 2][:, (D + E) * (q % 2):(D + E) * (q % 2 + 1)], xnT[:, b, P * q:P * q + P], wg_sb[:, :],
                              start=True, stop=True)
                last.then_inc(s_gate_done, 1)

            pe.wait_ge(s_wg_in, 32)
            pe.wait_ge(s_masks, 1)
            pe.wait_ge(s_m_copied, len(SQ_STEPS))
            turned(0, 0)
            turned(1, 1)
            gates(0, 0)
            for g in range(1, GROUPS - 1):
                turned(g + 1, (g + 1) % 2)
                gates(g, g % 2)
                square(1, g - 1)
            gates(GROUPS - 1, 1)
            pe.wait_ge(s_pre_ready, GROUPS + ONE)

            def count():
                pe.wait_ge(s_mask_ready, 1)
                mflat = mask[:, :, :].rearrange("p t e -> p (t e)")
                mm(bank[7][:, 0:TILES * E], causal[:, :], mflat, start=True, stop=True)
                mm(bank[7][:, TILES * E:2 * TILES * E], ones_sq[:, :], mflat, start=True, stop=True).then_inc(s_counted, 1)

            for q in range(len(SQ_STEPS)):
                square(2, q)
                if q == 3:
                    count()
            for lv in range(3, LEVELS):
                level(lv)
            pe.wait_ge(s_m_copied, len(SQ_STEPS) * LEVELS)
            for g in range(BLK):
                last = mm(bank[5][:, NJ // 2 * g:NJ // 2 * g + NJ // 2], M[:, g, 0:P], AjB[:, g, 0:NJ // 2], start=True, stop=True)
            last.then_inc(s_pr_done, 1)
            pe.wait_ge(s_rbd_ready, 1)
            for g in range(BLK):
                last = mm(bank[6][0:HR, NI * g:NI * g + NI], Rbd[:, g, :, :].rearrange("p d j -> p (d j)"), AiC[:, g, :], start=True, stop=True)
            last.then_inc(s_h_done, 1)
            pe.wait_ge(s_pos_ready, 1)
            with pe.Fori(0, GROUPS // 2) as h:
                for j in range(2):
                    pe.wait_ge(s_xg_ready, 2 * h + j + 1)
                    pe.wait_ge(s_rev_ready, 2 * h + ONE)
                    mm(bank[4 + 3 * j][:, :], flip[:, :], xg_all[:, bass.ds(GT * 2 * h + GT * j, GT), :].rearrange("p q d -> p (q d)"),
                       start=True, stop=True).then_inc(s_rev_done, 1)
            pe.wait_ge(s_rev_ready, GROUPS + ONE)

            def convolve(g, b, h):
                pe.wait_ge(s_toep_in[b], 16 * h + 16)
                pe.wait_ge(s_xc_ready, g + 1)
                for d in range(CHD):
                    k, c = d // 4, d % 4
                    last = mm(bank[2 * b + k // 2][TILES * c:TILES * c + TILES, SEQ * (k % 2):SEQ * (k % 2) + SEQ], xc[b][:, d, :], toep[b][:, d, :],
                              start=True, stop=True, tile_position=(0, TILES * c))
                last.then_inc(s_ssm_done, 1)

            def back(g, b):
                pe.wait_ge(s_conv_ready, g + 1)
                pe.wait_ge(s_y_ready, g - 1 + LEAD)
                for k in range(CHD // 4):
                    cols = slice(P * k, P * k + P)
                    mm(bank[4 + b][:, cols], conv[b][:, k, 0:P], ident[:, :], start=True, stop=False)
                    last = mm(bank[4 + b][:, cols], conv[b][:, k, P:SEQ], next_tile[:, :], start=False, stop=True)
                last.then_inc(s_back_done, 1)

            pe.wait_ge(s_h_ready, 1)
            convolve(0, 0, 0)
            convolve(1, 1, 0)
            back(0, 0)
            convolve(2, 0, 1)
            back(1, 1)
            back(2, 0)
            pe.wait_ge(s_conv_ready, 3)
            pe.wait_ge(s_y_ready, 3 + LEAD)

            def turn(j, k, r):
                pe.wait_ge(s_xt_in[r], 16 * k + 16)
                for q in range(MQ):
                    last = nc.tensor.transpose(bank[6 + r % 2][:, P * q:P * q + P], xt[:, r, q, :], ident[:, :])
                last.then_inc(s_xT_tr, 1)

            def first(j, p):
                pe.wait_ge(s_xT_ready, j + 1)
                pe.wait_ge(s_w1s_ready, j + 1)
                for c in range(FC):
                    last = mm(bank[2 * p + c // 2][:, MW * (c % 2):MW * (c % 2) + MW], w1s[:, p, P * c:P * c + P], xT[:, p, :],
                              start=True, stop=True)
                    if c % 2:
                        last.then_inc(s_hid_done, 1)

            def second(j, p):
                e = pe.value_load(eid[0:1, bass.ds(j, 1)], min_val=0, max_val=E - 1)
                pe.wait_ge(s_hid_ready, j + 1)
                pe.wait_ge(s_res_ready, j - 1 + LEAD)
                for q in range(MQ):
                    for c in range(FC):
                        last = mm(bank[4 + p][:, P * q:P * q + P], hT[:, p, c, P * q:P * q + P],
                                  w2_sb[:, bass.ds(e, 1), c, :].rearrange("p a d -> p (a d)"), start=(c == 0), stop=(c == FC - 1))
                last.then_inc(s_o_done, 1)

            pe.wait_ge(s_w_in, 16 * 12)
            pe.wait_ge(s_eid_ready, 1)
            turn(0, 0, 0)
            turn(1, 0, 1)
            first(0, 0)
            with pe.Fori(0, MTILES // 4 - 1) as i:
                for r in range(4):
                    pe.wait_ge(s_xT_ready, 4 * i + r + 1)
                    turn(4 * i + r + 2, i + (r + 2) // 4, (r + 2) % 4)
                    first(4 * i + r + 1, (r + 1) % 2)
                    second(4 * i + r, r % 2)
            for j in range(MTILES - 4, MTILES):
                if j + 2 < MTILES:
                    pe.wait_ge(s_xT_ready, j + 1)
                    turn(j + 2, (j + 2) // 4, (j + 2) % 4)
                if j + 1 < MTILES:
                    first(j + 1, (j + 1) % 2)
                second(j, j % 2)

            pe.wait_ge(s_res_ready, MTILES + LEAD)
            convolve(3, 1, 1)
            with pe.Fori(0, GROUPS // 2 - 2) as h:
                convolve(2 * h + 4, 0, h + 2)
                back(2 * h + 3, 1)
                convolve(2 * h + 5, 1, h + 2)
                back(2 * h + 4, 0)
            back(GROUPS - 1, 1)

            pe.wait_ge(s_l1_in, 160)
            pe.wait_ge(s_small_masks, 1)
            pe.wait_ge(s_y_ready, GROUPS + LEAD)

            def scores(g, p, q):
                cols = slice(P * q, P * q + P)
                for r in range(R4):
                    rows = slice(32 * r, 32 * r + 32)
                    if q:
                        pe.wait_ge(s_am_ready, GT * R4 * g + R4 * (q - 1) + r + 1)
                    else:
                        pe.wait_ge(s_hf_ready, FC * g + r + 1)
                    mm(bank[r][:, :].rearrange("p (k t) -> p k t", k=R4), KT[p][rows, cols], QTm[p][rows, :, cols],
                       start=True, stop=True).then_inc(s_sc_done, 1)

            def values(g, p, q):
                cols = slice(P * q, P * q + P)
                av = bank[5][:, cols]
                if q % 2:
                    mm(av, S[p][:, q // 2, :], QT[p][:, cols], start=True, stop=False, skip_group_check=True)
                for r in range(R4):
                    rows = slice(32 * r, 32 * r + 32)
                    pe.wait_ge(s_am_ready, GT * R4 * g + R4 * q + r + 1)
                    for k in range(R4):
                        last = mm(av[rows, :], Vm[p][:, q, r, k, :, :].rearrange("p l e -> p (l e)"), Am[q % 2][:, r, k, :],
                                  start=(k == 0 and q % 2 == 0), stop=(k == R4 - 1), skip_group_check=True,
                                  tile_position=(0, 32 * r))
                last.then_inc(s_av_done, 1)

            def tokens(n, j):
                mm(bank[7 - j][:, 0:2 * P], xnT[:, 0, 2 * P * j:2 * P * j + P], wkv[:, :, :].rearrange("p a d -> p (a d)"),
                   start=True, stop=True)
                last = mm(bank[7 - j][:, 2 * P:3 * P], xnT[:, 0, 2 * P * j + P:2 * P * j + 2 * P], wkv[:, 1, :], start=True, stop=True)
                last.then_inc(s_tok_done, 1)

            def step(g, n, p):
                back, front = g is not None, n is not None
                if back:
                    pe.wait_ge(s_kt_ready, g + 1)
                    pe.wait_ge(s_qtm_ready, R4 * g + R4)
                    scores(g, p, 0)
                    pe.wait_ge(s_den_ready, g + 1)
                    pe.wait_ge(s_hf_ready, FC * g + FC)
                    for c in range(FC):
                        last = mm(bank[7][RANK * c:RANK * c + RANK, :], u2_sb[:, c, :], Hf[:, c, :], start=True, stop=True,
                                  tile_position=(0, RANK * c))
                    last.then_inc(s_qf_done, 1)
                    scores(g, p, 1)
                    pe.wait_ge(s_qf_ready, g + 1)
                if front:
                    for q in range(GT):
                        pe.wait_ge(s_n_ready, GT * n + q + 1)
                        last = nc.tensor.transpose(bank[7][:, P * q:P * q + P], xn[:, 0, q, :], ident[:, :])
                    last.then_inc(s_n_tr, 1)
                if back:
                    pe.wait_ge(s_vm_ready, g + 1)
                    pe.wait_ge(s_attn_ready, g + ONE)
                    pe.wait_ge(s_s_ready, g + 1)
                    values(g, p, 0)
                if front:
                    pe.wait_ge(s_n_T, n + 1)
                    mm(bank[6][:, :], wqk[:, 0, :], xnT[:, 0, :], start=True, stop=True).then_inc(s_q_done, 1)
                if back:
                    scores(g, p, 2)
                if front:
                    mm(bank[7][:, :], wqk[:, 1, :], xnT[:, 0, :], start=True, stop=True).then_inc(s_k_done, 1)
                if back:
                    values(g, p, 1)
                if front:
                    pe.wait_ge(s_ekv_ready, 2 * n + 1)
                    mm(bank[6][:, :], u1_sb[:, :], xnT[:, 0, :], start=True, stop=True).then_inc(s_u_done, 1)
                if back:
                    scores(g, p, 3)
                if front:
                    pe.wait_ge(s_ekv_ready, 2 * n + 2)
                    tokens(n, 0)
                if back:
                    values(g, p, 2)
                if front:
                    pe.wait_ge(s_pt_ready, n + 1)
                    tokens(n, 1)
                    pe.wait_ge(s_v_ready, 2 * n + 1)
                    pe.wait_ge(s_qk_ready, 2 * n + 2)
                    mm(bank[7][:, :], head_sum[:, :], KT[1 - p], start=True, stop=True).then_inc(s_kc_done, 1)
                if back:
                    values(g, p, 3)
                if front:
                    for c in range(FC):
                        rows = slice(RANK * c, RANK * c + RANK)
                        mm(bank[c][:, :], v1_sb[rows, :], PT[rows, :], start=True, stop=True).then_inc(s_hf_done, 1)
                    pe.wait_ge(s_v_ready, 2 * n + 2)
                    pe.wait_ge(s_kt_ready, n + 1)
                    for b in range(2):
                        last = mm(bank[6][:, P * b:P * b + P], Ktok[:, P * b:P * b + P], Vtok[:, 2 * P * b:2 * P * b + P], start=True, stop=True)
                    last.then_inc(s_st_done, 1)
                if back:
                    pe.wait_ge(s_attn_ready, g + 1 + ONE)
                    pe.wait_ge(s_out_ready, g + ONE)
                    for q in range(GT):
                        cols = slice(P * q, P * q + P)
                        mm(bank[4][:, cols], attnT[:, cols], wo_sb[:, :], start=True, stop=False)
                        last = mm(bank[4][:, cols], QfT[:, cols], v2_sb[:, :], start=False, stop=True)
                    last.then_inc(s_y_done, 1)
                if front:
                    pe.wait_ge(s_prod_ready, n + 1)
                    mm(bank[7][:, :], same_head[:, :], prod, start=True, stop=True).then_inc(s_den_done, 1)

            step(None, 0, 1)
            with pe.Fori(0, GROUPS // 2 - 1) as i:
                step(2 * i, 2 * i + 1, 0)
                step(2 * i + 1, 2 * i + 2, 1)
            step(GROUPS - 2, GROUPS - 1, 0)
            step(GROUPS - 1, None, 1)

        @block.scalar
        def _(act):
            copy = nc.scalar.copy

            def level(lv):
                k = 2 ** (lv % NI_LEVELS)
                vec = AiC if lv < NI_LEVELS else AjB
                for q, blocks in enumerate(SQ_STEPS):
                    n = len(SQ_STEPS) * lv + q
                    act.wait_ge(s_sq_done, n + 1)
                    gs = slice(blocks[0], blocks[-1] + 1)
                    b, bt = [t[:, 0:SQ_W * len(blocks)].rearrange("p (g c) -> p g c", c=SQ_W) for t in sq_banks(lv, q)]
                    copy(vec[:, gs, k:2 * k], (b if lv < NI_LEVELS else bt)[:, :, P:P + k])
                    copy(M[:, gs, 0:P], b[:, :, 0:P])
                    copy(Mt[:, gs, 0:P], bt[:, :, 0:P]).then_inc(s_m_copied, 1)

            for lv in range(LEVELS):
                level(lv)
            act.wait_ge(s_pr_done, 1)
            copy(AjB[:, :, NJ // 2:], bank[5][:, 0:BLK * NJ // 2].rearrange("p (g k) -> p g k", g=BLK)).then_inc(s_columns_done, 1)
            for k in range(GROUPS // 2):
                act.wait_ge(s_pre_ready, 2 * k + 2 + ONE)
                xs = xg_all[:, 2 * GT * k:2 * GT * k + 2 * GT, :]
                nc.scalar.activation(xs, xs, ACT.Sigmoid).then_inc(s_sig_ready, 2)
            with act.Fori(0, GROUPS // 2) as h:
                for j in range(2):
                    act.wait_ge(s_rev_done, 2 * h + j + 1)
                    copy(xg_all[:, bass.ds(GT * 2 * h + GT * j, GT), :].rearrange("p q d -> p (q d)"), bank[4 + 3 * j][:, :]).then_inc(s_rev_ready, 1)
            act.wait_ge(s_gap_ready, 1)
            nc.scalar.activation(gw[:, 1, :], gw[:, 0, :], ACT.Exp).then_inc(s_gap_exp, 1)

            def convolved(g, b):
                act.wait_ge(s_ssm_done, g + 1)
                for i in range(2):
                    last = copy(conv[b][:, 2 * i:2 * i + 2, :], bank[2 * b + i][:, :].rearrange("p (k t) -> p k t", k=2))
                last.then_inc(s_conv_ready, 1)

            def recurred(g, b):
                act.wait_ge(s_back_done, g + 1)
                copy(y_all[:, :, bass.ds(CHD * g, CHD)], bank[4 + b][:, :].rearrange("p (d t) -> p t d", d=CHD)).then_inc(s_y_ready, 1)

            convolved(0, 0)
            convolved(1, 1)
            recurred(0, 0)
            convolved(2, 0)
            recurred(1, 1)
            recurred(2, 0)

            def turned(j, p):
                act.wait_ge(s_xT_tr, j + 1)
                copy(xT[:, p, :], bank[6 + p][:, 0:MW]).then_inc(s_xT_ready, 1)

            def weights(j, p):
                e = act.value_load(eid[0:1, bass.ds(j, 1)], min_val=0, max_val=E - 1)
                copy(w1s[:, p, :], w1_sb[:, bass.ds(e, 1), :].rearrange("p a f -> p (a f)")).then_inc(s_w1s_ready, 1)

            def hidden(j, p):
                e = act.value_load(eid[0:1, bass.ds(j, 1)], min_val=0, max_val=E - 1)
                act.wait_ge(s_o_done, j - 1 + LEAD)
                for c in range(FC):
                    if c % 2 == 0:
                        act.wait_ge(s_hid_done, 2 * j + c // 2 + 1)
                        act.sem_inc(s_act_pace, 1)
                    last = nc.scalar.activation(hT[:, p, c, :], bank[2 * p + c // 2][:, MW * (c % 2):MW * (c % 2) + MW], ACT.Gelu,
                                                bias=b1_sb[:, bass.ds(e, 1), c])
                last.then_inc(s_hid_ready, 1)

            act.wait_ge(s_w_in, 16 * 12)
            act.wait_ge(s_eid_ready, 1)
            for j in range(2):
                turned(j, j)
                weights(j, j)
            hidden(0, 0)
            with act.Fori(0, MTILES // 2 - 1) as i:
                for p in range(2):
                    turned(2 * i + p + 2, p)
                    weights(2 * i + p + 2, p)
                    hidden(2 * i + p + 1, 1 - p)
            hidden(MTILES - 1, 1)

            for g in range(3, GROUPS):
                convolved(g, g % 2)
                if g + 2 < GROUPS:
                    toeplitz(act, g + 2)
                if g > 3:
                    recurred(g - 1, 1 - g % 2)
            recurred(GROUPS - 1, 1)

            def step(g, n, p):
                if g is not None:
                    act.wait_ge(s_qf_done, g + 1)
                    copy(QfT, bank[7][:, :]).then_inc(s_qf_ready, 1)
                if n is None:
                    return
                act.wait_ge(s_n_tr, n + 1)
                copy(xnT[:, 0, :], bank[7][:, :]).then_inc(s_n_T, 1)
                act.wait_ge(s_q_done, n + 1)
                nc.scalar.activation(QT[1 - p], bank[6][:, :], ACT.Exp)
                nc.scalar.activation(Rq, bank[6][:, :], ACT.Relu).then_inc(s_ekv_ready, 1)
                act.wait_ge(s_k_done, n + 1)
                nc.scalar.activation(KT[1 - p], bank[7][:, :], ACT.Exp)
                nc.scalar.activation(Rk, bank[7][:, :], ACT.Relu).then_inc(s_ekv_ready, 1)
                act.wait_ge(s_u_done, n + 1)
                copy(PT, bank[6][:, :]).then_inc(s_pt_ready, 1)
                act.wait_ge(s_qk_ready, 2 * n + 1)
                for k in range(R4):
                    nc.scalar.activation(QTm[1 - p][:, k, :], QT[1 - p], ACT.Copy, scale=head_pick[:, k:k + 1]).then_inc(s_qtm_ready, 1)
                for j in range(2):
                    act.wait_ge(s_tok_done, 2 * n + j + 1)
                    nc.scalar.activation(Ktok[:, P * j:P * j + P], bank[7 - j][:, 0:P], ACT.Exp)
                    nc.scalar.activation(Rkt[:, P * j:P * j + P], bank[7 - j][:, 0:P], ACT.Relu)
                    copy(Vtok[:, 2 * P * j:2 * P * j + 2 * P], bank[7 - j][:, P:3 * P]).then_inc(s_v_ready, 1)
                for c in range(FC):
                    act.wait_ge(s_hf_done, FC * n + c + 1)
                    nc.scalar.activation(Hf[:, c, :], bank[c][:, :], ACT.Gelu_apprx_tanh, bias=fb1_sb[:, c:c + 1]).then_inc(s_hf_ready, 1)
                act.wait_ge(s_den_done, n + 1)
                nc.scalar.activation(zr, bank[7][:, :], ACT.Identity, bias=eps_sb[:, 0:1]).then_inc(s_den_ready, 1)

            step(None, 0, 1)
            with act.Fori(0, GROUPS // 2 - 1) as i:
                step(2 * i, 2 * i + 1, 0)
                step(2 * i + 1, 2 * i + 2, 1)
            step(GROUPS - 2, GROUPS - 1, 0)
            step(GROUPS - 1, None, 1)

        @block.vector
        def _(dve):
            v = nc.vector
            chain = Count(dve, s_dve_chain)

            def inverse_root(out, var, eps):
                w = var.shape[1]
                a, b = ve[:, 0:w], sq[:, 0:w]
                chain.mark(v.tensor_scalar(a, var, eps, None, ALU.add))
                chain.wait()
                chain.mark(v.tensor_scalar(out.bitcast(I32), a.bitcast(I32), 1, None, ALU.logical_shift_right))
                chain.wait()
                chain.mark(v.tensor_scalar(out.bitcast(I32), out.bitcast(I32), -1.0, float(0x5F3759DF), ALU.mult, ALU.add))
                chain.wait()
                for _ in range(NEWTON):
                    chain.mark(v.tensor_tensor(b, out, out, ALU.mult))
                    chain.wait()
                    chain.mark(v.scalar_tensor_tensor(out=b, in0=b, scalar=-0.5, in1=a, op0=ALU.mult, op1=ALU.mult))
                    chain.wait()
                    chain.mark(v.scalar_tensor_tensor(out=out, in0=b, scalar=1.5, in1=out, op0=ALU.add, op1=ALU.mult))
                    chain.wait()

            def moments(src, n, mean_var):
                dve.sem_inc(s_dve_pace, 1)
                for q in range(n):
                    last = v.bn_stats(stats[:, q, :], src(q))
                chain.mark(last)
                chain.wait()
                dve.sem_inc(s_dve_pace, 1)
                for q in range(n):
                    last = v.bn_aggr(mean_var[:, q, :], stats[:, q, :])
                chain.mark(last)
                chain.wait()

            def layer_norm(src, n, mean_var, root, eps):
                moments(src, n, mean_var)
                inverse_root(root, mean_var[:, 0:n, 1], eps)

            dve.wait_ge(s_mask8_ready, 1)
            dve.wait_ge(s_a_in, 32)
            v.tensor_tensor(M[:, :, 0:P].rearrange("p g (d m) -> p g d m", m=N),
                            A_rows[:, 0, :, :].rearrange("p g (a m) -> p g a m", a=1).broadcast_to([P, BLK, CH8, N]),
                            mask8[:, :].rearrange("p (a d b) -> p a d b", a=1, b=1).broadcast_to([P, BLK, CH8, N]), ALU.mult)\
                .then_inc(s_blocks_ready, 1)
            for k in range(4):
                dve.wait_ge(s_x_in[k], 16)
                for q in range(8 * k, 8 * k + 8):
                    last = v.bn_stats(stats[:, q, :], x_all[:, q, :])
            chain.mark(last)
            chain.wait()
            for q in range(TILES):
                last = v.bn_aggr(mv[:, q, :], stats[:, q, :])
            chain.mark(last)
            chain.wait()
            inverse_root(rstd[:, :], mv[:, :, 1], 1e-5)

            def normal(g, b, wait=True):
                if wait:
                    dve.wait_ge(s_tr_done, g - 1)
                    dve.wait_ge(s_xn_saved, g - 1)
                for q in range(GT):
                    t = bass.ds(GT * g + q, 1)
                    v.tensor_scalar(xn[:, b, q, :], x_all[:, t, :].rearrange("p a d -> p (a d)"), mv[:, t, 0], rstd[:, t],
                                    ALU.subtract, ALU.mult).then_inc(s_xn_ready, 1)

            def turned(g, b):
                dve.wait_ge(s_tr_done, g + 1)
                v.tensor_copy(xnT[:, b, :], bank[6 + b][:, :]).then_inc(s_xnT_ready, 1)

            def gated(g, b):
                dve.wait_ge(s_gate_done, g + 1)
                for j in range(2):
                    gp = bank[2 * b + j][:, 0:2 * (D + E)].rearrange("p (q c) -> p q c", q=2)
                    tiles = bass.ds(GT * g + 2 * j, 2)
                    v.tensor_copy(logits[:, tiles, :], gp[:, :, D:D + E])
                    last = v.tensor_tensor(xg_all[:, tiles, :], gp[:, :, 0:D],
                                           bg_bc[:, :].rearrange("p (a d) -> p a d", a=1).broadcast_to([P, 2, D]), ALU.add)
                last.then_inc(s_pre_ready, 1)

            normal(0, 0, wait=False)
            normal(1, 1, wait=False)
            turned(0, 0)
            dve.wait_ge(s_wg_in, 32)
            with dve.Fori(0, GROUPS // 2 - 1) as h:
                normal(2 * h + 2, 0)
                turned(2 * h + 1, 1)
                gated(2 * h, 0)
                normal(2 * h + 3, 1)
                turned(2 * h + 2, 0)
                gated(2 * h + 1, 1)
            turned(GROUPS - 1, 1)
            gated(GROUPS - 2, 0)
            gated(GROUPS - 1, 1)

            full = [P, TILES, E]
            bc = lambda t: t[:, :].rearrange("p (t a) -> p t a", a=1).broadcast_to(full)
            rk = rank8[:, :].rearrange("p (a e) -> p a e", a=1).broadcast_to(full)

            def best(lg, mx, onehot):
                chain.mark(v.tensor_reduce(mx[:, :], lg, AXX, ALU.max))
                chain.wait()
                chain.mark(v.tensor_tensor(onehot, lg, bc(mx), ALU.is_ge))
                chain.wait()
                chain.mark(v.tensor_tensor(onehot, onehot, rk, ALU.mult))
                chain.wait()
                chain.mark(v.tensor_reduce(m3[:, :], onehot, AXX, ALU.max))
                chain.wait()
                chain.mark(v.tensor_tensor(onehot, rk, bc(m3), ALU.is_equal))
                chain.wait()

            dve.wait_ge(s_masks, 1)
            dve.wait_ge(s_pre_ready, GROUPS + ONE)
            best(logits[:, :, :], m1, hot1[:, :, :])
            chain.mark(v.scalar_tensor_tensor(out=t2[:, :, :], in0=hot1[:, :, :], scalar=-3.0e38, in1=logits[:, :, :], op0=ALU.mult, op1=ALU.add))
            chain.wait()
            best(t2[:, :, :], m2, hot2[:, :, :])
            v.tensor_tensor(mask[:, :, :], hot1[:, :, :], hot2[:, :, :], ALU.add).then_inc(s_mask_ready, 1)
            v.tensor_tensor(gw[:, 0, :], m2[:, :], m1[:, :], ALU.subtract).then_inc(s_gap_ready, 1)

            dve.wait_ge(s_counted, 1)
            total = bank[7][:, TILES * E:2 * TILES * E].rearrange("p (t e) -> p t e", e=E)
            within = bank[7][:, 0:TILES * E].rearrange("p (t e) -> p t e", e=E)

            def running_sum(a, b, n):
                step = 1
                while step < n:
                    v.tensor_copy(b[:, 0:step], a[:, 0:step])
                    chain.mark(v.tensor_tensor(b[:, step:n], a[:, step:n], a[:, 0:n - step], ALU.add))
                    chain.wait()
                    a, b, step = b, a, 2 * step
                return a

            chain.mark(v.tensor_copy(cum[:, :, :], total))
            chain.wait()
            upto = running_sum(cum, t2, TILES)
            chain.mark(v.tensor_scalar(counts[:, 0, :].bitcast(I32), upto[:, TILES - 1, :], float(MW - 1), None, ALU.add))
            chain.wait()
            chain.mark(v.tensor_scalar(counts[:, 1, :].bitcast(I32), counts[:, 0, :].bitcast(I32), -MW, None, ALU.bitwise_and))
            chain.wait()
            v.tensor_copy(counts[:, 2, :], counts[:, 1, :].bitcast(I32))
            chain.mark(v.tensor_copy(ends[:, 0, :], counts[:, 1, :].bitcast(I32)))
            chain.wait()
            end = running_sum(ends[:, 0, :], ends[:, 1, :], E)
            chain.mark(v.tensor_tensor(counts[:, 3, :], end, counts[:, 2, :], ALU.subtract))
            chain.mark(v.tensor_tensor(off[:, :, :], upto[:, :, :], total, ALU.subtract))
            chain.wait()
            chain.mark(v.tensor_tensor(off[:, :, :], off[:, :, :], counts[:, 3:4, :].broadcast_to(full), ALU.add))
            chain.wait()
            chain.mark(v.scalar_tensor_tensor(out=off[:, :, :], in0=within, scalar=-1.0, in1=off[:, :, :], op0=ALU.add, op1=ALU.add))
            chain.wait()
            for k, hot in enumerate((hot1, hot2)):
                chain.mark(v.tensor_tensor(hot[:, :, :], hot[:, :, :], off[:, :, :], ALU.mult))
                chain.wait()
                chain.mark(v.tensor_reduce(posf[:, :], hot[:, :, :], AXX, ALU.add))
                chain.wait()
                v.tensor_copy(pos[:, k, :], posf[:, :]).then_inc(s_pos_ready, 1)
                dve.wait_ge(s_pos_ready, k + 1)
            v.memset(eidf[:, :], 0.0)
            chain.mark(v.memset(m3[:, :], 0.0))
            chain.wait()
            for e in range(E - 1):
                chain.mark(v.scalar_tensor_tensor(out=eidf[:, :], in0=starts[:, :], scalar=end[:, e:e + 1], in1=eidf[:, :], op0=ALU.is_ge, op1=ALU.add))
                chain.wait()
            v.tensor_copy(eid[:, :], eidf[:, :]).then_inc(s_eid_ready, 1)

            dve.wait_ge(s_masks, 1)
            v.tensor_reduce(head_pick[:, :], same_head[:, :].rearrange("p (r k e) -> p k r e", r=R4, k=R4)[:, :, :, 0], AXX, ALU.add)
            v.tensor_reduce(first_lag[:, :], ident[0:HR, 0:HR].rearrange("p (i j) -> p i j", j=NJ)[:, :, 0], AXX, ALU.add)
            chain.mark(v.tensor_reduce(place8[:, :], ident[:, :].rearrange("p (h e) -> p e h", h=H), AXX, ALU.add))
            chain.wait()
            hs = head_sum[:, :].rearrange("p (h e) -> p h e", h=H)
            v.tensor_tensor(hs, hs, place8[:, :].rearrange("p (a e) -> p a e", a=1).broadcast_to([P, H, DH]), ALU.mult).then_inc(s_small_masks, 1)

            dve.wait_ge(s_columns_done, 1)
            v.tensor_tensor(Rbd, AjB.rearrange("p g (a j) -> p g a j", a=1).broadcast_to([P, BLK, CH8, NJ]),
                            mask8[:, :].rearrange("p (a d b) -> p a d b", a=1, b=1).broadcast_to([P, BLK, CH8, NJ]), ALU.mult).then_inc(s_rbd_ready, 1)
            dve.wait_ge(s_const_in, 80)
            chain.mark(v.tensor_scalar(dp1[:, :], dp_sb[:, :], 1.0, first_lag[:, 0:1], ALU.add, ALU.mult))
            chain.wait()
            dve.wait_ge(s_h_done, 1)
            hp = bank[6][0:HR, :].rearrange("p (g i) -> p g i", g=BLK)
            chain.mark(v.tensor_copy(h_sb, hp))
            chain.wait()
            v.tensor_tensor(h_sb[:, :, 0], hp[:, :, 0], dp1[:, :], ALU.add).then_inc(s_h_ready, 1)

            with dve.Fori(0, GROUPS) as g:
                dve.wait_ge(s_xn_saved, g + 1)
                dve.wait_ge(s_sig_ready, g + 1)
                xs = xg_all[:, bass.ds(GT * g, GT), :]
                v.tensor_tensor(xs, xs, xn_all[:, bass.ds(GT * g, GT), :], ALU.mult).then_inc(s_xg_ready, 1)

            def channels(g, b):
                v.tensor_copy(xc[b][:, :, :], xg_all[:, :, bass.ds(CHD * g, CHD)].rearrange("p t d -> p d t")).then_inc(s_xc_ready, 1)

            dve.wait_ge(s_rev_ready, GROUPS + ONE)
            channels(0, 0)
            channels(1, 1)
            dve.wait_ge(s_gap_exp, 1)
            chain.mark(v.tensor_scalar(m3[:, :], gw[:, 1, :], 1.0, None, ALU.add))
            chain.wait()
            chain.mark(v.reciprocal(gw[:, 0, :], m3[:, :]))
            chain.wait()
            chain.mark(v.tensor_tensor(gw[:, 1, :], gw[:, 1, :], gw[:, 0, :], ALU.mult))

            for g in range(2, 5):
                dve.wait_ge(s_ssm_done, g - 1)
                channels(g, g % 2)

            one = lambda t, g, q: t[:, bass.ds(GT * g + q, 1), :].rearrange("p a d -> p (a d)")

            def experts(i):
                for b in range(2):
                    for p in range(2):
                        j = 4 * i + 2 * b + p
                        dve.wait_ge(s_o_done, j + 1 + LEAD)
                        dve.wait_ge(s_xb_ready, j + 1)
                        dve.wait_ge(s_e_ready, j - 1 + LEAD)
                        v.tensor_tensor(res[:, p, :, :], bank[4 + p][:, 0:MW].rearrange("p (q d) -> p q d", q=MQ), xb[:, 2 * b + p, :, :],
                                        ALU.add).then_inc(s_res_ready, 1)
                    dve.wait_ge(s_res_ready, 4 * i + 2 * b + 2 + LEAD)
                    layer_norm(lambda q: res[:, q // MQ, q % MQ, :], 2 * MQ, mv8, rstd8[:, 0:GT], 1e-6)
                    for p in range(2):
                        r = 2 * b + p
                        dve.wait_ge(s_st_out[r], 16 * i + ONE)
                        for q in range(MQ):
                            last = v.tensor_scalar(eo[:, r, q, :], res[:, p, q, :], mv8[:, MQ * p + q, 0:1],
                                                   rstd8[:, MQ * p + q:MQ * p + q + 1], ALU.subtract, ALU.mult)
                        last.then_inc(s_e_ready, 1)

            start = chain.base + chain.n
            with dve.Fori(0, MTILES // 4) as i:
                chain.base, chain.n = i * (2 * NORM) + start, 0
                experts(i)
            chain.base, chain.n = start + MTILES // 4 * 2 * NORM, 0

            for g in range(5, GROUPS):
                dve.wait_ge(s_ssm_done, g - 1)
                channels(g, g % 2)

            dve.wait_ge(s_st_ready, MTILES)
            dve.wait_ge(s_xc_ready, GROUPS)
            v.memset(Vm[0], 0.0)
            chain.mark(v.memset(Vm[1], 0.0))
            chain.wait()

            def outputs(m, k):
                dve.wait_ge(s_gathered, m + 1)
                if not isinstance(m, int) or m > 1:
                    dve.wait_ge(s_base_ready, m - 1)
                for q in range(GT):
                    last = v.scalar_tensor_tensor(out=one(x_all, m, q), in0=one((y1_all, y2_all)[k], m, q), scalar=gw[:, k, bass.ds(GT * m + q, 1)],
                                                  in1=one(x_all, m, q), op0=ALU.mult, op1=ALU.add)
                chain.mark(last)
                chain.wait()

            def normalise(m):
                for q in range(GT):
                    v.tensor_scalar(xn[:, 0, q, :], one(x_all, m, q), mv8[:, q, 0:1], rstd8[:, q:q + 1], ALU.subtract, ALU.mult).then_inc(s_n_ready, 1)

            def recurrence(g, at):
                for q in range(GT):
                    last = v.tensor_scalar(one(y_all, g, q), one(y_all, g, q), mv8[:, at + q, 0:1], rstd8[:, at + q:at + q + 1],
                                           ALU.subtract, ALU.mult)
                last.then_inc(s_yn_ready, 1)

            def statistics(m, ahead):
                layer_norm(lambda q: one(x_all, m, q) if q < GT else one(y_all, m + 1, q - GT), 2 * GT if ahead else GT,
                           mv8, rstd8[:, 0:2 * GT if ahead else GT], 1e-5)
                if ahead:
                    recurrence(m + 1, GT)

            def masked(g, q):
                dve.wait_ge(s_av_done, GT * g + q - 1 + LEAD)
                for r in range(R4):
                    dve.wait_ge(s_sc_done, GT * R4 * g + R4 * q + r + 1)
                    v.tensor_tensor(Am[q % 2][:, r, :, :], bank[r][:, :].rearrange("p (k t) -> p k t", k=R4),
                                    causal[:, :].rearrange("p (a t) -> p a t", a=1).broadcast_to([P, R4, P]), ALU.mult).then_inc(s_am_ready, 1)

            def feature(n, i, to, re):
                dve.wait_ge(s_ekv_ready, 2 * n + i + 1)
                v.scalar_tensor_tensor(out=to, in0=to, scalar=1.0, in1=re, op0=ALU.min, op1=ALU.add).then_inc(s_qk_ready, 1)

            STEP = 2 + NORM

            def keys(n, p):
                dve.wait_ge(s_v_ready, 2 * n + 2)
                v.scalar_tensor_tensor(out=Ktok[:, 0:2 * P], in0=Ktok[:, 0:2 * P], scalar=1.0, in1=Rkt[:, 0:2 * P], op0=ALU.min, op1=ALU.add).then_inc(s_kt_ready, 1)
                dve.wait_ge(s_kc_done, n + 1)
                dve.wait_ge(s_qk_ready, 2 * n + 2)
                v.tensor_tensor(prod, QT[1 - p], bank[7][:, :], ALU.mult).then_inc(s_prod_ready, 1)

            def value_heads(n, p):
                for q in range(GT):
                    full_v = Vm[1 - p][:, q, :, :, :, :].rearrange("p r k l e -> p r (k l) e")
                    last = v.tensor_copy(full_v[:, :, 0:16:5, :], Vtok[:, P * q:P * q + P].rearrange("p (r k e) -> p r k e", r=R4, k=R4))
                last.then_inc(s_vm_ready, 1)
                dve.wait_ge(s_st_done, n + 1)
                v.tensor_tensor(S[1 - p][:, :, :], bank[6][:, 0:2 * P].rearrange("p (b c) -> p b c", b=2),
                                same_head[:, :].rearrange("p (a c) -> p a c", a=1).broadcast_to([P, 2, P]), ALU.mult).then_inc(s_s_ready, 1)

            def step(g, n, m, p, i, ahead=True):
                front, norm = n is not None, m is not None
                dve.wait_ge(s_den_ready, g + 1)
                masked(g, 0)
                if norm:
                    outputs(m, 0)
                masked(g, 1)
                v.reciprocal(zr, zr).then_inc(s_zr_ready, 1)
                if front:
                    feature(n, 0, QT[1 - p], Rq)
                if norm:
                    outputs(m, 1)
                masked(g, 2)
                if front:
                    feature(n, 1, KT[1 - p], Rk)
                if norm:
                    statistics(m, ahead)
                masked(g, 3)
                if front:
                    keys(n, p)
                dve.wait_ge(s_zr_ready, g + 1)
                dve.wait_ge(s_av_done, GT * g + GT + LEAD)
                v.tensor_tensor(attnT, bank[5][:, :], zr, ALU.mult).then_inc(s_attn_ready, 1)
                if front:
                    value_heads(n, p)
                if norm:
                    normalise(m)
                dve.wait_ge(s_y_done, g + 1)
                dve.wait_ge(s_bias_ready, g + 2)
                dve.wait_ge(s_out_stored[p], 16 * i + ONE)
                v.tensor_tensor(yo[p].rearrange("p (q d) -> p q d", q=GT), bank[4][:, :].rearrange("p (q d) -> p q d", q=GT),
                                x_all[:, bass.ds(GT * g, GT), :], ALU.add).then_inc(s_out_ready, 1)

            row = lambda t: t[:, :].rearrange("p (a d) -> p a d", a=1).broadcast_to([P, GT, D])
            dve.wait_ge(s_const_in, 80)
            def centred(g, at):
                for q in range(GT):
                    t = GT * g + q
                    last = v.scalar_tensor_tensor(out=y_all[:, t, :], in0=y_all[:, t, :], scalar=mv8[:, at + q, 0:1], in1=gam_bc[:, :],
                                                  op0=ALU.subtract, op1=ALU.mult)
                chain.mark(last)

            def joined(g, at):
                for q in range(GT):
                    t = GT * g + q
                    last = v.scalar_tensor_tensor(out=x_all[:, t, :], in0=y_all[:, t, :], scalar=rstd8[:, at + q:at + q + 1], in1=x_all[:, t, :],
                                                  op0=ALU.mult, op1=ALU.add)
                chain.mark(last)
                chain.wait()

            for g in range(2):
                tiles = slice(GT * g, GT * g + GT)
                chain.mark(v.tensor_tensor(x_all[:, tiles, :], x_all[:, tiles, :], row(bet_bc), ALU.add))
            chain.wait()
            outputs(0, 0)
            outputs(0, 1)
            dve.wait_ge(s_y_ready, GROUPS + LEAD)
            moments(lambda q: y_all[:, q, :], 2 * GT, mv8)
            centred(0, 0)
            inverse_root(rstd8[:, :], mv8[:, :, 1], 1e-5)
            joined(0, 0)
            statistics(0, False)
            normalise(0)
            centred(1, GT)
            chain.wait()
            joined(1, GT)
            outputs(1, 0)
            outputs(1, 1)
            feature(0, 0, QT[0], Rq)
            feature(0, 1, KT[0], Rk)
            statistics(1, True)
            keys(0, 1)
            value_heads(0, 1)
            normalise(1)
            start = chain.base + chain.n
            with dve.Fori(0, GROUPS // 2 - 2) as i:
                chain.base, chain.n = i * (2 * STEP) + start, 0
                step(2 * i, 2 * i + 1, 2 * i + 2, 0, i)
                step(2 * i + 1, 2 * i + 2, 2 * i + 3, 1, i)
            chain.base, chain.n = start + (GROUPS // 2 - 2) * 2 * STEP, 0
            for g in range(GROUPS - 4, GROUPS):
                step(g, g + 1 if g < GROUPS - 1 else None, g + 2 if g < GROUPS - 2 else None, g % 2, g // 2, ahead=g < GROUPS - 3)


def kernel(**inputs):
    import numpy as np
    import concourse.bacc as bacc
    from concourse.bass_utils import run_bass_kernel_spmd

    a = {k: np.asarray(v) for k, v in inputs.items()}
    pairs = lambda t: t.reshape(BLK, CH8, N).transpose(1, 2, 0).reshape(P, BLK)
    laid = [
        ("x", a["L0_attn_x"].reshape(TILES * P, D)),
        ("A", a["L0_attn_A"]),
        ("At", a["L0_attn_A"].transpose(0, 2, 1)),
        ("BpT", pairs(a["L0_attn_Bp"])),
        ("CpT", pairs(a["L0_attn_Cp"])),
        ("DpR", np.repeat(a["L0_attn_Dp"].reshape(BLK, CH8).T, NJ, axis=0)),
        ("WgRw", np.concatenate([a["L0_attn_Wg"].T, a["L0_ffn_router_w"]], axis=1)),
        ("bg", a["L0_attn_bg"].reshape(1, D)),
        ("gamma", a["L0_attn_gamma"]),
        ("beta", a["L0_attn_beta"]),
        ("w1", a["L0_ffn_w1"]),
        ("b1T", a["L0_ffn_b1"].reshape(E, FC, P).transpose(2, 0, 1)),
        ("w2", a["L0_ffn_w2"]),
        ("b2", a["L0_ffn_b2"]),
        ("egamma", a["L0_ffn_gamma"]),
        ("ebeta", a["L0_ffn_beta"]),
        ("Wq", a["L1_attn_Wq"]),
        ("Wk", a["L1_attn_Wk"]),
        ("Wv", a["L1_attn_Wv"]),
        ("Wo", a["L1_attn_Wo"]),
        ("bo", a["L1_attn_bo"]),
        ("U1R", np.concatenate([a["L1_ffn_U1"]] * FC, axis=1)),
        ("V1", a["L1_ffn_V1"].reshape(RANK, FC, P).transpose(1, 0, 2).reshape(P, P)),
        ("fb1T", a["L1_ffn_b1"].reshape(FC, P).T),
        ("U2", a["L1_ffn_U2"]),
        ("V2R", np.concatenate([a["L1_ffn_V2"]] * FC, axis=0)),
        ("fb2", a["L1_ffn_b2"]),
    ]
    nc = bacc.Bacc("TRN2", target_bir_lowering=False, num_devices=1)
    arrays, args = {}, []
    for name, t in laid:
        t = np.ascontiguousarray(t)
        arrays[f"in_{name}"] = t
        args.append(nc.dram_tensor(f"in_{name}", t.shape, F32, kind="ExternalInput").ap())
    out = nc.dram_tensor("out_x", (TILES * P, D), F32, kind="ExternalOutput").ap()
    two_layer_kernel(nc, *args, out)
    r = run_bass_kernel_spmd(nc, [arrays], core_ids=[0])
    return r.results[0]["out_x"].reshape(BATCH, SEQ, D)
```
